# Optimizing a Trainium2 kernel written in Bass

```python
import numpy as np
import jax
import jax.numpy as jnp

def _softmax(x, axis=-1):
    return jax.nn.softmax(x, axis=axis)

def _gelu(x):
    return jax.nn.gelu(x, approximate=True)

def _silu(x):
    return jax.nn.silu(x)

def _sigmoid(x):
    return jax.nn.sigmoid(x)

def _layernorm(x, axis=-1, eps=1e-05):
    m = jnp.mean(x, axis=axis, keepdims=True)
    v = jnp.var(x, axis=axis, keepdims=True)
    return (x - m) / jnp.sqrt(v + eps)

def _scatter_add(tgt, idx, src, axis=0):
    return tgt.at[idx].add(src)

def _segment_sum(src, seg, n):
    return jax.ops.segment_sum(src, seg, n)
kernel_name = 'mk_flamingo_gated_d4_seqx_r8_8ae23c'

def setup_inputs(seed: int=0):
    np.random.seed(seed)
    _w = jnp.asarray

    def _rec_inputs():
        import jax
        import jax.numpy as jnp
        _rk = jax.random.key(seed)
        x = -0.0005207 + 1.001 * jax.random.normal(jax.random.fold_in(_rk, 1), (128, 64, 128), jnp.float32)
        _lenS = 64 - jax.random.randint(jax.random.fold_in(_rk, 7), (128,), 0, max(1, 64 // 4) + 1, jnp.int32)
        _lenS2 = 64 - jax.random.randint(jax.random.fold_in(_rk, 8), (128,), 0, max(1, 64 // 4) + 1, jnp.int32)
        _ctx_1024P = jax.random.normal(jax.random.fold_in(_rk, 11), (128, 16, 128), jnp.float32)
        _ctx_1024c = jax.random.dirichlet(jax.random.fold_in(_rk, 511), 0.3 * jnp.ones((16,), jnp.float32), (128, 64))
        _ctx_1024t = jnp.einsum('bsk,bkd->bsd', _ctx_1024c, _ctx_1024P)
        _ctx_1024t = _ctx_1024t * jax.lax.rsqrt(jnp.mean(jnp.square(_ctx_1024t)) + 1e-12) * 0.953939
        ctx_1024 = -0.000514642 + 1.00011 * (_ctx_1024t + 0.3 * jax.random.normal(jax.random.fold_in(_rk, 611), (128, 64, 128), jnp.float32))
        _validS = jnp.arange(64)[None, :] < _lenS[:, None]
        _validS2 = jnp.arange(64)[None, :] < _lenS2[:, None]
        _causal = jnp.tril(jnp.ones((64, 64), dtype=bool))
        mask_BxS_ik0 = jnp.where(jnp.broadcast_to(_validS[:, :], (128, 64)), 0, 1).astype(jnp.int32)
        mask_Bx1xSxS2_ik1 = jnp.where(jnp.broadcast_to(_validS2[:, None, None, :], (128, 1, 64, 64)), 1, 0).astype(jnp.int32)
        mask_BxS2_ik1 = jnp.where(jnp.broadcast_to(_validS2[:, :], (128, 64)), 1, 0).astype(jnp.int32)
        _g = jax.random.normal(jax.random.fold_in(_rk, 9001), (2, 4), jnp.float32)
        _g = jnp.sign(_g) * jnp.maximum(jnp.abs(_g), 1.0) + (_g == 0) * 1.0
        g_xattn = _g[0]
        g_ffn = _g[1]
        return (x, ctx_1024, mask_BxS_ik0, mask_Bx1xSxS2_ik1, mask_BxS2_ik1, g_xattn, g_ffn)
    x, ctx_1024, mask_BxS_ik0, mask_Bx1xSxS2_ik1, mask_BxS2_ik1, g_xattn, g_ffn = _rec_inputs()

    def _L0_xattn_setup():
        import jax, jax.numpy as jnp
        import numpy as np
        B, S, E, NH = (1, 256, 128, 8)
        DH = E // NH
        EPS_BACKEND = 1e-06
        EPS_NORM = 1e-05
        key = jax.random.key(seed)
        ks = jax.random.split(key, 8)
        q = jax.random.normal(ks[0], (B, S, E), jnp.float32)
        k = jax.random.normal(ks[1], (B, S, E), jnp.float32)
        v = jax.random.normal(ks[2], (B, S, E), jnp.float32)
        igate_w = jax.random.normal(ks[3], (NH, 3 * E), jnp.float32) * 0.02
        igate_b = jax.random.normal(ks[4], (NH,), jnp.float32) * 0.1
        fgate_w = jax.random.normal(ks[5], (NH, 3 * E), jnp.float32) * 0.02
        fgate_b = jnp.linspace(3.0, 6.0, NH).astype(jnp.float32)
        norm_w = 1.0 + 0.1 * jax.random.normal(ks[6], (E,), jnp.float32)
        return dict(q=q, k=k, v=v, igate_w=igate_w, igate_b=igate_b, fgate_w=fgate_w, fgate_b=fgate_b, norm_w=norm_w)
    _L0_xattn_all = _L0_xattn_setup()
    _L0_xattn_in = {k: v for k, v in _L0_xattn_all.items() if k in ('igate_w', 'igate_b', 'fgate_w', 'fgate_b', 'norm_w')}
    del _L0_xattn_all

    def _L0_ffn_setup():
        import jax, jax.numpy as jnp
        import numpy as np
        D_IN, D_HID = (128, 512)

        def _ternary(key, shape):
            return jax.random.randint(key, shape, -1, 2).astype(jnp.float32)

        def _tlin(x, w, s):
            return jnp.einsum('bsi,oi->bso', x, w) * s
        key = jax.random.key(seed)
        ks = jax.random.split(key, 12)
        inv = lambda fan: 1.0 / np.sqrt(fan).astype(np.float32)
        return {'x': jax.random.normal(ks[0], (4, 256, D_IN), dtype=jnp.float32), 'w1_w': _ternary(ks[1], (D_HID, D_IN)), 'w1_s': jax.random.uniform(ks[2], (D_HID,), dtype=jnp.float32) * inv(D_IN), 'w2_w': _ternary(ks[3], (D_HID, D_IN)), 'w2_s': jax.random.uniform(ks[4], (D_HID,), dtype=jnp.float32) * inv(D_IN), 'h1_w': _ternary(ks[5], (D_HID, D_HID)), 'h1_s': jax.random.uniform(ks[6], (D_HID,), dtype=jnp.float32) * inv(D_HID), 'h2_w': _ternary(ks[7], (D_HID, D_HID)), 'h2_s': jax.random.uniform(ks[8], (D_HID,), dtype=jnp.float32) * inv(D_HID), 'w3_w': _ternary(ks[9], (D_IN, D_HID)), 'w3_s': jax.random.uniform(ks[10], (D_IN,), dtype=jnp.float32) * inv(D_HID)}
    _L0_ffn_all = _L0_ffn_setup()
    _L0_ffn_in = {k: v for k, v in _L0_ffn_all.items() if k in ('w1_w', 'w1_s', 'w2_w', 'w2_s', 'h1_w', 'h1_s', 'h2_w', 'h2_s', 'w3_w', 'w3_s')}
    del _L0_ffn_all

    def _L1_xattn_setup():
        import jax, jax.numpy as jnp
        import numpy as np
        HEADS = 16
        HIDDEN = 128
        DH = HIDDEN // HEADS
        STD = 0.02

        def _split_heads(x):
            B, S, _ = x.shape
            return x.reshape(B, S, HEADS, DH).transpose(0, 2, 1, 3)
        key = jax.random.key(seed)
        ks = jax.random.split(key, 12)
        B, S = (4, 256)
        inp = {'q': jax.random.normal(ks[0], (B, S, HIDDEN), jnp.float32), 'k': jax.random.normal(ks[1], (B, S, HIDDEN), jnp.float32), 'v': jax.random.normal(ks[2], (B, S, HIDDEN), jnp.float32), 'mask': jax.random.randint(ks[3], (B, S), 0, 2, jnp.int32), 'wq': STD * jax.random.normal(ks[4], (HIDDEN, HIDDEN), jnp.float32), 'bq': jnp.zeros((HIDDEN,), jnp.float32), 'wk': STD * jax.random.normal(ks[5], (HIDDEN, HIDDEN), jnp.float32), 'bk': jnp.zeros((HIDDEN,), jnp.float32), 'wv': STD * jax.random.normal(ks[6], (HIDDEN, HIDDEN), jnp.float32), 'bv': jnp.zeros((HIDDEN,), jnp.float32), 'wo': STD * jax.random.normal(ks[7], (HIDDEN, HIDDEN), jnp.float32), 'bo': jnp.zeros((HIDDEN,), jnp.float32)}
        return inp
    _L1_xattn_all = _L1_xattn_setup()
    _L1_xattn_in = {k: v for k, v in _L1_xattn_all.items() if k in ('wq', 'bq', 'wk', 'bk', 'wv', 'bv', 'wo', 'bo')}
    del _L1_xattn_all

    def _L1_ffn_setup():
        import jax, jax.numpy as jnp
        import numpy as np
        BLOCK = 32
        W_BITS = 4
        ACT_BITS = 16

        def act_qdq(x):
            qmax = 2.0 ** (ACT_BITS - 1) - 1.0
            scale = jnp.maximum(jnp.max(jnp.abs(x)) / qmax, 1e-12)
            return jnp.clip(jnp.round(x / scale), -qmax - 1.0, qmax) * scale

        def fixed_qdq_u16(x):
            scale = 1.0 / 65536.0
            return jnp.clip(jnp.round(x / scale), 0.0, 65535.0) * scale

        def lpbq_dequant(w):
            O, I = w.shape
            qmax = 2.0 ** (W_BITS - 1) - 1.0
            wb = w.reshape(O, I // BLOCK, BLOCK)
            s = jnp.maximum(jnp.max(jnp.abs(wb), axis=-1, keepdims=True) / qmax, 1e-12)
            wq = jnp.clip(jnp.round(wb / s), -qmax - 1.0, qmax) * s
            return wq.reshape(O, I)
        key = jax.random.key(seed)
        k1, k2, k3, k4 = jax.random.split(key, 4)
        B, S, H, I = (2, 512, 128, 384)
        x = jax.random.normal(k1, (B, S, H), jnp.float32)
        w_gate = jax.random.normal(k2, (I, H), jnp.float32) * 0.02
        w_up = jax.random.normal(k3, (I, H), jnp.float32) * 0.02
        w_down = jax.random.normal(k4, (H, I), jnp.float32) * 0.02
        return {'x': x, 'w_gate': w_gate, 'w_up': w_up, 'w_down': w_down}
    _L1_ffn_all = _L1_ffn_setup()
    _L1_ffn_in = {k: v for k, v in _L1_ffn_all.items() if k in ('w_gate', 'w_up', 'w_down')}
    del _L1_ffn_all

    def _L2_xattn_setup():
        import jax, jax.numpy as jnp
        import numpy as np
        EMBED = 128
        HEADS = 16
        HEAD_DIM = EMBED // HEADS
        key = jax.random.key(seed)
        k1, k2, k3, k4, k5, k6 = jax.random.split(key, 6)
        N, S = (4, 256)
        return {'values': jax.random.normal(k1, (N, S, EMBED), dtype=jnp.float32), 'keys': jax.random.normal(k2, (N, S, EMBED), dtype=jnp.float32), 'query': jax.random.normal(k3, (N, S, EMBED), dtype=jnp.float32), 'mask': jax.random.randint(k4, (N, 1, S, S), 0, 2, dtype=jnp.int32), 'W_out': jax.random.normal(k5, (EMBED, EMBED), dtype=jnp.float32) * (1.0 / np.sqrt(EMBED)), 'b_out': jax.random.normal(k6, (EMBED,), dtype=jnp.float32) * 0.01}
    _L2_xattn_all = _L2_xattn_setup()
    _L2_xattn_in = {k: v for k, v in _L2_xattn_all.items() if k in ('W_out', 'b_out')}
    del _L2_xattn_all

    def _L2_ffn_setup():
        import jax, jax.numpy as jnp
        import numpy as np
        import math
        GOLDEN_CENTER = 1.0 / math.e
        GOLDEN_LOWER = 0.5 - math.log(4.0 / 3.0)
        GOLDEN_UPPER = 0.5
        B, T, D = (4, 256, 128)
        E = 8
        I = 512 // (E // 2)

        def _routing_weights(x, Wr, temperature):
            inh = jax.nn.sigmoid(x @ Wr / temperature)
            in_zone = (inh >= GOLDEN_LOWER) & (inh <= GOLDEN_UPPER)
            dist = jnp.abs(inh - GOLDEN_CENTER)
            w = jnp.exp(-dist / 0.1) * in_zone.astype(x.dtype)
            wsum = w.sum(axis=-1, keepdims=True)
            no_expert = wsum < 1e-08
            fb = jnp.exp(-dist / 0.3)
            _, top2 = jax.lax.top_k(fb, 2)
            fb_mask = jax.nn.one_hot(top2, E, dtype=x.dtype).sum(axis=-2)
            fb_w = fb * fb_mask
            fb_w = fb_w / jnp.clip(fb_w.sum(axis=-1, keepdims=True), 1e-08)
            w = jnp.where(no_expert, fb_w, w)
            wsum = w.sum(axis=-1, keepdims=True)
            return w / jnp.clip(wsum, 1e-08)
        key = jax.random.key(seed)
        k = jax.random.split(key, 6)
        s_d = 1.0 / math.sqrt(D)
        s_i = 1.0 / math.sqrt(I)
        return {'x': jax.random.normal(k[0], (B, T, D), jnp.float32), 'Wg': jax.random.normal(k[1], (E, D, I), jnp.float32) * s_d, 'Wu': jax.random.normal(k[2], (E, D, I), jnp.float32) * s_d, 'Wd': jax.random.normal(k[3], (E, I, D), jnp.float32) * s_i, 'Wr': jax.random.normal(k[4], (D, E), jnp.float32) * s_d, 'temperature': jnp.ones((1,), jnp.float32)}
    _L2_ffn_all = _L2_ffn_setup()
    _L2_ffn_in = {k: v for k, v in _L2_ffn_all.items() if k in ('Wg', 'Wu', 'Wd', 'Wr', 'temperature')}
    del _L2_ffn_all

    def _L3_xattn_setup():
        import jax, jax.numpy as jnp
        import numpy as np
        D = 128
        B, LQ, LK = (8, 256, 256)
        NEG = -1000000000.0
        key = jax.random.key(seed)
        ks = jax.random.split(key, 8)
        query = jax.random.normal(ks[0], (B, LQ, D), dtype=jnp.float32)
        k_in = jax.random.normal(ks[1], (B, LK, D), dtype=jnp.float32)
        value = jax.random.normal(ks[2], (B, LK, D), dtype=jnp.float32)
        mask = jax.random.randint(ks[3], (B, LK), 0, 2, dtype=jnp.int32)
        s = 1.0 / np.sqrt(D)
        Wq_w = jax.random.normal(ks[4], (D, D), dtype=jnp.float32) * s
        Wq_b = jnp.zeros((D,), dtype=jnp.float32)
        Wk_w = jax.random.normal(ks[5], (D, D), dtype=jnp.float32) * s
        Wk_b = jnp.zeros((D,), dtype=jnp.float32)
        return {'query': query, 'key': k_in, 'value': value, 'mask': mask, 'Wq_w': Wq_w, 'Wq_b': Wq_b, 'Wk_w': Wk_w, 'Wk_b': Wk_b}
    _L3_xattn_all = _L3_xattn_setup()
    _L3_xattn_in = {k: v for k, v in _L3_xattn_all.items() if k in ('Wq_w', 'Wq_b', 'Wk_w', 'Wk_b')}
    del _L3_xattn_all

    def _L3_ffn_setup():
        import jax, jax.numpy as jnp
        import numpy as np
        DIM = 128
        DEPTH = 2
        HEADS = 8
        DIM_HEAD = 64
        WINDOW = 64
        INNER = HEADS * DIM_HEAD
        HID = int(DIM * 4 * 2 / 3)
        B, N = (2, 1024)
        QK_SCALE = 8.0

        def shift_token(t):
            t1, t2 = jnp.split(t, 2, axis=-1)
            t2 = jnp.pad(t2, ((0, 0), (1, 0), (0, 0)))[:, :-1]
            return jnp.concatenate([t1, t2], axis=-1)

        def l2norm(t):
            return t / jnp.clip(jnp.linalg.norm(t, axis=-1, keepdims=True), 1e-12)

        def rotate_half(x):
            x1, x2 = jnp.split(x, 2, axis=-1)
            return jnp.concatenate([-x2, x1], axis=-1)

        def rotary_xpos(q, k):
            n = q.shape[-2]
            half_idx = jnp.arange(0, DIM_HEAD, 2, dtype=jnp.float32)
            inv_freq = 1.0 / 10000.0 ** (half_idx / DIM_HEAD)
            t = jnp.arange(n, dtype=jnp.float32)
            freqs = t[:, None] * inv_freq[None, :]
            freqs = jnp.concatenate([freqs, freqs], axis=-1)
            base = (half_idx + 0.4 * DIM_HEAD) / (1.4 * DIM_HEAD)
            power = (t - n // 2) / float(WINDOW // 2)
            scale = base[None, :] ** power[:, None]
            scale = jnp.concatenate([scale, scale], axis=-1)
            cos, sin = (jnp.cos(freqs), jnp.sin(freqs))
            q = q * cos * scale + rotate_half(q) * sin * scale
            k = k * cos / scale + rotate_half(k) * sin / scale
            return (q, k)

        def local_attention(q, k, v):
            b, h, n, d = q.shape
            w = n // WINDOW
            bq = q.reshape(b, h, w, WINDOW, d) * QK_SCALE
            bk = k.reshape(b, h, w, WINDOW, d)
            bv = v.reshape(b, h, w, WINDOW, d)

            def look_around(t):
                p = jnp.pad(t, ((0, 0), (0, 0), (1, 0), (0, 0), (0, 0)))
                return jnp.concatenate([p[:, :, :w], p[:, :, 1:]], axis=3)
            bk, bv = (look_around(bk), look_around(bv))
            bt = jnp.arange(n).reshape(w, WINDOW)
            btp = jnp.pad(bt, ((1, 0), (0, 0)), constant_values=-1)
            btk = jnp.concatenate([btp[:w], btp[1:]], axis=1)
            sim = jnp.einsum('bhwid,bhwjd->bhwij', bq, bk)
            i = bt[:, :, None]
            j = btk[:, None, :]
            mask = (i < j) | (i > j + WINDOW) | (j == -1)
            sim = jnp.where(mask, -jnp.finfo(sim.dtype).max, sim)
            attn = jax.nn.softmax(sim, axis=-1)
            out = jnp.einsum('bhwij,bhwjd->bhwid', attn, bv)
            return out.reshape(b, h, n, d)

        def _layer(x, wqkv, qs, ksc, wo, lg, lb, w1, b1, w2, b2):
            b, n, _ = x.shape
            h = shift_token(x)
            qkv = h @ wqkv
            q, k, v = jnp.split(qkv, 3, axis=-1)
            to_heads = lambda t: t.reshape(b, n, HEADS, DIM_HEAD).transpose(0, 2, 1, 3)
            q, k, v = (to_heads(q), to_heads(k), to_heads(v))
            q = l2norm(q) * qs
            k = l2norm(k) * ksc
            q, k = rotary_xpos(q, k)
            o = local_attention(q, k, v)
            o = o.transpose(0, 2, 1, 3).reshape(b, n, INNER)
            x = x + o @ wo
            h = shift_token(x)
            mu = h.mean(-1, keepdims=True)
            var = h.var(-1, keepdims=True)
            h = (h - mu) / jnp.sqrt(var + 1e-05) * lg + lb
            h = h @ w1 + b1
            a, g = jnp.split(h, 2, axis=-1)
            h = a * jax.nn.gelu(g, approximate=False)
            x = x + h @ w2 + b2
            return x
        key = jax.random.key(seed)
        ks = jax.random.split(key, 6)
        return {'x': jax.random.normal(ks[0], (B, N, DIM), jnp.float32), 'wqkv': jax.random.normal(ks[1], (DEPTH, DIM, 3 * INNER), jnp.float32) * 0.02, 'q_scale': jnp.ones((DEPTH, DIM_HEAD), jnp.float32), 'k_scale': jnp.ones((DEPTH, DIM_HEAD), jnp.float32), 'wo': jax.random.normal(ks[2], (DEPTH, INNER, DIM), jnp.float32) * 0.02, 'ln_g': jnp.ones((DEPTH, DIM), jnp.float32), 'ln_b': jnp.zeros((DEPTH, DIM), jnp.float32), 'w1': jax.random.normal(ks[3], (DEPTH, DIM, 2 * HID), jnp.float32) * 0.02, 'b1': jnp.zeros((DEPTH, 2 * HID), jnp.float32), 'w2': jax.random.normal(ks[4], (DEPTH, HID, DIM), jnp.float32) * 0.02, 'b2': jnp.zeros((DEPTH, DIM), jnp.float32)}
    _L3_ffn_all = _L3_ffn_setup()
    _L3_ffn_in = {k: v for k, v in _L3_ffn_all.items() if k in ('wqkv', 'q_scale', 'k_scale', 'wo', 'ln_g', 'ln_b', 'w1', 'b1', 'w2', 'b2')}
    del _L3_ffn_all
    return {'x': x, 'ctx_1024': ctx_1024, 'mask_BxS_ik0': mask_BxS_ik0, 'mask_Bx1xSxS2_ik1': mask_Bx1xSxS2_ik1, 'mask_BxS2_ik1': mask_BxS2_ik1, 'g_xattn': g_xattn, 'g_ffn': g_ffn, 'L0_xattn_igate_w': _L0_xattn_in['igate_w'], 'L0_xattn_igate_b': _L0_xattn_in['igate_b'], 'L0_xattn_fgate_w': _L0_xattn_in['fgate_w'], 'L0_xattn_fgate_b': _L0_xattn_in['fgate_b'], 'L0_xattn_norm_w': _L0_xattn_in['norm_w'], 'L0_ffn_w1_w': _L0_ffn_in['w1_w'], 'L0_ffn_w1_s': _L0_ffn_in['w1_s'], 'L0_ffn_w2_w': _L0_ffn_in['w2_w'], 'L0_ffn_w2_s': _L0_ffn_in['w2_s'], 'L0_ffn_h1_w': _L0_ffn_in['h1_w'], 'L0_ffn_h1_s': _L0_ffn_in['h1_s'], 'L0_ffn_h2_w': _L0_ffn_in['h2_w'], 'L0_ffn_h2_s': _L0_ffn_in['h2_s'], 'L0_ffn_w3_w': _L0_ffn_in['w3_w'], 'L0_ffn_w3_s': _L0_ffn_in['w3_s'], 'L1_xattn_wq': _L1_xattn_in['wq'], 'L1_xattn_bq': _L1_xattn_in['bq'], 'L1_xattn_wk': _L1_xattn_in['wk'], 'L1_xattn_bk': _L1_xattn_in['bk'], 'L1_xattn_wv': _L1_xattn_in['wv'], 'L1_xattn_bv': _L1_xattn_in['bv'], 'L1_xattn_wo': _L1_xattn_in['wo'], 'L1_xattn_bo': _L1_xattn_in['bo'], 'L1_ffn_w_gate': _L1_ffn_in['w_gate'], 'L1_ffn_w_up': _L1_ffn_in['w_up'], 'L1_ffn_w_down': _L1_ffn_in['w_down'], 'L2_xattn_W_out': _L2_xattn_in['W_out'], 'L2_xattn_b_out': _L2_xattn_in['b_out'], 'L2_ffn_Wg': _L2_ffn_in['Wg'], 'L2_ffn_Wu': _L2_ffn_in['Wu'], 'L2_ffn_Wd': _L2_ffn_in['Wd'], 'L2_ffn_Wr': _L2_ffn_in['Wr'], 'L2_ffn_temperature': _L2_ffn_in['temperature'], 'L3_xattn_Wq_w': _L3_xattn_in['Wq_w'], 'L3_xattn_Wq_b': _L3_xattn_in['Wq_b'], 'L3_xattn_Wk_w': _L3_xattn_in['Wk_w'], 'L3_xattn_Wk_b': _L3_xattn_in['Wk_b'], 'L3_ffn_wqkv': _L3_ffn_in['wqkv'], 'L3_ffn_q_scale': _L3_ffn_in['q_scale'], 'L3_ffn_k_scale': _L3_ffn_in['k_scale'], 'L3_ffn_wo': _L3_ffn_in['wo'], 'L3_ffn_ln_g': _L3_ffn_in['ln_g'], 'L3_ffn_ln_b': _L3_ffn_in['ln_b'], 'L3_ffn_w1': _L3_ffn_in['w1'], 'L3_ffn_b1': _L3_ffn_in['b1'], 'L3_ffn_w2': _L3_ffn_in['w2'], 'L3_ffn_b2': _L3_ffn_in['b2']}

def reference(x, ctx_1024, mask_BxS_ik0, mask_Bx1xSxS2_ik1, mask_BxS2_ik1, g_xattn, g_ffn, L0_xattn_igate_w, L0_xattn_igate_b, L0_xattn_fgate_w, L0_xattn_fgate_b, L0_xattn_norm_w, L0_ffn_w1_w, L0_ffn_w1_s, L0_ffn_w2_w, L0_ffn_w2_s, L0_ffn_h1_w, L0_ffn_h1_s, L0_ffn_h2_w, L0_ffn_h2_s, L0_ffn_w3_w, L0_ffn_w3_s, L1_xattn_wq, L1_xattn_bq, L1_xattn_wk, L1_xattn_bk, L1_xattn_wv, L1_xattn_bv, L1_xattn_wo, L1_xattn_bo, L1_ffn_w_gate, L1_ffn_w_up, L1_ffn_w_down, L2_xattn_W_out, L2_xattn_b_out, L2_ffn_Wg, L2_ffn_Wu, L2_ffn_Wd, L2_ffn_Wr, L2_ffn_temperature, L3_xattn_Wq_w, L3_xattn_Wq_b, L3_xattn_Wk_w, L3_xattn_Wk_b, L3_ffn_wqkv, L3_ffn_q_scale, L3_ffn_k_scale, L3_ffn_wo, L3_ffn_ln_g, L3_ffn_ln_b, L3_ffn_w1, L3_ffn_b1, L3_ffn_w2, L3_ffn_b2):
    import jax
    import jax.numpy as jnp

    def _L0_xattn_ref(q, k, v, igate_w, igate_b, fgate_w, fgate_b, norm_w):
        import jax, jax.numpy as jnp
        import numpy as np
        B, S, E, NH = (1, 256, 128, 8)
        DH = E // NH
        EPS_BACKEND = 1e-06
        EPS_NORM = 1e-05
        Bq, Sq, Eq = q.shape
        nh = igate_w.shape[0]
        dh = Eq // nh
        gate_in = jnp.concatenate([q, k, v], axis=-1)
        ig = jnp.transpose(gate_in @ igate_w.T + igate_b, (0, 2, 1))
        fg = jnp.transpose(gate_in @ fgate_w.T + fgate_b, (0, 2, 1))
        qh = q.reshape(Bq, Sq, nh, dh).transpose(0, 2, 1, 3)
        kh = k.reshape(Bq, Sq, nh, dh).transpose(0, 2, 1, 3)
        vh = v.reshape(Bq, Sq, nh, dh).transpose(0, 2, 1, 3)
        log_f_cum = jnp.cumsum(jax.nn.log_sigmoid(fg), axis=-1)
        log_fg_mat = log_f_cum[:, :, :, None] - log_f_cum[:, :, None, :]
        ltr = jnp.tril(jnp.ones((Sq, Sq), dtype=bool))
        log_D = jnp.where(ltr, log_fg_mat + ig[:, :, None, :], -jnp.inf)
        max_log_D = jnp.max(log_D, axis=-1, keepdims=True)
        D = jnp.exp(log_D - max_log_D)
        qk = jnp.einsum('bhsd,bhtd->bhst', qh, kh) / jnp.sqrt(jnp.float32(dh))
        C = qk * D
        normalizer = jnp.maximum(jnp.abs(jnp.sum(C, axis=-1, keepdims=True)), jnp.exp(-max_log_D))
        h = jnp.einsum('bhst,bhtd->bhsd', C / (normalizer + EPS_BACKEND), vh)
        mean = jnp.mean(h, axis=-1, keepdims=True)
        var = jnp.var(h, axis=-1, keepdims=True)
        h_norm = (h - mean) / jnp.sqrt(var + EPS_NORM)
        h_norm = h_norm * norm_w.reshape(nh, dh)[None, :, None, :]
        return h_norm.transpose(0, 2, 1, 3).reshape(Bq, Sq, Eq)

    def _L0_ffn_ref(x, w1_w, w1_s, w2_w, w2_s, h1_w, h1_s, h2_w, h2_s, w3_w, w3_s):
        import jax, jax.numpy as jnp
        import numpy as np
        D_IN, D_HID = (128, 512)

        def _ternary(key, shape):
            return jax.random.randint(key, shape, -1, 2).astype(jnp.float32)

        def _tlin(x, w, s):
            return jnp.einsum('bsi,oi->bso', x, w) * s
        h = jax.nn.silu(_tlin(x, w1_w, w1_s)) * _tlin(x, w2_w, w2_s)
        h = jax.nn.gelu(_tlin(h, h1_w, h1_s), approximate=False)
        h = jax.nn.gelu(_tlin(h, h2_w, h2_s), approximate=False)
        return _tlin(h, w3_w, w3_s)

    def _L1_xattn_ref(q, k, v, mask, wq, bq, wk, bk, wv, bv, wo, bo):
        import jax, jax.numpy as jnp
        import numpy as np
        HEADS = 16
        HIDDEN = 128
        DH = HIDDEN // HEADS
        STD = 0.02

        def _split_heads(x):
            B, S, _ = x.shape
            return x.reshape(B, S, HEADS, DH).transpose(0, 2, 1, 3)
        B, S, _ = q.shape
        qh = _split_heads(q @ wq.T + bq)
        kh = _split_heads(k @ wk.T + bk)
        vh = _split_heads(v @ wv.T + bv)
        scale = 1.0 / jnp.sqrt(jnp.float32(DH))
        corr = jnp.einsum('bhqd,bhkd->bhqk', qh, kh) * scale
        row_mask = (mask != 0)[:, None, :, None]
        corr = jnp.where(row_mask, corr, jnp.float32(-1000000000.0))
        prob = jax.nn.softmax(corr, axis=-1)
        hidden = jnp.einsum('bhqk,bhkd->bhqd', prob, vh)
        hidden = hidden.transpose(0, 2, 1, 3).reshape(B, S, HIDDEN)
        return hidden @ wo.T + bo

    def _L1_ffn_ref(x, w_gate, w_up, w_down):
        import jax, jax.numpy as jnp
        import numpy as np
        BLOCK = 32
        W_BITS = 4
        ACT_BITS = 16

        def act_qdq(x):
            qmax = 2.0 ** (ACT_BITS - 1) - 1.0
            scale = jnp.maximum(jnp.max(jnp.abs(x)) / qmax, 1e-12)
            return jnp.clip(jnp.round(x / scale), -qmax - 1.0, qmax) * scale

        def fixed_qdq_u16(x):
            scale = 1.0 / 65536.0
            return jnp.clip(jnp.round(x / scale), 0.0, 65535.0) * scale

        def lpbq_dequant(w):
            O, I = w.shape
            qmax = 2.0 ** (W_BITS - 1) - 1.0
            wb = w.reshape(O, I // BLOCK, BLOCK)
            s = jnp.maximum(jnp.max(jnp.abs(wb), axis=-1, keepdims=True) / qmax, 1e-12)
            wq = jnp.clip(jnp.round(wb / s), -qmax - 1.0, qmax) * s
            return wq.reshape(O, I)
        x = act_qdq(x)
        up = act_qdq(x @ lpbq_dequant(w_up).T)
        gate = act_qdq(x @ lpbq_dequant(w_gate).T)
        sig = fixed_qdq_u16(jax.nn.sigmoid(gate))
        gate = act_qdq(gate * sig)
        o = act_qdq(gate * up)
        return o @ lpbq_dequant(w_down).T

    def _L2_xattn_ref(values, keys, query, mask, W_out, b_out):
        import jax, jax.numpy as jnp
        import numpy as np
        EMBED = 128
        HEADS = 16
        HEAD_DIM = EMBED // HEADS
        N, Q = (query.shape[0], query.shape[1])
        K = keys.shape[1]
        v = values.reshape(N, K, HEADS, HEAD_DIM)
        k = keys.reshape(N, K, HEADS, HEAD_DIM)
        q = query.reshape(N, Q, HEADS, HEAD_DIM)
        energy = jnp.einsum('nqhd,nkhd->nhqk', q, k)
        energy = jnp.where(mask == 0, jnp.float32(-1e+20), energy)
        attn = jax.nn.softmax(energy / jnp.sqrt(jnp.float32(EMBED)), axis=3)
        out = jnp.einsum('nhqk,nkhd->nqhd', attn, v).reshape(N, Q, EMBED)
        return out @ W_out.T + b_out

    def _L2_ffn_ref(x, Wg, Wu, Wd, Wr, temperature):
        import jax, jax.numpy as jnp
        import numpy as np
        import math
        GOLDEN_CENTER = 1.0 / math.e
        GOLDEN_LOWER = 0.5 - math.log(4.0 / 3.0)
        GOLDEN_UPPER = 0.5
        B, T, D = (4, 256, 128)
        E = 8
        I = 512 // (E // 2)

        def _routing_weights(x, Wr, temperature):
            inh = jax.nn.sigmoid(x @ Wr / temperature)
            in_zone = (inh >= GOLDEN_LOWER) & (inh <= GOLDEN_UPPER)
            dist = jnp.abs(inh - GOLDEN_CENTER)
            w = jnp.exp(-dist / 0.1) * in_zone.astype(x.dtype)
            wsum = w.sum(axis=-1, keepdims=True)
            no_expert = wsum < 1e-08
            fb = jnp.exp(-dist / 0.3)
            _, top2 = jax.lax.top_k(fb, 2)
            fb_mask = jax.nn.one_hot(top2, E, dtype=x.dtype).sum(axis=-2)
            fb_w = fb * fb_mask
            fb_w = fb_w / jnp.clip(fb_w.sum(axis=-1, keepdims=True), 1e-08)
            w = jnp.where(no_expert, fb_w, w)
            wsum = w.sum(axis=-1, keepdims=True)
            return w / jnp.clip(wsum, 1e-08)
        weights = _routing_weights(x, Wr, temperature)
        gate = jnp.einsum('btd,edi->beti', x, Wg)
        up = jnp.einsum('btd,edi->beti', x, Wu)
        h = jax.nn.silu(gate) * up
        e_out = jnp.einsum('beti,eid->betd', h, Wd)
        out = jnp.einsum('bte,betd->btd', weights, e_out)
        return out

    def _L3_xattn_ref(query, key, value, mask, Wq_w, Wq_b, Wk_w, Wk_b):
        import jax, jax.numpy as jnp
        import numpy as np
        D = 128
        B, LQ, LK = (8, 256, 256)
        NEG = -1000000000.0
        q = jnp.einsum('bld,ed->ble', query, Wq_w) + Wq_b
        k = jnp.einsum('bld,ed->ble', key, Wk_w) + Wk_b
        scale = 1.0 / jnp.sqrt(jnp.asarray(D, dtype=q.dtype))
        aw = jnp.einsum('bqd,bkd->bqk', q, k) * scale
        m = mask.astype(aw.dtype)[:, None, :]
        aw = aw * m
        aw = jnp.where(m == 0, jnp.asarray(NEG, dtype=aw.dtype), aw)
        attn = jax.nn.softmax(aw, axis=-1)
        return jnp.einsum('bqk,bkd->bqd', attn, value)

    def _L3_ffn_ref(x, wqkv, q_scale, k_scale, wo, ln_g, ln_b, w1, b1, w2, b2):
        import jax, jax.numpy as jnp
        import numpy as np
        DIM = 128
        DEPTH = 2
        HEADS = 8
        DIM_HEAD = 64
        WINDOW = 64
        INNER = HEADS * DIM_HEAD
        HID = int(DIM * 4 * 2 / 3)
        B, N = (2, 1024)
        QK_SCALE = 8.0

        def shift_token(t):
            t1, t2 = jnp.split(t, 2, axis=-1)
            t2 = jnp.pad(t2, ((0, 0), (1, 0), (0, 0)))[:, :-1]
            return jnp.concatenate([t1, t2], axis=-1)

        def l2norm(t):
            return t / jnp.clip(jnp.linalg.norm(t, axis=-1, keepdims=True), 1e-12)

        def rotate_half(x):
            x1, x2 = jnp.split(x, 2, axis=-1)
            return jnp.concatenate([-x2, x1], axis=-1)

        def rotary_xpos(q, k):
            n = q.shape[-2]
            half_idx = jnp.arange(0, DIM_HEAD, 2, dtype=jnp.float32)
            inv_freq = 1.0 / 10000.0 ** (half_idx / DIM_HEAD)
            t = jnp.arange(n, dtype=jnp.float32)
            freqs = t[:, None] * inv_freq[None, :]
            freqs = jnp.concatenate([freqs, freqs], axis=-1)
            base = (half_idx + 0.4 * DIM_HEAD) / (1.4 * DIM_HEAD)
            power = (t - n // 2) / float(WINDOW // 2)
            scale = base[None, :] ** power[:, None]
            scale = jnp.concatenate([scale, scale], axis=-1)
            cos, sin = (jnp.cos(freqs), jnp.sin(freqs))
            q = q * cos * scale + rotate_half(q) * sin * scale
            k = k * cos / scale + rotate_half(k) * sin / scale
            return (q, k)

        def local_attention(q, k, v):
            b, h, n, d = q.shape
            w = n // WINDOW
            bq = q.reshape(b, h, w, WINDOW, d) * QK_SCALE
            bk = k.reshape(b, h, w, WINDOW, d)
            bv = v.reshape(b, h, w, WINDOW, d)

            def look_around(t):
                p = jnp.pad(t, ((0, 0), (0, 0), (1, 0), (0, 0), (0, 0)))
                return jnp.concatenate([p[:, :, :w], p[:, :, 1:]], axis=3)
            bk, bv = (look_around(bk), look_around(bv))
            bt = jnp.arange(n).reshape(w, WINDOW)
            btp = jnp.pad(bt, ((1, 0), (0, 0)), constant_values=-1)
            btk = jnp.concatenate([btp[:w], btp[1:]], axis=1)
            sim = jnp.einsum('bhwid,bhwjd->bhwij', bq, bk)
            i = bt[:, :, None]
            j = btk[:, None, :]
            mask = (i < j) | (i > j + WINDOW) | (j == -1)
            sim = jnp.where(mask, -jnp.finfo(sim.dtype).max, sim)
            attn = jax.nn.softmax(sim, axis=-1)
            out = jnp.einsum('bhwij,bhwjd->bhwid', attn, bv)
            return out.reshape(b, h, n, d)

        def _layer(x, wqkv, qs, ksc, wo, lg, lb, w1, b1, w2, b2):
            b, n, _ = x.shape
            h = shift_token(x)
            qkv = h @ wqkv
            q, k, v = jnp.split(qkv, 3, axis=-1)
            to_heads = lambda t: t.reshape(b, n, HEADS, DIM_HEAD).transpose(0, 2, 1, 3)
            q, k, v = (to_heads(q), to_heads(k), to_heads(v))
            q = l2norm(q) * qs
            k = l2norm(k) * ksc
            q, k = rotary_xpos(q, k)
            o = local_attention(q, k, v)
            o = o.transpose(0, 2, 1, 3).reshape(b, n, INNER)
            x = x + o @ wo
            h = shift_token(x)
            mu = h.mean(-1, keepdims=True)
            var = h.var(-1, keepdims=True)
            h = (h - mu) / jnp.sqrt(var + 1e-05) * lg + lb
            h = h @ w1 + b1
            a, g = jnp.split(h, 2, axis=-1)
            h = a * jax.nn.gelu(g, approximate=False)
            x = x + h @ w2 + b2
            return x
        for l in range(DEPTH):
            x = _layer(x, wqkv[l], q_scale[l], k_scale[l], wo[l], ln_g[l], ln_b[l], w1[l], b1[l], w2[l], b2[l])
        return x
    x = x + jnp.tanh(g_xattn[0]) * _L0_xattn_ref(_layernorm(x, axis=-1), ctx_1024, ctx_1024, L0_xattn_igate_w, L0_xattn_igate_b, L0_xattn_fgate_w, L0_xattn_fgate_b, L0_xattn_norm_w)
    x = x + jnp.tanh(g_ffn[0]) * _L0_ffn_ref(_layernorm(x, axis=-1), L0_ffn_w1_w, L0_ffn_w1_s, L0_ffn_w2_w, L0_ffn_w2_s, L0_ffn_h1_w, L0_ffn_h1_s, L0_ffn_h2_w, L0_ffn_h2_s, L0_ffn_w3_w, L0_ffn_w3_s)
    x = x + jnp.tanh(g_xattn[1]) * _L1_xattn_ref(_layernorm(x, axis=-1), ctx_1024, ctx_1024, mask_BxS_ik0, L1_xattn_wq, L1_xattn_bq, L1_xattn_wk, L1_xattn_bk, L1_xattn_wv, L1_xattn_bv, L1_xattn_wo, L1_xattn_bo)
    x = x + jnp.tanh(g_ffn[1]) * _L1_ffn_ref(_layernorm(x, axis=-1), L1_ffn_w_gate, L1_ffn_w_up, L1_ffn_w_down)
    x = x + jnp.tanh(g_xattn[2]) * _L2_xattn_ref(ctx_1024, ctx_1024, _layernorm(x, axis=-1), mask_Bx1xSxS2_ik1, L2_xattn_W_out, L2_xattn_b_out)
    x = x + jnp.tanh(g_ffn[2]) * _L2_ffn_ref(_layernorm(x, axis=-1), L2_ffn_Wg, L2_ffn_Wu, L2_ffn_Wd, L2_ffn_Wr, L2_ffn_temperature)
    x = x + jnp.tanh(g_xattn[3]) * _L3_xattn_ref(_layernorm(x, axis=-1), ctx_1024, ctx_1024, mask_BxS2_ik1, L3_xattn_Wq_w, L3_xattn_Wq_b, L3_xattn_Wk_w, L3_xattn_Wk_b)
    x = x + jnp.tanh(g_ffn[3]) * _L3_ffn_ref(_layernorm(x, axis=-1), L3_ffn_wqkv, L3_ffn_q_scale, L3_ffn_k_scale, L3_ffn_wo, L3_ffn_ln_g, L3_ffn_ln_b, L3_ffn_w1, L3_ffn_b1, L3_ffn_w2, L3_ffn_b2)
    return x

_drawn_inputs = setup_inputs


def setup_inputs(seed=0):
    import zlib

    import numpy as np

    out = dict(_drawn_inputs(seed))
    spreads = {'L1_xattn_bq': (0.0, 0.1),
     'L1_xattn_bk': (0.0, 0.1),
     'L1_xattn_bv': (0.0, 0.1),
     'L1_xattn_bo': (0.0, 0.1),
     'L3_xattn_Wq_b': (0.0, 0.1),
     'L3_xattn_Wk_b': (0.0, 0.1),
     'L3_ffn_q_scale': (1.0, 0.2),
     'L3_ffn_k_scale': (1.0, 0.2),
     'L3_ffn_ln_g': (1.0, 0.2),
     'L3_ffn_ln_b': (0.0, 0.1),
     'L3_ffn_b1': (0.0, 0.1),
     'L3_ffn_b2': (0.0, 0.1)}
    factors = {}
    for name, (base, spread) in spreads.items():
        noise = np.random.default_rng([zlib.crc32(name.encode()), seed]).standard_normal(out[name].shape)
        drawn = base * np.exp(spread * noise) if base else spread * noise
        out[name] = jnp.asarray(drawn.astype(out[name].dtype))
    for name, factor in factors.items():
        out[name] = (out[name] * factor).astype(out[name].dtype)
    return out
```

```python
from contextlib import ExitStack

import numpy as np

import concourse.bass as bass
from concourse import mybir

F32 = mybir.dt.float32
BF16 = mybir.dt.bfloat16
I32 = mybir.dt.int32
I16 = mybir.dt.int16
ALU = mybir.AluOpType
ACT = mybir.ActivationFunctionType
AX = mybir.AxisListType.X

P = 128
S = 64
NB = 128
NT = NB * S // P
PAIRS = NT // 2
CH = 512
NCH = NB * S // CH
TPC = CH // P
NEG = -1e30
ROUND = 12582912.0


class Stage:

    def __init__(self, nc, name):
        self.nc, self.name, self.stack, self.sems = nc, name, ExitStack(), []

    def __enter__(self):
        return self

    def __exit__(self, *exc):
        if exc[0] is None:
            self.nc.clear_and_free_semaphores(self.sems)
            self.nc.all_engine_barrier()
            self.stack.close()

    def sb(self, name, shape, dt=F32):
        return self.stack.enter_context(self.nc.sbuf_tensor(f"{self.name}_{name}", list(shape), dt))

    def two(self, name, shape, dt=F32):
        return [self.sb(f"{name}{j}", shape, dt) for j in range(2)]

    def sem(self, name):
        self.sems.append(self.nc.alloc_semaphore(f"{self.name}_{name}"))
        return self.sems[-1]

    def sem2(self, name):
        return [self.sem(f"{name}{j}") for j in range(2)]


def setup(nc, m, d):
    with Stage(nc, "setup") as st:
        loaded, filled = st.sem("loaded"), st.sem("filled")
        consts = [(m.ident, d["c_ident"]), (m.blockones, d["c_blockones"]), (m.tri, d["c_tri"]),
                  (m.shift, d["c_shift"]), (m.eye64, d["c_eye64"]), (m.causal, d["c_causal"]),
                  (m.half, d["c_half"]), (m.head16, d["c_head16"]), (m.head8, d["c_head8"]), (m.gates, d["gates"])]
        n_loads = 16 * (1 + len(consts))
        with nc.Block() as block:
            @block.sync
            def _(sp):
                sp.dma_start(m.X[:], d["x"]).then_inc(loaded, 16)
                for tile, src in consts:
                    sp.dma_start(tile[:], src).then_inc(loaded, 16)

            @block.scalar
            def _(act):
                act.wait_ge(loaded, n_loads)
                act.activation(m.tanh_g[:], m.gates[:], ACT.Tanh)
                act.copy(m.ident_bf[:], m.ident[:])
                act.copy(m.causal_bf[:], m.causal[:])
                act.wait_ge(filled, 1)

            @block.vector
            def _(dve):
                dve.memset(m.ones_row[:], 1.0).then_inc(filled, 1)
                dve.wait_ge(loaded, n_loads)
                with dve.Fori(0, NT) as t:
                    dve.bn_stats(m.S6[:, t, :], m.X[:, t, :])


def norm_header(nc, m, name, s6=None):
    s6 = m.S6 if s6 is None else s6
    with Stage(nc, name) as st:
        delta, spread = st.sb("delta", [P, NT]), st.sb("spread", [P, NT])
        step, rooted = st.sem("step"), st.sem("rooted")
        mean_e, m2_e, mean_o, m2_o = (s6[:, :, k] for k in (1, 2, 4, 5))
        with nc.Block() as block:
            @block.vector
            def _(dve):
                dve.tensor_tensor(m.mean[:], mean_e, mean_o, ALU.add)
                dve.tensor_tensor(delta[:], mean_e, mean_o, ALU.subtract)
                dve.tensor_tensor(spread[:], m2_e, m2_o, ALU.add).then_inc(step, 1)
                dve.wait_ge(step, 1)
                dve.tensor_scalar(m.mean[:], m.mean[:], 0.5, None, ALU.mult)
                dve.scalar_tensor_tensor(delta[:], delta[:], 0.25, delta[:], ALU.mult, ALU.mult)
                dve.tensor_scalar(spread[:], spread[:], 1.0 / P, 1e-5, ALU.mult, ALU.add).then_inc(step, 1)
                dve.wait_ge(step, 2)
                dve.tensor_tensor(spread[:], spread[:], delta[:], ALU.add).then_inc(step, 1)
                dve.wait_ge(rooted, 1)
                dve.reciprocal(m.rstd[:], delta[:])

            @block.scalar
            def _(act):
                act.wait_ge(step, 3)
                act.activation(delta[:], spread[:], ACT.Sqrt).then_inc(rooted, 1)


def normed(dve, m, dst, t, src=None):
    src = m.X if src is None else src
    return dve.tensor_scalar(dst, src[:, t, :], m.mean[:, bass.ds(t, 1)], m.rstd[:, bass.ds(t, 1)],
                             ALU.subtract, ALU.mult)


def per_head(ap, h, w):
    return ap.rearrange("p (h w) -> p h w", h=h, w=w)


def spread_heads(ap, w):
    return ap[:, :, None].broadcast_to([ap.shape[0], ap.shape[1], w])


def repeat_heads(ap, h):
    return ap[:, None, :].broadcast_to([ap.shape[0], h, ap.shape[1]])


def gated_memory(nc, m, d):
    H, W = 8, 16
    KW = H * S

    with Stage(nc, "gates") as st:
        wq, wk, wv = st.sb("wq", [P, 2 * H]), st.sb("wk", [P, 2 * H]), st.sb("wv", [P, 2 * H])
        bias, weights = st.sb("bias", [P, 2 * H]), st.sem("weights")
        xn, xnT, ctxT = st.two("xn", [P, P]), st.two("xnT", [P, P]), st.two("ctxT", [P, P])
        ctx_in, normed_x, turned, copied = (st.sem2(n) for n in ("ctx_in", "normed_x", "turned", "copied"))
        summed, biased = st.sem2("summed"), st.sem2("biased")
        with nc.Block() as block:
            @block.sync
            def _(sp):
                for tile, src in ((wq, "l0_gate_q"), (wk, "l0_gate_k"), (wv, "l0_gate_v"), (bias, "l0_gate_b")):
                    sp.dma_start(tile[:], d[src]).then_inc(weights, 16)
                with sp.Fori(0, PAIRS) as it:
                    for j in range(2):
                        sp.wait_ge(summed[j], it)
                        sp.dma_start(ctxT[j][:], d["ctxT"][it * 2 + j]).then_inc(ctx_in[j], 16)

            @block.vector
            def _(dve):
                dve.wait_ge(weights, 64)
                with dve.Fori(0, PAIRS) as it:
                    for j in range(2):
                        dve.wait_ge(turned[j], it)
                        normed(dve, m, xn[j][:], it * 2 + j).then_inc(normed_x[j], 1)
                    for j in range(2):
                        dve.wait_ge(summed[j], it + 1)
                        dve.tensor_tensor(m.gate[:, it * 2 + j, :], m.B[j][:, 0:2 * H], bias[:],
                                          ALU.add).then_inc(biased[j], 1)

            @block.tensor
            def _(pe):
                pe.wait_ge(weights, 64)
                with pe.Fori(0, PAIRS) as it:
                    for j in range(2):
                        pe.wait_ge(normed_x[j], it + 1)
                        pe.wait_ge(copied[j], it)
                        pe.transpose(m.A[j][:, 0:P], xn[j][:], m.ident[:]).then_inc(turned[j], 1)
                    for j in range(2):
                        pe.wait_ge(copied[j], it + 1)
                        pe.wait_ge(ctx_in[j], it * 16 + 16)
                        pe.wait_ge(biased[j], it)
                        g = m.B[j][:, 0:2 * H]
                        pe.matmul(g, xnT[j][:], wq[:], start=True, stop=False)
                        pe.matmul(g, ctxT[j][:], wk[:], start=False, stop=False)
                        pe.matmul(g, ctxT[j][:], wv[:], start=False, stop=True).then_inc(summed[j], 1)

            @block.scalar
            def _(act):
                with act.Fori(0, PAIRS) as it:
                    for j in range(2):
                        act.wait_ge(turned[j], it + 1)
                        act.wait_ge(summed[j], it)
                        act.copy(xnT[j][:], m.A[j][:, 0:P]).then_inc(copied[j], 1)

    with Stage(nc, "decay") as st:
        f0, l0 = st.sb("f0", [P, NT, H]), st.sb("l0", [P, NT, H])
        step, logged, cum = st.sem("step"), st.sem("logged"), st.sem("cum")
        forget = m.gate[:, :, H:2 * H]
        flat = lambda x: x[:].rearrange("p t h -> p (t h)")
        with nc.Block() as block:
            @block.vector
            def _(dve):
                dve.scalar_tensor_tensor(f0[:], forget, -1.0, forget, ALU.mult, ALU.min).then_inc(step, 1)
                dve.wait_ge(logged, 2)
                dve.scalar_tensor_tensor(f0[:], forget, 0.0, l0[:], ALU.min, ALU.subtract).then_inc(step, 1)
                dve.wait_ge(cum, 1)
                sums = m.A[0][:, 0:NT * H].rearrange("p (t h) -> p t h", t=NT)
                dve.tensor_copy(m.fsum[:], sums)
                dve.tensor_tensor(m.a[:], m.gate[:, :, 0:H], sums, ALU.subtract)

            @block.scalar
            def _(act):
                act.wait_ge(step, 1)
                act.activation(l0[:], f0[:], ACT.Exp).then_inc(logged, 1)
                act.wait_ge(logged, 1)
                act.activation(l0[:], l0[:], ACT.Ln, bias=1.0).then_inc(logged, 1)

            @block.tensor
            def _(pe):
                pe.wait_ge(step, 2)
                pe.matmul(m.A[0][:, 0:NT * H], m.tri[:], flat(f0), start=True, stop=True).then_inc(cum, 1)

    with Stage(nc, "memory") as st:
        xn, qT, ctxT = st.two("xn", [P, P]), st.two("qT", [P, P]), st.two("ctxT", [P, P])
        ctx2 = st.two("ctx2", [P, 2, P])
        kx = st.two("kx", [P, 2, H, S])
        ax = st.two("ax", [P, H, S])
        vd = st.two("vd", [P, 2, H // 2, 2, W + 1])
        dmat, cT = st.two("dmat", [P, H, S]), st.two("cT", [P, H // 2, P])
        top, low, den = st.two("top", [P, H]), st.two("low", [P, H]), st.two("den", [P, H])
        names = ("ctx_in ctx2_in normed_x turned copied keys_apart a_apart values_apart scored z_done max_done"
                 " shifted exped weighted c_turned c_copied mixed floor_in floored den_abs den_max den_eps den_inv"
                 " h_done")
        e = {n: st.sem2(n) for n in names.split()}
        ctx_in, ctx2_in, normed_x, turned, copied = (e[n] for n in ("ctx_in", "ctx2_in", "normed_x", "turned", "copied"))
        ones_set = st.sem("ones_set")
        with nc.Block() as block:
            @block.sync
            def _(sp):
                with sp.Fori(0, PAIRS) as it:
                    for j in range(2):
                        sp.wait_ge(e["keys_apart"][j], it)
                        sp.dma_start(ctxT[j][:], d["ctxT"][it * 2 + j]).then_inc(ctx_in[j], 16)
                        sp.wait_ge(e["values_apart"][j], it)
                        for half in range(2):
                            sp.dma_start(ctx2[j][half * S:half * S + S], d["ctx"][:, bass.ds(it * 4 + 2 * j, 2), :])\
                              .then_inc(ctx2_in[j], 16)

            @block.gpsimd
            def _(pool):
                for j in range(2):
                    for b in range(2):
                        pool.tensor_copy(vd[j][:, b, :, :, W], repeat_heads(m.half[:], H // 2)).then_inc(ones_set, 1)
                with pool.Fori(0, PAIRS) as it:
                    for j in range(2):
                        pool.wait_ge(ctx_in[j], it * 16 + 16)
                        pool.wait_ge(e["scored"][j], it)
                        for b in range(2):
                            last = pool.tensor_tensor(kx[j][:, b], repeat_heads(ctxT[j][:, b * S:b * S + S], H),
                                                      spread_heads(m.head8[:], S), ALU.mult)
                        last.then_inc(e["keys_apart"][j], 1)
                        pool.wait_ge(e["z_done"][j], it)
                        pool.tensor_tensor(ax[j][:], spread_heads(m.a[:, it * 2 + j, :], S),
                                           repeat_heads(m.eye64[:], H), ALU.mult).then_inc(e["a_apart"][j], 1)
                        pool.wait_ge(ctx2_in[j], it * 32 + 32)
                        pool.wait_ge(e["mixed"][j], it)
                        for b in range(2):
                            last = pool.tensor_tensor(
                                vd[j][:, b, :, :, 0:W], ctx2[j][:, b].rearrange("p (g u w) -> p g u w", g=H // 2, u=2),
                                m.half[:, None, :, None].broadcast_to([P, H // 2, 2, W]), ALU.mult)
                        last.then_inc(e["values_apart"][j], 1)

            @block.vector
            def _(dve):
                with dve.Fori(0, PAIRS) as it:
                    for j in range(2):
                        dve.wait_ge(turned[j], it)
                        normed(dve, m, xn[j][:], it * 2 + j).then_inc(normed_x[j], 1)
                    for j in range(2):
                        z = per_head(m.B[j][:, 0:KW], H, S)
                        dve.wait_ge(e["z_done"][j], it + 1)
                        dve.wait_ge(e["floored"][j], it)
                        dve.tensor_reduce(top[j][:], z, AX, ALU.max).then_inc(e["max_done"][j], 1)
                        dve.wait_ge(e["max_done"][j], it + 1)
                        dve.wait_ge(e["weighted"][j], it)
                        dve.tensor_tensor(dmat[j][:], z, spread_heads(top[j][:], S), ALU.subtract)\
                           .then_inc(e["shifted"][j], 1)
                        dve.wait_ge(e["floored"][j], it)
                        dve.tensor_tensor(low[j][:], top[j][:], m.fsum[:, it * 2 + j, :], ALU.add)\
                           .then_inc(e["floor_in"][j], 1)
                    for j in range(2):
                        dve.wait_ge(e["exped"][j], it + 1)
                        dve.wait_ge(e["scored"][j], it + 1)
                        dve.wait_ge(e["c_turned"][j], it)
                        dve.tensor_tensor(dmat[j][:], per_head(m.A[j][:, 512:512 + KW], H, S), dmat[j][:], ALU.mult)\
                           .then_inc(e["weighted"][j], 1)
                    for j in range(2):
                        out = m.A[j][:, 0:H * (W + 1)].rearrange("p (h w) -> p h w", h=H)
                        dve.wait_ge(e["mixed"][j], it + 1)
                        dve.tensor_reduce(den[j][:], out[:, :, W:W + 1], AX, ALU.max, apply_absolute_value=True).then_inc(e["den_abs"][j], 1)
                        dve.wait_ge(e["den_abs"][j], it + 1)
                        dve.wait_ge(e["floored"][j], it + 1)
                        dve.tensor_tensor(den[j][:], den[j][:], low[j][:], ALU.max).then_inc(e["den_max"][j], 1)
                        dve.wait_ge(e["den_max"][j], it + 1)
                        dve.tensor_scalar(den[j][:], den[j][:], 1e-6, None, ALU.add).then_inc(e["den_eps"][j], 1)
                        dve.wait_ge(e["den_eps"][j], it + 1)
                        dve.reciprocal(den[j][:], den[j][:]).then_inc(e["den_inv"][j], 1)
                        dve.wait_ge(e["den_inv"][j], it + 1)
                        dve.tensor_tensor(per_head(m.h[:, it * 2 + j, :], H, W), out[:, :, 0:W],
                                          spread_heads(den[j][:], W), ALU.mult).then_inc(e["h_done"][j], 1)

            @block.scalar
            def _(act):
                with act.Fori(0, PAIRS) as it:
                    for j in range(2):
                        act.wait_ge(turned[j], it + 1)
                        act.wait_ge(e["scored"][j], it)
                        act.activation(qT[j][:], m.A[j][:, 0:P], ACT.Copy, scale=float(W) ** -0.5).then_inc(copied[j], 1)
                    for j in range(2):
                        act.wait_ge(e["shifted"][j], it + 1)
                        act.activation(dmat[j][:], dmat[j][:], ACT.Exp).then_inc(e["exped"][j], 1)
                        act.wait_ge(e["floor_in"][j], it + 1)
                        act.wait_ge(e["den_max"][j], it)
                        act.activation(low[j][:], low[j][:], ACT.Exp, scale=-1.0).then_inc(e["floored"][j], 1)
                    for j in range(2):
                        act.wait_ge(e["c_turned"][j], it + 1)
                        act.wait_ge(e["mixed"][j], it)
                        act.copy(cT[j][:], m.B[j][:, 512:512 + KW].rearrange("p (g q) -> p g q", q=P))\
                           .then_inc(e["c_copied"][j], 1)

            @block.tensor
            def _(pe):
                pe.wait_ge(ones_set, 4)
                with pe.Fori(0, PAIRS) as it:
                    for j in range(2):
                        pe.wait_ge(normed_x[j], it + 1)
                        pe.wait_ge(e["h_done"][j], it)
                        pe.transpose(m.A[j][:, 0:P], xn[j][:], m.ident[:]).then_inc(turned[j], 1)
                    for j in range(2):
                        pe.wait_ge(e["a_apart"][j], it + 1)
                        pe.wait_ge(e["shifted"][j], it)
                        pe.matmul(m.B[j][:, 0:KW], m.blockones[:], ax[j][:], start=True, stop=False)
                        pe.matmul(m.B[j][:, 0:KW], m.ident_bf[:], repeat_heads(m.causal_bf[:], H),
                                  start=False, stop=True).then_inc(e["z_done"][j], 1)
                        pe.wait_ge(copied[j], it + 1)
                        pe.wait_ge(e["keys_apart"][j], it + 1)
                        pe.wait_ge(e["weighted"][j], it)
                        for b in range(2):
                            last = pe.matmul(m.A[j][b * S:b * S + S, 512:512 + KW], qT[j][:, b * S:b * S + S],
                                             kx[j][:, b], start=True, stop=True)
                        last.then_inc(e["scored"][j], 1)
                    for j in range(2):
                        pe.wait_ge(e["weighted"][j], it + 1)
                        pe.wait_ge(e["c_copied"][j], it)
                        c = dmat[j][:].rearrange("p h k -> p (h k)")
                        for g in range(H // 2):
                            last = pe.transpose(m.B[j][:, 512 + g * P:512 + g * P + P], c[:, g * P:g * P + P], m.ident[:])
                        last.then_inc(e["c_turned"][j], 1)
                    for j in range(2):
                        pe.wait_ge(e["c_copied"][j], it + 1)
                        pe.wait_ge(e["values_apart"][j], it + 1)
                        for b in range(2):
                            for g in range(H // 2):
                                n = 2 * (W + 1)
                                last = pe.matmul(m.A[j][b * S:b * S + S, g * n:g * n + n], cT[j][:, g, b * S:b * S + S],
                                                 vd[j][:, b, g], start=True, stop=True)
                        last.then_inc(e["mixed"][j], 1)

    with Stage(nc, "headnorm") as st:
        G = 8
        STEPS = NT // G
        w = st.sb("w", [P, P])
        mean, var, sq = st.sb("mean", [P, G, H]), st.sb("var", [P, G, H]), st.sb("sq", [P, G * H, W])
        loaded, scaled, step, root, added = (st.sem(n) for n in ("loaded", "scaled", "step", "root", "added"))
        with nc.Block() as block:
            @block.sync
            def _(sp):
                sp.dma_start(w[:], d["l0_norm_w"]).then_inc(loaded, 16)

            @block.vector
            def _(dve):
                dve.wait_ge(loaded, 16)
                dve.tensor_scalar(w[:], w[:], m.tanh_g[:, 0:1], None, ALU.mult).then_inc(scaled, 1)
                dve.wait_ge(scaled, 1)
                with dve.Fori(0, STEPS) as it:
                    hs = m.h[:, bass.ds(it * G, G), :]
                    heads = hs.rearrange("p t (h w) -> p (t h) w", h=H)
                    flat = lambda x: x[:].rearrange("p t h -> p (t h)")
                    base = it * 7
                    dve.tensor_reduce(flat(mean), heads, AX, ALU.add).then_inc(step, 1)
                    dve.wait_ge(step, base + 1)
                    dve.tensor_scalar(flat(mean), flat(mean), 1.0 / W, None, ALU.mult).then_inc(step, 1)
                    dve.wait_ge(step, base + 2)
                    dve.tensor_tensor(heads, heads, spread_heads(flat(mean), W), ALU.subtract).then_inc(step, 1)
                    dve.wait_ge(step, base + 3)
                    dve.tensor_tensor(sq[:], heads, heads, ALU.mult).then_inc(step, 1)
                    dve.wait_ge(step, base + 4)
                    dve.tensor_reduce(flat(var), sq[:], AX, ALU.add).then_inc(step, 1)
                    dve.wait_ge(step, base + 5)
                    dve.tensor_scalar(flat(var), flat(var), 1.0 / W, 1e-5, ALU.mult, ALU.add).then_inc(step, 1)
                    dve.wait_ge(root, it + 1)
                    dve.reciprocal(flat(mean), flat(mean)).then_inc(step, 1)
                    dve.wait_ge(step, base + 7)
                    dve.tensor_tensor(heads, heads, spread_heads(flat(mean), W), ALU.mult).then_inc(added, 1)
                    dve.wait_ge(added, it * 3 + 1)
                    dve.tensor_tensor(hs, hs, repeat_heads(w[:], G), ALU.mult).then_inc(added, 1)
                    dve.wait_ge(added, it * 3 + 2)
                    xs = m.X[:, bass.ds(it * G, G), :]
                    dve.tensor_tensor(xs, xs, hs, ALU.add).then_inc(added, 1)
                    dve.wait_ge(added, it * 3 + 3)
                    for k in range(G):
                        dve.bn_stats(m.S6[:, it * G + k, :], m.X[:, it * G + k, :])

            @block.scalar
            def _(act):
                with act.Fori(0, STEPS) as it:
                    act.wait_ge(step, it * 7 + 6)
                    act.activation(mean[:], var[:], ACT.Sqrt).then_inc(root, 1)


def feature_major(nc, m, name, dst, router=None):
    with Stage(nc, name) as st:
        xn, xnT = st.two("xn", [P, P]), st.two("xnT", [P, P])
        normed_x, turned, copied, placed = (st.sem2(n) for n in ("normed_x", "turned", "copied", "placed"))
        routed, kept = st.sem2("routed"), st.sem2("kept")
        with nc.Block() as block:
            @block.vector
            def _(dve):
                with dve.Fori(0, PAIRS) as it:
                    for j in range(2):
                        dve.wait_ge(turned[j], it)
                        normed(dve, m, xn[j][:], it * 2 + j).then_inc(normed_x[j], 1)
                    if router:
                        for j in range(2):
                            dve.wait_ge(routed[j], it + 1)
                            dve.tensor_copy(router[1][:, it * 2 + j, :], m.B[j][:, 0:8]).then_inc(kept[j], 1)

            @block.tensor
            def _(pe):
                with pe.Fori(0, PAIRS) as it:
                    for j in range(2):
                        pe.wait_ge(normed_x[j], it + 1)
                        pe.wait_ge(copied[j], it)
                        pe.transpose(m.A[j][:, 0:P], xn[j][:], m.ident[:]).then_inc(turned[j], 1)
                    if router:
                        for j in range(2):
                            pe.wait_ge(copied[j], it + 1)
                            pe.wait_ge(kept[j], it)
                            pe.matmul(m.B[j][:, 0:8], xnT[j][:], router[0][:], start=True, stop=True)\
                              .then_inc(routed[j], 1)

            @block.scalar
            def _(act):
                with act.Fori(0, PAIRS) as it:
                    for j in range(2):
                        act.wait_ge(turned[j], it + 1)
                        act.wait_ge(placed[j], it)
                        if router:
                            act.wait_ge(routed[j], it)
                        act.copy(xnT[j][:], m.A[j][:, 0:P]).then_inc(copied[j], 1)

            @block.gpsimd
            def _(pool):
                with pool.Fori(0, PAIRS) as it:
                    for j in range(2):
                        pool.wait_ge(copied[j], it + 1)
                        pool.tensor_copy(dst[:, it * 2 + j, :], xnT[j][:]).then_inc(placed[j], 1)


def add_tiles(dve, m, added, count, it, first, y):
    xs = m.X[:, bass.ds(first, TPC), :]
    dve.tensor_tensor(xs, xs, y, ALU.add).then_inc(added, 1)
    dve.wait_ge(added, count)
    for k in range(TPC):
        last = dve.bn_stats(m.S6[:, first + k, :], m.X[:, first + k, :])
    return last


def l0_ffn(nc, m, d, own):
    F = 4
    xnT = own.enter_context(nc.sbuf_tensor("l0f_xnT", [P, NT, P], F32))
    feature_major(nc, m, "l0f_turn", xnT)
    with Stage(nc, "l0f") as st:
        w1, w2 = st.sb("w1", [P, F * P]), st.sb("w2", [P, F * P])
        h1, h2, w3 = st.sb("h1", [P, F, F * P]), st.sb("h2", [P, F, F * P]), st.sb("w3", [P, F, P])
        s = st.sb("s", [P, 4, F])
        s3 = st.sb("s3", [P, P])
        gate, hid, mid, y = (st.two(n, [P, F, CH]) for n in ("gate", "hid", "mid", "y"))
        loaded, scaled = st.sem("loaded"), st.sem("scaled")
        up, silued, hidden, sum1, act1, sum2, act2 = (
            st.sem2(n) for n in ("up", "silued", "hidden", "sum1", "act1", "sum2", "act2"))
        down, scaled_y, added = st.sem2("down"), st.sem2("scaled_y"), st.sem2("added")
        banks = [m.A[0][:, 0:CH], m.A[0][:, CH:2 * CH], m.B[0][:, 0:CH], m.B[0][:, CH:2 * CH]], \
                [m.A[1][:, 0:CH], m.A[1][:, CH:2 * CH], m.B[1][:, 0:CH], m.B[1][:, CH:2 * CH]]
        srcs = [(w1, "l0f_w1"), (w2, "l0f_w2"), (h1, "l0f_h1"), (h2, "l0f_h2"), (w3, "l0f_w3"), (s, "l0f_s"),
                (s3, "l0f_s3")]
        with nc.Block() as block:
            @block.sync
            def _(sp):
                for tile, src in srcs:
                    sp.dma_start(tile[:], d[src]).then_inc(loaded, 16)

            @block.tensor
            def _(pe):
                pe.wait_ge(loaded, 16 * len(srcs))
                with pe.Fori(0, NCH // 2) as it:
                    for j in range(2):
                        x = xnT[:, bass.ds(it * 8 + 4 * j, TPC), :]
                        for o in range(F):
                            if o == 0:
                                pe.wait_ge(scaled_y[j], it)
                            if o >= 2:
                                pe.wait_ge(hidden[j], it * 4 + o - 1)
                            c = slice(o * P, o * P + P)
                            pe.matmul(banks[j][2 * (o % 2)], w1[:, c], x, start=True, stop=True)
                            pe.matmul(banks[j][2 * (o % 2) + 1], w2[:, c], x, start=True, stop=True)\
                              .then_inc(up[j], 1)
                    for weights, src, ready, done in ((h1, hid, hidden, sum1), (h2, mid, act1, sum2)):
                        for j in range(2):
                            pe.wait_ge(ready[j], it * 4 + 4)
                            for o in range(F):
                                for k in range(F):
                                    last = pe.matmul(banks[j][o], weights[:, k, o * P:o * P + P], src[j][:, k],
                                                     start=(k == 0), stop=(k == F - 1))
                                last.then_inc(done[j], 1)
                    for j in range(2):
                        pe.wait_ge(act2[j], it * 4 + 4)
                        for t in range(TPC):
                            for k in range(F):
                                last = pe.matmul(banks[j][0][:, t * P:t * P + P], hid[j][:, k, t * P:t * P + P],
                                                 w3[:, k], start=(k == 0), stop=(k == F - 1))
                        last.then_inc(down[j], 1)

            @block.scalar
            def _(act):
                act.wait_ge(loaded, 16 * len(srcs))
                with act.Fori(0, NCH // 2) as it:
                    for j in range(2):
                        for o in range(F):
                            act.wait_ge(up[j], it * 4 + o + 1)
                            act.activation(gate[j][:, o], banks[j][2 * (o % 2)], ACT.Silu, scale=s[:, 0, o:o + 1])\
                               .then_inc(silued[j], 1)
                    for n, ready, dst, done in ((2, sum1, mid, act1), (3, sum2, hid, act2)):
                        for j in range(2):
                            for o in range(F):
                                act.wait_ge(ready[j], it * 4 + o + 1)
                                act.activation(dst[j][:, o], banks[j][o], ACT.Gelu, scale=s[:, n, o:o + 1])\
                                   .then_inc(done[j], 1)

            @block.vector
            def _(dve):
                dve.wait_ge(loaded, 16 * len(srcs))
                dve.tensor_scalar(s3[:], s3[:], m.tanh_g[:, 4:5], None, ALU.mult).then_inc(scaled, 1)
                dve.wait_ge(scaled, 1)
                with dve.Fori(0, NCH // 2) as it:
                    for j in range(2):
                        for o in range(F):
                            dve.wait_ge(silued[j], it * 4 + o + 1)
                            dve.scalar_tensor_tensor(hid[j][:, o], banks[j][2 * (o % 2) + 1], s[:, 1, o:o + 1],
                                                     gate[j][:, o], ALU.mult, ALU.mult).then_inc(hidden[j], 1)
                    for j in range(2):
                        dve.wait_ge(down[j], it + 1)
                        out = banks[j][0].rearrange("p (t w) -> p t w", t=TPC)
                        z = y[j][:, 0].rearrange("p (t w) -> p t w", t=TPC)
                        dve.tensor_tensor(z, out, repeat_heads(s3[:], TPC), ALU.mult).then_inc(scaled_y[j], 1)
                        dve.wait_ge(scaled_y[j], it + 1)
                        add_tiles(dve, m, added[j], it + 1, it, it * 8 + 4 * j, z)


def l2_ffn(nc, m, d, own):
    E = 8
    LOWER, UPPER, CENTER = 0.5 - float(np.log(4.0 / 3.0)), 0.5, 1.0 / float(np.e)
    xnT = own.enter_context(nc.sbuf_tensor("l2f_xnT", [P, NT, P], F32))
    wr = own.enter_context(nc.sbuf_tensor("l2f_wr", [P, E], F32))
    mix = own.enter_context(nc.sbuf_tensor("l2f_mix", [P, NT, E], F32))
    temp = own.enter_context(nc.sbuf_tensor("l2f_temp", [P, 1], F32))
    lower_e = own.enter_context(nc.sbuf_tensor("l2f_lower_e", [P, E, E], F32))
    with Stage(nc, "l2f_in") as st:
        loaded = st.sem("loaded")
        with nc.Block() as block:
            @block.sync
            def _(sp):
                for tile, src in ((wr, "l2f_wr"), (temp, "l2f_temp"), (lower_e, "c_lower_e")):
                    sp.dma_start(tile[:], d[src]).then_inc(loaded, 16)
                sp.wait_ge(loaded, 48)
    feature_major(nc, m, "l2f_turn", xnT, router=(wr, mix))

    with Stage(nc, "route") as st:
        inh, w, fb, mask, dist = (st.sb(n, [P, NT, E]) for n in ("inh", "w", "fb", "mask", "dist"))
        above, equal = st.sb("above", [P, NT, E, E]), st.sb("equal", [P, NT, E, E])
        total, none, some = st.sb("total", [P, NT]), st.sb("none", [P, NT]), st.sb("some", [P, NT])
        flat = lambda x: x[:].rearrange("p t e -> p (t e)")
        step, exped = st.sem("step"), st.sem("exped")
        with nc.Block() as block:
            @block.vector
            def _(dve):
                count = [0]

                def then(ins):
                    count[0] += 1
                    ins.then_inc(step, 1)
                    dve.wait_ge(step, count[0])

                then(dve.reciprocal(temp[:], temp[:]))
                then(dve.tensor_scalar(flat(mix), flat(mix), temp[:], None, ALU.mult))
                dve.wait_ge(exped, 1)
                then(dve.tensor_scalar(flat(inh), flat(inh), 1.0, None, ALU.add))
                then(dve.reciprocal(flat(inh), flat(inh)))
                then(dve.tensor_scalar(flat(mask), flat(inh), LOWER, None, ALU.is_ge))
                then(dve.scalar_tensor_tensor(flat(mask), flat(inh), UPPER, flat(mask), ALU.is_le, ALU.mult))
                then(dve.tensor_scalar(flat(inh), flat(inh), CENTER, None, ALU.subtract))
                then(dve.scalar_tensor_tensor(flat(dist), flat(inh), -1.0, flat(inh), ALU.mult, ALU.max))
                dve.wait_ge(exped, 3)
                then(dve.tensor_tensor(flat(w), flat(w), flat(mask), ALU.mult))
                then(dve.tensor_reduce(total[:], w[:], AX, ALU.add))
                then(dve.tensor_scalar(none[:], total[:], 1e-8, None, ALU.is_lt))
                then(dve.tensor_scalar(some[:], none[:], -1.0, 1.0, ALU.mult, ALU.add))
                mine = fb[:, :, :, None].broadcast_to([P, NT, E, E])
                theirs = fb[:, :, None, :].broadcast_to([P, NT, E, E])
                then(dve.tensor_tensor(above[:], theirs, mine, ALU.is_gt))
                then(dve.tensor_tensor(equal[:], theirs, mine, ALU.is_equal))
                then(dve.tensor_tensor(equal[:], equal[:], lower_e[:, None, :, :].broadcast_to([P, NT, E, E]), ALU.mult))
                then(dve.tensor_tensor(above[:], above[:], equal[:], ALU.add))
                then(dve.tensor_reduce(mask[:], above[:], AX, ALU.add))
                then(dve.scalar_tensor_tensor(flat(fb), flat(mask), 2.0, flat(fb), ALU.is_lt, ALU.mult))
                then(dve.tensor_reduce(total[:], fb[:], AX, ALU.add))
                then(dve.tensor_scalar(total[:], total[:], 1e-8, None, ALU.max))
                then(dve.reciprocal(total[:], total[:]))
                then(dve.tensor_tensor(total[:], total[:], none[:], ALU.mult))
                then(dve.tensor_tensor(fb[:], fb[:], spread_heads(total[:], E), ALU.mult))
                then(dve.tensor_tensor(w[:], w[:], spread_heads(some[:], E), ALU.mult))
                then(dve.tensor_tensor(flat(w), flat(w), flat(fb), ALU.add))
                then(dve.tensor_reduce(total[:], w[:], AX, ALU.add))
                then(dve.tensor_scalar(total[:], total[:], 1e-8, None, ALU.max))
                then(dve.reciprocal(total[:], total[:]))
                then(dve.tensor_scalar(total[:], total[:], m.tanh_g[:, 6:7], None, ALU.mult))
                dve.tensor_tensor(mix[:], w[:], spread_heads(total[:], E), ALU.mult)

            @block.scalar
            def _(act):
                act.wait_ge(step, 2)
                act.activation(inh[:], mix[:], ACT.Exp, scale=-1.0).then_inc(exped, 1)
                act.wait_ge(step, 8)
                act.activation(w[:], dist[:], ACT.Exp, scale=-10.0).then_inc(exped, 1)
                act.activation(fb[:], dist[:], ACT.Exp, scale=-1.0 / 0.3).then_inc(exped, 1)

    with Stage(nc, "l2f") as st:
        wg, wu, wd = (st.sb(n, [P, E, P]) for n in ("wg", "wu", "wd"))
        gate, hid = st.two("gate", [P, 2, CH]), st.two("hid", [P, 2, CH])
        loaded = st.sem("loaded")
        up, silued, hidden, down, added = (st.sem2(n) for n in ("up", "silued", "hidden", "down", "added"))
        stats = st.sem("stats")
        bank = lambda j, e, n: (m.A, m.B)[e % 2][j][:, n * CH:n * CH + CH]
        with nc.Block() as block:
            @block.sync
            def _(sp):
                for tile, src in ((wg, "l2f_wg"), (wu, "l2f_wu"), (wd, "l2f_wd")):
                    sp.dma_start(tile[:], d[src]).then_inc(loaded, 16)

            @block.tensor
            def _(pe):
                pe.wait_ge(loaded, 48)
                with pe.Fori(0, NCH // 2) as it:
                    for e in range(E + 1):
                        for j in range(2):
                            if e < E:
                                x = xnT[:, bass.ds(it * 8 + 4 * j, TPC), :]
                                if e == 0:
                                    pe.wait_ge(added[j], it * E * TPC)
                                if e >= 2:
                                    pe.wait_ge(added[j], it * E * TPC + (e - 1) * TPC)
                                pe.matmul(bank(j, e, 0), wg[:, e], x, start=True, stop=True)
                                pe.matmul(bank(j, e, 1), wu[:, e], x, start=True, stop=True).then_inc(up[j], 1)
                        for j in range(2):
                            if e >= 1:
                                f = e - 1
                                pe.wait_ge(hidden[j], it * E + f + 1)
                                for t in range(TPC):
                                    last = pe.matmul(bank(j, f, 0)[:, t * P:t * P + P],
                                                     hid[j][:, f % 2, t * P:t * P + P], wd[:, f],
                                                     start=True, stop=True)
                                last.then_inc(down[j], 1)

            @block.scalar
            def _(act):
                with act.Fori(0, NCH // 2) as it:
                    for e in range(E):
                        for j in range(2):
                            act.wait_ge(up[j], it * E + e + 1)
                            act.activation(gate[j][:, e % 2], bank(j, e, 0), ACT.Silu).then_inc(silued[j], 1)

            @block.vector
            def _(dve):
                with dve.Fori(0, NCH // 2) as it:
                    for e in range(E + 1):
                        for j in range(2):
                            if e < E:
                                dve.wait_ge(silued[j], it * E + e + 1)
                                dve.tensor_tensor(hid[j][:, e % 2], bank(j, e, 1), gate[j][:, e % 2], ALU.mult)\
                                   .then_inc(hidden[j], 1)
                        for j in range(2):
                            if e >= 1:
                                f = e - 1
                                dve.wait_ge(down[j], it * E + f + 1)
                                if f:
                                    dve.wait_ge(added[j], it * E * TPC + f * TPC)
                                for t in range(TPC):
                                    tile = it * 8 + 4 * j + t
                                    dve.scalar_tensor_tensor(
                                        m.X[:, tile, :], bank(j, f, 0)[:, t * P:t * P + P],
                                        mix[:, tile, f:f + 1], m.X[:, tile, :],
                                        ALU.mult, ALU.add).then_inc(added[j], 1)
                    for j in range(2):
                        dve.wait_ge(added[j], it * E * TPC + E * TPC)
                        for t in range(TPC):
                            tile = it * 8 + 4 * j + t
                            dve.bn_stats(m.S6[:, tile, :], m.X[:, tile, :])


def attention16(nc, m, d, name, projected, gate_at):
    H, W = 16, 8
    G = H // 2
    half = CH
    with Stage(nc, name) as st:
        wo, bo = st.sb("wo", [P, P]), st.sb("bo", [1, P])
        loads = [(wo, f"{name}_wo"), (bo, f"{name}_bo")]
        if projected:
            wq, wk, wv = st.sb("wq", [P, P]), st.sb("wk", [P, P]), st.sb("wv", [P, P])
            bq, bk, bv = st.sb("bq", [P, 1]), st.sb("bk", [P, 1]), st.sb("bv", [P, P])
            rows = st.sb("rows", [P, NT], I32)
            scale = st.sb("scale", [P, NT])
            loads += [(wq, f"{name}_wq"), (wk, f"{name}_wk"), (wv, f"{name}_wv"), (bq, f"{name}_bq"),
                      (bk, f"{name}_bk"), (bv, f"{name}_bv"), (rows, f"{name}_mask")]
            kT = st.two("kT", [P, P])
        else:
            raw = st.sb("raw", [P, NT, S], I32)
            masks = st.sb("masks", [P, NT, S], BF16)
            loads += [(raw, f"{name}_mask")]
            ctx2 = st.two("ctx2", [P, 2, P])
        xn, xnT, ctxT = st.two("xn", [P, P]), st.two("xnT", [P, P]), st.two("ctxT", [P, P])
        qT = st.two("qT", [P, P]) if projected else xnT
        kx = st.two("kx", [P, 2, H, S])
        vd = st.two("vd", [P, 2, G, 2, W + 1])
        prob, pT = st.two("prob", [P, H, S]), st.two("pT", [P, G, P])
        top, inv = st.two("top", [P, H]), st.two("inv", [P, H])
        o, oT = st.two("o", [P, P]), st.two("oT", [P, P])
        loaded, masked, ones_set = st.sem("loaded"), st.sem("masked"), st.sem("ones_set")
        (ctx_in, ctx2_in, normed_x, turned, copied, proj, q_set, k_set, values, keys, scored, max_done, shifted,
         exped, p_turned, p_copied, mixed, inverted, o_done, o_turned, o_copied, out_done, added, stats) = (
            st.sem2(n) for n in ("ctx_in", "ctx2_in", "normed_x", "turned", "copied", "proj", "q_set", "k_set",
                                 "values", "keys", "scored", "max_done", "shifted", "exped", "p_turned",
                                 "p_copied", "mixed", "inverted", "o_done", "o_turned", "o_copied", "out_done",
                                 "added", "stats"))
        n_loaded = 16 * len(loads)
        with nc.Block() as block:
            @block.sync
            def _(sp):
                for tile, src in loads:
                    sp.dma_start(tile[:], d[src]).then_inc(loaded, 16)
                with sp.Fori(0, PAIRS) as it:
                    for j in range(2):
                        sp.wait_ge(proj[j] if projected else keys[j], it)
                        sp.dma_start(ctxT[j][:], d["ctxT"][it * 2 + j]).then_inc(ctx_in[j], 16)
                        if not projected:
                            sp.wait_ge(values[j], it)
                            for u in range(2):
                                sp.dma_start(ctx2[j][u * S:u * S + S], d["ctx"][:, bass.ds(it * 4 + 2 * j, 2), :])\
                                  .then_inc(ctx2_in[j], 16)

            @block.gpsimd
            def _(pool):
                for j in range(2):
                    for b in range(2):
                        pool.tensor_copy(vd[j][:, b, :, :, W], repeat_heads(m.half[:], G)).then_inc(ones_set, 1)
                with pool.Fori(0, PAIRS) as it:
                    for j in range(2):
                        if projected:
                            pool.wait_ge(k_set[j], it + 1)
                        else:
                            pool.wait_ge(ctx_in[j], it * 16 + 16)
                        pool.wait_ge(scored[j], it)
                        keyT = kT[j] if projected else ctxT[j]
                        for b in range(2):
                            last = pool.tensor_tensor(kx[j][:, b], repeat_heads(keyT[:, b * S:b * S + S], H),
                                                      spread_heads(m.head16[:], S), ALU.mult)
                        last.then_inc(keys[j], 1)
                        if not projected:
                            pool.wait_ge(ctx2_in[j], it * 32 + 32)
                            pool.wait_ge(mixed[j], it)
                            for b in range(2):
                                last = pool.tensor_tensor(
                                    vd[j][:, b, :, :, 0:W], ctx2[j][:, b].rearrange("p (g u w) -> p g u w", g=G, u=2),
                                    m.half[:, None, :, None].broadcast_to([P, G, 2, W]), ALU.mult)
                            last.then_inc(values[j], 1)

            @block.vector
            def _(dve):
                if projected:
                    for j in range(2):
                        dve.memset(vd[j][:, :, :, :, 0:W], 0.0).then_inc(masked, 1)
                dve.wait_ge(loaded, n_loaded)
                if projected:
                    dve.tensor_scalar(scale[:], rows[:], 0, float(W) ** -0.5, ALU.not_equal, ALU.mult)\
                       .then_inc(masked, 1)
                else:
                    dve.tensor_scalar(masks[:], raw[:], 0, -1e20, ALU.is_equal, ALU.mult).then_inc(masked, 1)
                dve.wait_ge(masked, 3 if projected else 1)
                with dve.Fori(0, PAIRS) as it:
                    for j in range(2):
                        dve.wait_ge(turned[j], it)
                        normed(dve, m, xn[j][:], it * 2 + j).then_inc(normed_x[j], 1)
                    if projected:
                        for j in range(2):
                            dve.wait_ge(proj[j], it + 1)
                            dve.wait_ge(mixed[j], it)
                            v = m.B[j][:, CH:CH + 2 * P].rearrange("p (b g u w) -> p b g u w", b=2, g=G, u=2)
                            b_v = bv[:].rearrange("p (g u w) -> p g u w", g=G, u=2)
                            for u in range(2):
                                r = slice(u * S, u * S + S)
                                for b in range(2):
                                    last = dve.tensor_tensor(vd[j][r, b, :, u, 0:W], v[r, b, :, u], b_v[r, :, u], ALU.add)
                            last.then_inc(values[j], 1)
                    for j in range(2):
                        s = per_head(m.A[j][:], H, S)
                        dve.wait_ge(scored[j], it + 1)
                        dve.tensor_reduce(top[j][:], s, AX, ALU.max).then_inc(max_done[j], 1)
                        dve.wait_ge(max_done[j], it + 1)
                        dve.wait_ge(p_turned[j], it)
                        dve.tensor_tensor(prob[j][:], s, spread_heads(top[j][:], S), ALU.subtract)\
                           .then_inc(shifted[j], 1)
                    for j in range(2):
                        out = m.A[j][:, 0:H * (W + 1)].rearrange("p (h w) -> p h w", h=H)
                        dve.wait_ge(mixed[j], it + 1)
                        dve.reciprocal(inv[j][:], out[:, :, W]).then_inc(inverted[j], 1)
                        dve.wait_ge(inverted[j], it + 1)
                        dve.wait_ge(o_turned[j], it)
                        dve.tensor_tensor(per_head(o[j][:], H, W), out[:, :, 0:W], spread_heads(inv[j][:], W),
                                          ALU.mult).then_inc(o_done[j], 1)
                    for j in range(2):
                        t = it * 2 + j
                        dve.wait_ge(out_done[j], it + 1)
                        dve.scalar_tensor_tensor(m.X[:, t, :], m.B[j][:, P:2 * P],
                                                 m.tanh_g[:, gate_at:gate_at + 1], m.X[:, t, :],
                                                 ALU.mult, ALU.add).then_inc(added[j], 1)
                        dve.wait_ge(added[j], it + 1)
                        dve.bn_stats(m.S6[:, t, :], m.X[:, t, :])

            @block.scalar
            def _(act):
                act.wait_ge(loaded, n_loaded)
                act.wait_ge(masked, 3 if projected else 1)
                with act.Fori(0, PAIRS) as it:
                    for j in range(2):
                        act.wait_ge(turned[j], it + 1)
                        act.wait_ge(proj[j] if projected else scored[j], it)
                        act.copy(xnT[j][:], m.A[j][:, 0:P]).then_inc(copied[j], 1)
                    if projected:
                        for j in range(2):
                            act.wait_ge(proj[j], it + 1)
                            act.wait_ge(keys[j], it)
                            act.activation(kT[j][:], m.B[j][:, 0:P], ACT.Identity, bias=bk[:]).then_inc(k_set[j], 1)
                            act.wait_ge(scored[j], it)
                            act.activation(qT[j][:], m.A[j][:, P:2 * P], ACT.Identity, bias=bq[:]).then_inc(q_set[j], 1)
                    for j in range(2):
                        t = it * 2 + j
                        act.wait_ge(shifted[j], it + 1)
                        act.activation(prob[j][:], prob[j][:], ACT.Exp,
                                       scale=scale[:, bass.ds(t, 1)] if projected else float(P) ** -0.5)\
                           .then_inc(exped[j], 1)
                    for j in range(2):
                        act.wait_ge(p_turned[j], it + 1)
                        act.wait_ge(mixed[j], it)
                        act.copy(pT[j][:], m.B[j][:].rearrange("p (g q) -> p g q", g=G)).then_inc(p_copied[j], 1)
                    for j in range(2):
                        act.wait_ge(o_turned[j], it + 1)
                        act.wait_ge(out_done[j], it)
                        act.copy(oT[j][:], m.B[j][:, 0:P]).then_inc(o_copied[j], 1)

            @block.tensor
            def _(pe):
                pe.wait_ge(loaded, n_loaded)
                pe.wait_ge(masked, 3 if projected else 1)
                pe.wait_ge(ones_set, 4)
                with pe.Fori(0, PAIRS) as it:
                    for j in range(2):
                        pe.wait_ge(normed_x[j], it + 1)
                        pe.wait_ge(o_done[j], it)
                        pe.transpose(m.A[j][:, 0:P], xn[j][:], m.ident[:]).then_inc(turned[j], 1)
                    if projected:
                        for j in range(2):
                            pe.wait_ge(ctx_in[j], it * 16 + 16)
                            pe.wait_ge(added[j], it)
                            pe.matmul(m.B[j][:, 0:P], wk[:], ctxT[j][:], start=True, stop=True)
                            for b in range(2):
                                for u in range(2):
                                    pe.matmul(m.B[j][u * S:u * S + S, CH + b * P:CH + b * P + P],
                                              ctxT[j][:, b * S:b * S + S], wv[:], start=True, stop=True)
                            pe.wait_ge(copied[j], it + 1)
                            pe.matmul(m.A[j][:, P:2 * P], wq[:], xnT[j][:], start=True, stop=True)\
                              .then_inc(proj[j], 1)
                    for j in range(2):
                        pe.wait_ge(q_set[j] if projected else copied[j], it + 1)
                        pe.wait_ge(keys[j], it + 1)
                        for n in range(2):
                            s = m.A[j][:, n * half:n * half + half]
                            if not projected:
                                pe.matmul(s, m.ident_bf[:],
                                          masks[:, it * 2 + j, :][:, None, :].broadcast_to([P, G, S]),
                                          start=True, stop=False)
                            for b in range(2):
                                last = pe.matmul(s[b * S:b * S + S], qT[j][:, b * S:b * S + S],
                                                 kx[j][:, b, n * G:n * G + G], start=projected, stop=True)
                        last.then_inc(scored[j], 1)
                    for j in range(2):
                        pe.wait_ge(exped[j], it + 1)
                        pe.wait_ge(values[j], it + 1)
                        pe.wait_ge(added[j], it)
                        p = prob[j][:].rearrange("p h k -> p (h k)")
                        for g in range(G):
                            last = pe.transpose(m.B[j][:, g * P:g * P + P], p[:, g * P:g * P + P], m.ident[:])
                        last.then_inc(p_turned[j], 1)
                    for j in range(2):
                        pe.wait_ge(p_copied[j], it + 1)
                        for b in range(2):
                            for g in range(G):
                                n = 2 * (W + 1)
                                last = pe.matmul(m.A[j][b * S:b * S + S, g * n:g * n + n], pT[j][:, g, b * S:b * S + S],
                                                 vd[j][:, b, g], start=True, stop=True)
                        last.then_inc(mixed[j], 1)
                    for j in range(2):
                        pe.wait_ge(o_done[j], it + 1)
                        pe.transpose(m.B[j][:, 0:P], o[j][:], m.ident[:]).then_inc(o_turned[j], 1)
                    for j in range(2):
                        pe.wait_ge(o_copied[j], it + 1)
                        y = m.B[j][:, P:2 * P]
                        pe.matmul(y, m.ones_row[:], bo[:], start=True, stop=False)
                        pe.matmul(y, oT[j][:], wo[:], start=False, stop=True).then_inc(out_done[j], 1)


def l1_xattn(nc, m, d, own):
    attention16(nc, m, d, "l1x", True, 1)


def l2_xattn(nc, m, d, own):
    attention16(nc, m, d, "l2x", False, 2)


def l3_xattn(nc, m, d, own):
    with Stage(nc, "l3x") as st:
        wq, wk, bq, bk = st.sb("wq", [P, P]), st.sb("wk", [P, P]), st.sb("bq", [P, 1]), st.sb("bk", [P, 1])
        raw = st.sb("raw", [P, NT, S], I32)
        factor, extra = st.sb("factor", [P, NT, S]), st.sb("extra", [P, NT, S])
        loads = [(wq, "l3x_wq"), (wk, "l3x_wk"), (bq, "l3x_bq"), (bk, "l3x_bk"), (raw, "l3x_mask")]
        xn, xnT, ctxT, qT, kT = (st.two(n, [P, P]) for n in ("xn", "xnT", "ctxT", "qT", "kT"))
        val = st.two("val", [P, 2, P])
        probs, pT = st.two("prob", [P, P]), st.two("pT", [P, P])
        prob = [x[:, 0:S] for x in probs]
        top, total, inv = (st.two(n, [P, 1]) for n in ("top", "total", "inv"))
        loaded, masked, zeroed = st.sem("loaded"), st.sem("masked"), st.sem("zeroed")
        (ctx_in, val_in, normed_x, turned, copied, proj, q_set, scored, times, plus, max_done, shifted, exped,
         p_turned, p_copied, mixed, inverted, added) = (
            st.sem2(n) for n in ("ctx_in", "val_in", "normed_x", "turned", "copied", "proj", "q_set", "scored",
                                 "times", "plus", "max_done", "shifted", "exped", "p_turned", "p_copied", "mixed",
                                 "inverted", "added"))
        with nc.Block() as block:
            @block.sync
            def _(sp):
                for tile, src in loads:
                    sp.dma_start(tile[:], d[src]).then_inc(loaded, 16)
                with sp.Fori(0, PAIRS) as it:
                    for j in range(2):
                        sp.wait_ge(proj[j], it)
                        sp.dma_start(ctxT[j][:], d["ctxT"][it * 2 + j]).then_inc(ctx_in[j], 16)
                        sp.wait_ge(mixed[j], it)
                        sp.dma_start(val[j][0:S], d["ctx"][:, bass.ds(it * 4 + 2 * j, 2), :]).then_inc(val_in[j], 16)

            @block.vector
            def _(dve):
                for j in range(2):
                    dve.memset(val[j][S:P], 0.0).then_inc(zeroed, 1)
                    dve.memset(probs[j][:, S:P], 0.0).then_inc(zeroed, 1)
                dve.wait_ge(loaded, 16 * len(loads))
                dve.tensor_scalar(factor[:], raw[:], float(P) ** -0.5, None, ALU.mult)
                dve.tensor_scalar(extra[:], raw[:], 0, -1e9, ALU.is_equal, ALU.mult).then_inc(masked, 1)
                dve.wait_ge(masked, 1)
                with dve.Fori(0, PAIRS) as it:
                    for j in range(2):
                        dve.wait_ge(turned[j], it)
                        normed(dve, m, xn[j][:], it * 2 + j).then_inc(normed_x[j], 1)
                    for j in range(2):
                        t = it * 2 + j
                        dve.wait_ge(scored[j], it + 1)
                        dve.wait_ge(p_turned[j], it)
                        dve.tensor_tensor(prob[j], m.B[j][:, 0:S], factor[:, t, :], ALU.mult).then_inc(times[j], 1)
                        dve.wait_ge(times[j], it + 1)
                        dve.tensor_tensor(prob[j], prob[j], extra[:, t, :], ALU.add).then_inc(plus[j], 1)
                        dve.wait_ge(plus[j], it + 1)
                        dve.tensor_reduce(top[j][:], prob[j], AX, ALU.max, negate=True).then_inc(max_done[j], 1)
                    for j in range(2):
                        t = it * 2 + j
                        dve.wait_ge(exped[j], it + 1)
                        dve.reciprocal(inv[j][:], total[j][:]).then_inc(inverted[j], 1)
                        dve.wait_ge(inverted[j], it + 1)
                        dve.wait_ge(mixed[j], it + 1)
                        dve.tensor_scalar(xn[j][:], m.B[j][:, 2 * P:3 * P], inv[j][:], m.tanh_g[:, 3:4],
                                          ALU.mult, ALU.mult).then_inc(shifted[j], 1)
                        dve.wait_ge(shifted[j], it + 1)
                        dve.tensor_tensor(m.X[:, t, :], m.X[:, t, :], xn[j][:], ALU.add).then_inc(added[j], 1)
                        dve.wait_ge(added[j], it + 1)
                        dve.bn_stats(m.S6[:, t, :], m.X[:, t, :])

            @block.scalar
            def _(act):
                act.wait_ge(loaded, 16 * len(loads))
                with act.Fori(0, PAIRS) as it:
                    for j in range(2):
                        act.wait_ge(turned[j], it + 1)
                        act.wait_ge(proj[j], it)
                        act.copy(xnT[j][:], m.A[j][:, 0:P]).then_inc(copied[j], 1)
                    for j in range(2):
                        act.wait_ge(proj[j], it + 1)
                        act.wait_ge(scored[j], it)
                        act.activation(kT[j][:], m.A[j][:, P:2 * P], ACT.Identity, bias=bk[:])
                        act.activation(qT[j][:], m.A[j][:, 2 * P:3 * P], ACT.Identity, bias=bq[:]).then_inc(q_set[j], 1)
                    for j in range(2):
                        act.wait_ge(max_done[j], it + 1)
                        act.wait_ge(inverted[j], it)
                        act.activation(prob[j], prob[j], ACT.Exp, bias=top[j][:], accum_out=total[j][:])\
                           .then_inc(exped[j], 1)
                    for j in range(2):
                        act.wait_ge(p_turned[j], it + 1)
                        act.wait_ge(mixed[j], it)
                        act.copy(pT[j][:], m.B[j][:, CH:CH + P]).then_inc(p_copied[j], 1)

            @block.tensor
            def _(pe):
                pe.wait_ge(loaded, 16 * len(loads))
                pe.wait_ge(zeroed, 4)
                with pe.Fori(0, PAIRS) as it:
                    for j in range(2):
                        pe.wait_ge(normed_x[j], it + 1)
                        pe.wait_ge(q_set[j], it)
                        pe.transpose(m.A[j][:, 0:P], xn[j][:], m.ident[:]).then_inc(turned[j], 1)
                    for j in range(2):
                        pe.wait_ge(ctx_in[j], it * 16 + 16)
                        pe.wait_ge(copied[j], it + 1)
                        pe.matmul(m.A[j][:, P:2 * P], wk[:], ctxT[j][:], start=True, stop=True)
                        pe.matmul(m.A[j][:, 2 * P:3 * P], wq[:], xnT[j][:], start=True, stop=True).then_inc(proj[j], 1)
                    for j in range(2):
                        pe.wait_ge(q_set[j], it + 1)
                        pe.wait_ge(shifted[j], it)
                        for b in range(2):
                            last = pe.matmul(m.B[j][b * S:b * S + S, 0:S], qT[j][:, b * S:b * S + S],
                                             kT[j][:, b * S:b * S + S], start=True, stop=True)
                        last.then_inc(scored[j], 1)
                    for j in range(2):
                        pe.wait_ge(exped[j], it + 1)
                        pe.transpose(m.B[j][:, CH:CH + P], probs[j][:], m.ident[:]).then_inc(p_turned[j], 1)
                    for j in range(2):
                        pe.wait_ge(p_copied[j], it + 1)
                        pe.wait_ge(val_in[j], it * 16 + 16)
                        for b in range(2):
                            last = pe.matmul(m.B[j][b * S:b * S + S, 2 * P:3 * P], pT[j][:, b * S:b * S + S],
                                             val[j][:, b], start=True, stop=True)
                        last.then_inc(mixed[j], 1)


def quantizer(nc, m, name, maxima, scale, inverse):
    with Stage(nc, name) as st:
        own, all_ = st.sb("own", [P, 1]), st.sb("all", [P, 1])
        own_max, all_max, step = st.sem("own_max"), st.sem("all_max"), st.sem("step")
        with nc.Block() as block:
            @block.vector
            def _(dve):
                dve.tensor_reduce(own[:], maxima, AX, ALU.max).then_inc(own_max, 1)
                dve.wait_ge(all_max, 1)
                dve.tensor_scalar(scale, all_[:], 1.0 / 32767.0, 1e-12, ALU.mult, ALU.max).then_inc(step, 1)
                dve.wait_ge(step, 1)
                dve.reciprocal(inverse, scale)

            @block.gpsimd
            def _(pool):
                pool.wait_ge(own_max, 1)
                pool.partition_all_reduce(all_[:], own[:], P, bass.bass_isa.ReduceOp.max).then_inc(all_max, 1)


def l1_ffn(nc, m, d, own):
    F = 3
    BLOCK = 32
    NBL = 3 * F * P // BLOCK
    sb = lambda n, s, dt=F32: own.enter_context(nc.sbuf_tensor("l1f_" + n, s, dt))
    wT = sb("wT", [P, 3 * F, P])
    xT = sb("xT", [P, NT, P])
    upq, gateq = sb("upq", [P, F, NT * P], I16), sb("gateq", [P, F, NT * P], I16)
    maxima = sb("maxima", [P, 2, NCH * F])
    sc = sb("sc", [P, 16])
    rnd = sb("rnd", [P, 1])
    col = lambda n: sc[:, n:n + 1]
    X_S, X_R, U_S, U_R, G_S, G_R, H_S, H_R, O_S, O_R, TMP, GH_R, O_F, GATE, O_U = range(15)
    banks = [[r[j][:, h * CH:h * CH + CH] for r in (m.A, m.B) for h in range(2)] for j in range(2)]

    with Stage(nc, "l1f_w") as st:
        w, q = st.sb("w", [P, 3 * F * P]), st.sb("q", [P, 3 * F * P])
        big, inv = st.sb("big", [P, NBL]), st.sb("inv", [P, NBL])
        loaded, step, turned, ready = st.sem("loaded"), st.sem("step"), st.sem("turned"), st.sem("ready")
        with nc.Block() as block:
            @block.sync
            def _(sp):
                sp.dma_start(w[:], d["l1f_w"]).then_inc(loaded, 16)

            @block.vector
            def _(dve):
                blocks = lambda x: x[:].rearrange("p (n k) -> p n k", k=BLOCK)
                count = [0]

                def then(ins):
                    count[0] += 1
                    ins.then_inc(step, 1)
                    dve.wait_ge(step, count[0])

                then(dve.memset(rnd[:], ROUND))
                dve.wait_ge(loaded, 16)
                then(dve.tensor_reduce(big[:], blocks(w), AX, ALU.max, apply_absolute_value=True))
                then(dve.tensor_scalar(big[:], big[:], 1.0 / 7.0, 1e-12, ALU.mult, ALU.max))
                then(dve.reciprocal(inv[:], big[:]))
                then(dve.tensor_tensor(blocks(q), blocks(w), spread_heads(inv[:], BLOCK), ALU.mult))
                then(dve.tensor_scalar(q[:], q[:], 7.0, -8.0, ALU.min, ALU.max))
                then(dve.tensor_scalar(q[:], q[:], ROUND, None, ALU.add))
                then(dve.tensor_scalar(q[:], q[:], -ROUND, None, ALU.add))
                dve.tensor_tensor(blocks(q), blocks(q), spread_heads(big[:], BLOCK), ALU.mult).then_inc(ready, 1)
                dve.wait_ge(turned, 1)
                for n in range(3 * F):
                    dve.tensor_copy(wT[:, n], banks[n % 2][n // 2 % 4][:, n // 8 * P:n // 8 * P + P])

            @block.tensor
            def _(pe):
                pe.wait_ge(ready, 1)
                for n in range(3 * F):
                    last = pe.transpose(banks[n % 2][n // 2 % 4][:, n // 8 * P:n // 8 * P + P],
                                        q[:, n * P:n * P + P], m.ident[:])
                last.then_inc(turned, 1)

    with Stage(nc, "l1f_xmax") as st:
        xn = st.two("xn", [P, P])
        normed_x, found = st.sem2("normed_x"), st.sem2("found")
        xmax = st.sb("xmax", [P, NT])
        with nc.Block() as block:
            @block.vector
            def _(dve):
                with dve.Fori(0, PAIRS) as it:
                    for j in range(2):
                        dve.wait_ge(found[j], it)
                        normed(dve, m, xn[j][:], it * 2 + j).then_inc(normed_x[j], 1)
                    for j in range(2):
                        dve.wait_ge(normed_x[j], it + 1)
                        dve.tensor_reduce(xmax[:, bass.ds(it * 2 + j, 1)], xn[j][:], AX, ALU.max,
                                          apply_absolute_value=True).then_inc(found[j], 1)
        quantizer(nc, m, "l1f_xs", xmax[:], col(X_S), col(X_R))

    with Stage(nc, "l1f_x") as st:
        xn, xr = st.two("xn", [P, P]), st.two("xr", [P, P])
        normed_x, rounded, quantized, turned, copied = (
            st.sem2(n) for n in ("normed_x", "rounded", "quantized", "turned", "copied"))
        with nc.Block() as block:
            @block.vector
            def _(dve):
                with dve.Fori(0, PAIRS) as it:
                    for j in range(2):
                        dve.wait_ge(rounded[j], it)
                        normed(dve, m, xn[j][:], it * 2 + j).then_inc(normed_x[j], 1)
                    for j in range(2):
                        dve.wait_ge(normed_x[j], it + 1)
                        dve.wait_ge(turned[j], it)
                        dve.tensor_scalar(xr[j][:], xn[j][:], col(X_R), ROUND, ALU.mult, ALU.add).then_inc(rounded[j], 1)
                    for j in range(2):
                        dve.wait_ge(rounded[j], it + 1)
                        dve.tensor_scalar(xr[j][:], xr[j][:], -ROUND, col(X_S), ALU.add, ALU.mult)\
                           .then_inc(quantized[j], 1)

            @block.tensor
            def _(pe):
                with pe.Fori(0, PAIRS) as it:
                    for j in range(2):
                        pe.wait_ge(quantized[j], it + 1)
                        pe.wait_ge(copied[j], it)
                        pe.transpose(m.A[j][:, 0:P], xr[j][:], m.ident[:]).then_inc(turned[j], 1)

            @block.scalar
            def _(act):
                with act.Fori(0, PAIRS) as it:
                    for j in range(2):
                        act.wait_ge(turned[j], it + 1)
                        act.copy(xT[:, it * 2 + j, :], m.A[j][:, 0:P]).then_inc(copied[j], 1)

    with Stage(nc, "l1f_ugmax") as st:
        made, seen = st.sem2("made"), st.sem2("seen")
        with nc.Block() as block:
            @block.tensor
            def _(pe):
                with pe.Fori(0, NCH) as it:
                    x = xT[:, bass.ds(it * TPC, TPC), :]
                    for o in range(F):
                        for n in range(2):
                            pe.wait_ge(seen[n], it * F)
                            pe.matmul(banks[n][o], wT[:, n * F + o], x, start=True, stop=True).then_inc(made[n], 1)

            @block.vector
            def _(dve):
                with dve.Fori(0, NCH) as it:
                    for o in range(F):
                        for n in range(2):
                            dve.wait_ge(made[n], it * F + o + 1)
                            dve.tensor_reduce(maxima[:, n, bass.ds(it * F + o, 1)], banks[n][o], AX, ALU.max,
                                              apply_absolute_value=True).then_inc(seen[n], 1)
    quantizer(nc, m, "l1f_us", maxima[:, 0], col(U_S), col(U_R))
    quantizer(nc, m, "l1f_gs", maxima[:, 1], col(G_S), col(G_R))

    def tokens(t, o, it):
        return t[:, o, bass.ds(it * CH, CH)]

    with Stage(nc, "l1f_ug") as st:
        ur, gr, sig, h = (st.sb(n, [P, F, CH]) for n in ("ur", "gr", "sig", "h"))
        made, up_rounded, gate_rounded, up_kept, gate_kept, siged, clipped, rounded, times, seen = (
            st.sem(n) for n in ("made", "up_rounded", "gate_rounded", "up_kept", "gate_kept", "siged", "clipped",
                                "rounded", "times", "seen"))
        with nc.Block() as block:
            @block.tensor
            def _(pe):
                with pe.Fori(0, NCH) as it:
                    x = xT[:, bass.ds(it * TPC, TPC), :]
                    for o in range(F):
                        pe.wait_ge(gate_rounded, it * F)
                        pe.matmul(banks[0][o], wT[:, o], x, start=True, stop=True)
                        pe.matmul(banks[1][o], wT[:, F + o], x, start=True, stop=True).then_inc(made, 1)

            @block.scalar
            def _(act):
                with act.Fori(0, NCH) as it:
                    for o in range(F):
                        n = it * F + o + 1
                        act.wait_ge(made, n)
                        act.wait_ge(up_kept, it * F)
                        act.activation(ur[:, o], banks[0][o], ACT.Identity, scale=col(U_R), bias=rnd[:])\
                           .then_inc(up_rounded, 1)
                        act.wait_ge(gate_kept, it * F)
                        act.activation(gr[:, o], banks[1][o], ACT.Identity, scale=col(G_R), bias=rnd[:])\
                           .then_inc(gate_rounded, 1)
                    for o in range(F):
                        act.wait_ge(gate_kept, it * F + o + 1)
                        act.wait_ge(times, it * F)
                        act.activation(sig[:, o], tokens(gateq, o, it), ACT.Sigmoid, scale=col(G_S)).then_inc(siged, 1)

            @block.vector
            def _(dve):
                with dve.Fori(0, NCH) as it:
                    for o in range(F):
                        n = it * F + o + 1
                        dve.wait_ge(gate_rounded, n)
                        dve.tensor_scalar(tokens(gateq, o, it), gr[:, o], -ROUND, 32767.0, ALU.add, ALU.min)\
                           .then_inc(gate_kept, 1)
                        dve.wait_ge(up_rounded, n)
                        dve.tensor_scalar(tokens(upq, o, it), ur[:, o], -ROUND, 32767.0, ALU.add, ALU.min)\
                           .then_inc(up_kept, 1)
                    for o in range(F):
                        dve.wait_ge(siged, it * F + o + 1)
                        dve.tensor_scalar(sig[:, o], sig[:, o], 65536.0, 65535.0, ALU.mult, ALU.min).then_inc(clipped, 1)
                    for o in range(F):
                        dve.wait_ge(clipped, it * F + o + 1)
                        dve.tensor_scalar(sig[:, o], sig[:, o], 0.0, ROUND, ALU.max, ALU.add).then_inc(rounded, 1)
                    for o in range(F):
                        n = it * F + o + 1
                        dve.wait_ge(rounded, n)
                        dve.scalar_tensor_tensor(h[:, o], sig[:, o], -ROUND, tokens(gateq, o, it), ALU.add, ALU.mult)\
                           .then_inc(times, 1)
                    for o in range(F):
                        dve.wait_ge(times, it * F + o + 1)
                        dve.tensor_reduce(maxima[:, 0, bass.ds(it * F + o, 1)], h[:, o], AX, ALU.max,
                                          apply_absolute_value=True).then_inc(seen, 1)

    def small(name, *ops):
        with Stage(nc, name) as st:
            step = st.sem("step")
            with nc.Block() as block:
                @block.vector
                def _(dve):
                    for n, op in enumerate(ops):
                        op(dve).then_inc(step, 1)
                        dve.wait_ge(step, n + 1)

    small("l1f_hunit",
          lambda dve: dve.tensor_scalar(col(TMP), col(G_S), 1.0 / 65536.0, None, ALU.mult),
          lambda dve: dve.tensor_scalar(maxima[:, 0], maxima[:, 0], col(TMP), None, ALU.mult))
    quantizer(nc, m, "l1f_hs", maxima[:, 0], col(H_S), col(H_R))
    small("l1f_hfactor",
          lambda dve: dve.tensor_scalar(col(GH_R), col(TMP), col(H_R), None, ALU.mult),
          lambda dve: dve.tensor_scalar(col(O_U), col(H_S), col(U_S), None, ALU.mult))

    with Stage(nc, "l1f_h") as st:
        sig, h, hr = (st.sb(n, [P, F, CH]) for n in ("sig", "h", "hr"))
        siged, clipped, rounded, times, h_rounded, kept, product, seen = (
            st.sem(n) for n in ("siged", "clipped", "rounded", "times", "h_rounded", "kept", "product", "seen"))
        with nc.Block() as block:
            @block.scalar
            def _(act):
                with act.Fori(0, NCH) as it:
                    for o in range(F):
                        act.wait_ge(times, it * F)
                        act.activation(sig[:, o], tokens(gateq, o, it), ACT.Sigmoid, scale=col(G_S)).then_inc(siged, 1)
                    for o in range(F):
                        act.wait_ge(times, it * F + o + 1)
                        act.wait_ge(product, it * F)
                        act.activation(hr[:, o], h[:, o], ACT.Identity, scale=col(GH_R), bias=rnd[:])\
                           .then_inc(h_rounded, 1)

            @block.vector
            def _(dve):
                with dve.Fori(0, NCH) as it:
                    for o in range(F):
                        dve.wait_ge(siged, it * F + o + 1)
                        dve.tensor_scalar(sig[:, o], sig[:, o], 65536.0, 65535.0, ALU.mult, ALU.min).then_inc(clipped, 1)
                    for o in range(F):
                        dve.wait_ge(clipped, it * F + o + 1)
                        dve.tensor_scalar(sig[:, o], sig[:, o], 0.0, ROUND, ALU.max, ALU.add).then_inc(rounded, 1)
                    for o in range(F):
                        dve.wait_ge(rounded, it * F + o + 1)
                        dve.wait_ge(seen, it * F)
                        dve.scalar_tensor_tensor(h[:, o], sig[:, o], -ROUND, tokens(gateq, o, it), ALU.add, ALU.mult)\
                           .then_inc(times, 1)
                    for o in range(F):
                        n = it * F + o + 1
                        dve.wait_ge(h_rounded, n)
                        dve.tensor_scalar(tokens(gateq, o, it), hr[:, o], -ROUND, 32767.0, ALU.add, ALU.min)\
                           .then_inc(kept, 1)
                        dve.scalar_tensor_tensor(h[:, o], hr[:, o], -ROUND, tokens(upq, o, it), ALU.add, ALU.mult)\
                           .then_inc(product, 1)
                    for o in range(F):
                        dve.wait_ge(product, it * F + o + 1)
                        dve.tensor_reduce(maxima[:, 0, bass.ds(it * F + o, 1)], h[:, o], AX, ALU.max,
                                          apply_absolute_value=True).then_inc(seen, 1)

    small("l1f_ounit", lambda dve: dve.tensor_scalar(maxima[:, 0], maxima[:, 0], col(O_U), None, ALU.mult))
    quantizer(nc, m, "l1f_os", maxima[:, 0], col(O_S), col(O_R))
    small("l1f_ofactor", lambda dve: dve.tensor_scalar(col(O_F), col(O_U), col(O_R), None, ALU.mult))

    with Stage(nc, "l1f_down") as st:
        prod, oq, y = st.two("prod", [P, F, CH]), st.two("oq", [P, F, CH]), st.two("y", [P, CH])
        multiplied, rounded, quantized, down, scaled, added, used = (
            st.sem2(n) for n in ("multiplied", "rounded", "quantized", "down", "scaled", "added", "used"))
        with nc.Block() as block:
            @block.vector
            def _(dve):
                with dve.Fori(0, NCH // 2) as it:
                    for j in range(2):
                        c = it * 2 + j
                        dve.wait_ge(rounded[j], it * F)
                        for o in range(F):
                            dve.tensor_tensor(prod[j][:, o], tokens(gateq, o, c), tokens(upq, o, c), ALU.mult)\
                               .then_inc(multiplied[j], 1)
                    for j in range(2):
                        for o in range(F):
                            dve.wait_ge(rounded[j], it * F + o + 1)
                            dve.tensor_scalar(oq[j][:, o], oq[j][:, o], -ROUND, col(O_S), ALU.add, ALU.mult)\
                               .then_inc(quantized[j], 1)
                    for j in range(2):
                        dve.wait_ge(down[j], it + 1)
                        dve.tensor_scalar(y[j][:], banks[j][0], m.tanh_g[:, 5:6], None, ALU.mult).then_inc(scaled[j], 1)
                        dve.wait_ge(scaled[j], it + 1)
                        add_tiles(dve, m, added[j], it + 1, it, it * 8 + 4 * j,
                                  y[j][:].rearrange("p (t w) -> p t w", t=TPC))

            @block.scalar
            def _(act):
                with act.Fori(0, NCH // 2) as it:
                    for j in range(2):
                        act.wait_ge(down[j], it)
                        for o in range(F):
                            act.wait_ge(multiplied[j], it * F + o + 1)
                            act.activation(oq[j][:, o], prod[j][:, o], ACT.Identity, scale=col(O_F), bias=rnd[:])\
                               .then_inc(rounded[j], 1)

            @block.tensor
            def _(pe):
                with pe.Fori(0, NCH // 2) as it:
                    for j in range(2):
                        pe.wait_ge(quantized[j], it * F + F)
                        pe.wait_ge(scaled[j], it)
                        for t in range(TPC):
                            for o in range(F):
                                last = pe.matmul(banks[j][0][:, t * P:t * P + P], oq[j][:, o, t * P:t * P + P],
                                                 wT[:, 2 * F + o], start=(o == 0), stop=(o == F - 1))
                        last.then_inc(down[j], 1)


HEADS3, W3 = 8, 64
INNER = HEADS3 * W3
HID3 = int(P * 4 * 2 / 3)
PARTS3 = [(n, min(P, HID3 - n)) for n in range(0, HID3, P)]


def local_attention(nc, m, d, y, layer):
    G = HEADS3 // 2
    with Stage(nc, f"la{layer}") as st:
        wq, wk, wv = (st.sb(n, [P, INNER]) for n in ("wq", "wk", "wv"))
        wo = st.sb("wo", [P, G, P])
        cos, sin = st.sb("cos", [P, 2, W3]), st.sb("sin", [P, 2, W3])
        by, by_swapped = st.sb("by", [P, 2, W3]), st.sb("by_swapped", [P, 2, W3])
        half_power = st.sb("half_power", [P, 2 * HEADS3])
        loads = [(wq, d["l3f_wq"][layer]), (wk, d["l3f_wk"][layer]), (wv, d["l3f_wv"][layer]),
                 (wo, d["l3f_wo"][layer]), (cos, d["c_cos"]), (sin, d["c_sin"]), (by, d["l3f_scale"][layer]),
                 (by_swapped, d["l3f_scale_swapped"][layer])]
        ys, hT, hT2 = st.two("ys", [P, P]), st.two("hT", [P, P]), st.two("hT2", [P, 2, 2, S])
        sq, qk = st.two("sq", [P, 2, INNER]), st.two("qk", [P, 2, INNER])
        length, rlen = st.two("length", [P, 2 * HEADS3]), st.two("rlen", [P, 2 * HEADS3])
        qT = st.two("qT", [P, G, P])
        kd = st.two("kd", [P, G, 2, 2, S])
        vd = st.two("vd", [P, 2, G, 2, W3 + 1])
        prob = st.two("prob", [P, HEADS3, S])
        top, inv = st.two("top", [P, HEADS3]), st.two("inv", [P, HEADS3])
        pT = [x[:, 0].rearrange("p (g q) -> p g q", g=G) for x in sq]
        oT = [x[:, 1].rearrange("p (g q) -> p g q", g=G) for x in sq]
        o = [x[:, 0] for x in qk]
        loaded, ready, ones_set = st.sem("loaded"), st.sem("ready"), st.sem("ones_set")
        (y_copied, y_turned, h_copied, qkv, squared, summed, floored, rooted, scaled, v_kept, cosed, sined, rotated,
         qk_turned, q_copied, k_kept, scored, max_done, shifted, exped, p_turned, p_copied, mixed, inverted,
         o_done, o_turned, o_copied, out_done, added) = (
            st.sem2(n) for n in ("y_copied", "y_turned", "h_copied", "qkv", "squared", "summed", "floored",
                                 "rooted", "scaled", "v_kept", "cosed", "sined", "rotated", "qk_turned",
                                 "q_copied", "k_kept", "scored", "max_done", "shifted", "exped", "p_turned",
                                 "p_copied", "mixed", "inverted", "o_done", "o_turned", "o_copied", "out_done",
                                 "added"))
        A0, A1 = [x[:, 0:CH] for x in m.A], [x[:, CH:2 * CH] for x in m.A]
        B0, B1 = [x[:, 0:CH] for x in m.B], [x[:, CH:2 * CH] for x in m.B]
        with nc.Block() as block:
            @block.sync
            def _(sp):
                for tile, src in loads:
                    sp.dma_start(tile[:], src).then_inc(loaded, 16)

            @block.scalar
            def _(act):
                with act.Fori(0, PAIRS) as it:
                    for j in range(2):
                        act.wait_ge(y_turned[j], it)
                        act.wait_ge(added[j], it)
                        act.copy(ys[j][:], y[:, it * 2 + j, :]).then_inc(y_copied[j], 1)
                    for j in range(2):
                        act.wait_ge(y_turned[j], it + 1)
                        act.wait_ge(qkv[j], it)
                        act.copy(hT[j][:], A1[j][:, 0:P])
                        for b in range(2):
                            last = act.copy(hT2[j][:, b], repeat_heads(A1[j][:, b * S:b * S + S], 2))
                        last.then_inc(h_copied[j], 1)
                    for j in range(2):
                        act.wait_ge(qkv[j], it + 1)
                        act.wait_ge(out_done[j], it)
                        act.activation(sq[j][:, 0], A0[j], ACT.Square)
                        act.activation(sq[j][:, 1], B0[j], ACT.Square).then_inc(squared[j], 1)
                    for j in range(2):
                        act.wait_ge(qk_turned[j], it + 1)
                        act.wait_ge(scored[j], it)
                        act.copy(qT[j][:], A0[j].rearrange("p (g q) -> p g q", g=G)).then_inc(q_copied[j], 1)
                    for j in range(2):
                        act.wait_ge(shifted[j], it + 1)
                        act.activation(prob[j][:], prob[j][:], ACT.Exp, scale=8.0).then_inc(exped[j], 1)
                    for j in range(2):
                        act.wait_ge(p_turned[j], it + 1)
                        act.copy(pT[j], B1[j].rearrange("p (g q) -> p g q", g=G)).then_inc(p_copied[j], 1)
                    for j in range(2):
                        act.wait_ge(o_turned[j], it + 1)
                        act.copy(oT[j], A1[j].rearrange("p (g q) -> p g q", g=G)).then_inc(o_copied[j], 1)

            @block.vector
            def _(dve):
                for j in range(2):
                    dve.memset(kd[j][:], 0.0).then_inc(ones_set, 1)
                    dve.memset(vd[j][:, :, :, :, 0:W3], 0.0).then_inc(ones_set, 1)
                dve.wait_ge(loaded, 16 * len(loads))
                dve.tensor_tensor(cos[:], cos[:], by[:], ALU.mult).then_inc(ready, 1)
                dve.tensor_tensor(sin[:], sin[:], by_swapped[:], ALU.mult).then_inc(ready, 1)
                dve.wait_ge(ones_set, 4 + 4)
                with dve.Fori(0, PAIRS) as it:
                    for j in range(2):
                        dve.wait_ge(squared[j], it + 1)
                        dve.wait_ge(rooted[j], it)
                        dve.tensor_reduce(length[j][:], sq[j][:].rearrange("p n (h w) -> p (n h) w", h=HEADS3), AX,
                                          ALU.add).then_inc(summed[j], 1)
                        dve.wait_ge(summed[j], it + 1)
                        dve.tensor_scalar(length[j][:], length[j][:], 1e-24, None, ALU.max).then_inc(floored[j], 1)
                        dve.wait_ge(mixed[j], it)
                        for u in range(2):
                            r = slice(u * S, u * S + S)
                            for b, src in enumerate((A1[j], B1[j])):
                                v = src.rearrange("p (g u w) -> p g u w", g=G, u=2)
                                last = dve.tensor_copy(vd[j][r, b, :, u, 0:W3], v[r, :, u])
                        last.then_inc(v_kept[j], 1)
                    for j in range(2):
                        dve.wait_ge(rooted[j], it + 1)
                        dve.wait_ge(o_turned[j], it)
                        for n, src in enumerate((A0[j], B0[j])):
                            last = dve.tensor_tensor(per_head(qk[j][:, n], HEADS3, W3), per_head(src, HEADS3, W3),
                                                     spread_heads(rlen[j][:, n * HEADS3:(n + 1) * HEADS3], W3), ALU.mult)
                        last.then_inc(scaled[j], 1)
                    for j in range(2):
                        dve.wait_ge(qk_turned[j], it + 1)
                        dve.wait_ge(scored[j], it)
                        for u in range(2):
                            r = slice(u * S, u * S + S)
                            last = dve.tensor_copy(kd[j][r, :, :, u], B0[j].rearrange("p (g b k) -> p g b k", g=G, b=2)[r])
                        last.then_inc(k_kept[j], 1)
                    for j in range(2):
                        s = per_head(A1[j], HEADS3, S)
                        dve.wait_ge(scored[j], it + 1)
                        dve.tensor_reduce(top[j][:], s, AX, ALU.max).then_inc(max_done[j], 1)
                        dve.wait_ge(max_done[j], it + 1)
                        dve.wait_ge(p_turned[j], it)
                        dve.tensor_tensor(prob[j][:], s, spread_heads(top[j][:], S), ALU.subtract)\
                           .then_inc(shifted[j], 1)
                    for j in range(2):
                        dve.wait_ge(mixed[j], it + 1)
                        outs = [x[:, 0:4 * (W3 + 1)].rearrange("p (h w) -> p h w", h=4) for x in (A0[j], B0[j])]
                        for n in range(2):
                            dve.reciprocal(inv[j][:, 4 * n:4 * n + 4], outs[n][:, :, W3]).then_inc(inverted[j], 1)
                        dve.wait_ge(inverted[j], it * 2 + 2)
                        for n in range(2):
                            last = dve.tensor_tensor(per_head(o[j], HEADS3, W3)[:, 4 * n:4 * n + 4], outs[n][:, :, 0:W3],
                                                     spread_heads(inv[j][:, 4 * n:4 * n + 4], W3), ALU.mult)
                        last.then_inc(o_done[j], 1)
                    for j in range(2):
                        t = it * 2 + j
                        dve.wait_ge(out_done[j], it + 1)
                        dve.tensor_tensor(y[:, t, :], y[:, t, :], B1[j][:, 0:P], ALU.add).then_inc(added[j], 1)

            @block.gpsimd
            def _(pool):
                for j in range(2):
                    for b in range(2):
                        pool.tensor_copy(vd[j][:, b, :, :, W3], repeat_heads(m.half[:], G)).then_inc(ones_set, 1)
                pool.memset(half_power[:], -0.5).then_inc(ready, 1)
                pool.wait_ge(ready, 3)
                with pool.Fori(0, PAIRS) as it:
                    for j in range(2):
                        pool.wait_ge(floored[j], it + 1)
                        pool.wait_ge(scaled[j], it)
                        pool.tensor_tensor(rlen[j][:], length[j][:], half_power[:], ALU.pow).then_inc(rooted[j], 1)
                    for j in range(2):
                        x = qk[j][:].rearrange("p n (h w) -> p n h w", h=HEADS3)
                        z = sq[j][:].rearrange("p n (h w) -> p n h w", h=HEADS3)
                        along = lambda table, w: table[:, :, None, w].broadcast_to([P, 2, HEADS3, w.stop - w.start])
                        lo, hi, full = slice(0, W3 // 2), slice(W3 // 2, W3), slice(0, W3)
                        pool.wait_ge(scaled[j], it + 1)
                        pool.tensor_tensor(z[:, :, :, lo], x[:, :, :, hi], along(sin, lo), ALU.mult)
                        pool.tensor_tensor(z[:, :, :, hi], x[:, :, :, lo], along(sin, hi), ALU.mult).then_inc(sined[j], 1)
                        pool.wait_ge(sined[j], it + 1)
                        pool.tensor_tensor(x, x, along(cos, full), ALU.mult).then_inc(cosed[j], 1)
                        pool.wait_ge(cosed[j], it + 1)
                        pool.tensor_tensor(qk[j][:], qk[j][:], sq[j][:], ALU.add).then_inc(rotated[j], 1)

            @block.tensor
            def _(pe):
                pe.wait_ge(loaded, 16 * len(loads))
                pe.wait_ge(ones_set, 8)
                with pe.Fori(0, PAIRS) as it:
                    for j in range(2):
                        pe.wait_ge(y_copied[j], it + 1)
                        pe.wait_ge(o_copied[j], it)
                        pe.matmul(A1[j][0:S, 0:P], ys[j][:, 0:P // 2], m.ident[:], start=True, stop=True)
                        pe.matmul(A1[j][S:P, 0:P], ys[j][:, P // 2:P], m.shift[:], start=True, stop=True)\
                          .then_inc(y_turned[j], 1)
                    for j in range(2):
                        pe.wait_ge(h_copied[j], it + 1)
                        pe.wait_ge(added[j], it)
                        pe.matmul(A0[j], hT[j][:], wq[:], start=True, stop=True)
                        pe.matmul(B0[j], hT[j][:], wk[:], start=True, stop=True)
                        for b, dst in enumerate((A1[j], B1[j])):
                            last = pe.matmul(dst, hT2[j][:, b].rearrange("p u k -> p (u k)"), wv[:],
                                             start=True, stop=True)
                        last.then_inc(qkv[j], 1)
                    for j in range(2):
                        pe.wait_ge(rotated[j], it + 1)
                        for n, dst in enumerate((A0[j], B0[j])):
                            for g in range(G):
                                last = pe.transpose(dst[:, g * P:g * P + P], qk[j][:, n, g * P:g * P + P], m.ident[:])
                        last.then_inc(qk_turned[j], 1)
                    for j in range(2):
                        pe.wait_ge(v_kept[j], it + 1)
                        pe.matmul(A1[j], m.ident_bf[:], repeat_heads(m.causal_bf[:], HEADS3), start=True, stop=False)
                        pe.wait_ge(q_copied[j], it + 1)
                        pe.wait_ge(k_kept[j], it + 1)
                        for b in range(2):
                            for g in range(G):
                                last = pe.matmul(A1[j][b * S:b * S + S, g * P:g * P + P], qT[j][:, g, b * S:b * S + S],
                                                 kd[j][:, g, b].rearrange("p u k -> p (u k)"), start=False,
                                                 stop=(g == G - 1))
                        last.then_inc(scored[j], 1)
                    for j in range(2):
                        pe.wait_ge(exped[j], it + 1)
                        p = prob[j][:].rearrange("p h k -> p (h k)")
                        for g in range(G):
                            last = pe.transpose(B1[j][:, g * P:g * P + P], p[:, g * P:g * P + P], m.ident[:])
                        last.then_inc(p_turned[j], 1)
                    for j in range(2):
                        pe.wait_ge(p_copied[j], it + 1)
                        n = 2 * (W3 + 1)
                        for b in range(2):
                            for g in range(G):
                                dst = (A0, B0)[g // 2][j]
                                last = pe.matmul(dst[b * S:b * S + S, g % 2 * n:g % 2 * n + n],
                                                 pT[j][:, g, b * S:b * S + S],
                                                 vd[j][:, b, g].rearrange("p u w -> p (u w)"), start=True, stop=True)
                        last.then_inc(mixed[j], 1)
                    for j in range(2):
                        pe.wait_ge(o_done[j], it + 1)
                        for g in range(G):
                            last = pe.transpose(A1[j][:, g * P:g * P + P], o[j][:, g * P:g * P + P], m.ident[:])
                        last.then_inc(o_turned[j], 1)
                    for j in range(2):
                        pe.wait_ge(o_copied[j], it + 1)
                        for g in range(G):
                            last = pe.matmul(B1[j][:, 0:P], oT[j][:, g], wo[:, g], start=(g == 0), stop=(g == G - 1))
                        last.then_inc(out_done[j], 1)


def gated_gelu(nc, m, d, y, layer):
    with Stage(nc, f"gg{layer}") as st:
        F = len(PARTS3)
        w1, w2 = st.sb("w1", [P, 2 * HID3]), st.sb("w2", [P, F, P])
        b1, b2 = st.sb("b1", [P, 2, F]), st.sb("b2", [1, P])
        lg, lb = st.sb("lg", [P, 1]), st.sb("lb", [P, 1])
        loads = [(w1, "l3f_w1"), (w2, "l3f_w2"), (b1, "l3f_b1"), (b2, "l3f_b2"), (lg, "l3f_lg"), (lb, "l3f_lb")]
        half_power = st.sb("half_power", [P, TPC])
        h, hT = st.two("h", [P, TPC, P]), st.two("hT", [P, CH])
        stats = st.two("stats", [P, TPC, 6])
        mean, delta, var, rstd = (st.two(n, [P, TPC]) for n in ("mean", "delta", "var", "rstd"))
        gate, hid = st.two("gate", [P, F, CH]), st.two("hid", [P, F, CH])
        loaded, ready = st.sem("loaded"), st.sem("ready")
        (moved, h_set, stat, parts, terms, aggregated, rooted, normed_h, turned, copied, up, gelued, hidden, down, added) = (
            st.sem2(n) for n in ("moved", "h_set", "stat", "parts", "terms", "aggregated", "rooted", "normed_h", "turned",
                                 "copied", "up", "gelued", "hidden", "down", "added"))
        A0, A1 = [x[:, 0:CH] for x in m.A], [x[:, CH:2 * CH] for x in m.A]
        B0, B1 = [x[:, 0:CH] for x in m.B], [x[:, CH:2 * CH] for x in m.B]
        up_bank = lambda j, o: (A0, A1)[o % 2][j]
        gate_bank = lambda j, o: (B0, B1)[o % 2][j]
        with nc.Block() as block:
            @block.sync
            def _(sp):
                for tile, src in loads:
                    sp.dma_start(tile[:], d[src][layer]).then_inc(loaded, 16)

            @block.vector
            def _(dve):
                dve.wait_ge(loaded, 16 * len(loads))
                with dve.Fori(0, NCH // 2) as it:
                    for j in range(2):
                        ty = y[:, bass.ds(it * 8 + 4 * j, TPC), :]
                        dve.wait_ge(turned[j], it)
                        dve.tensor_copy(h[j][:, :, 0:S], ty[:, :, 0:S])
                        dve.wait_ge(moved[j], it + 1)
                        dve.tensor_copy(h[j][:, :, S:P], A0[j][:, 0:TPC * S].rearrange("p (t w) -> p t w", t=TPC))\
                           .then_inc(h_set[j], 1)
                    for j in range(2):
                        dve.wait_ge(h_set[j], it + 1)
                        for t in range(TPC):
                            last = dve.bn_stats(stats[j][:, t], h[j][:, t])
                        last.then_inc(stat[j], 1)
                    for j in range(2):
                        dve.wait_ge(stat[j], it + 1)
                        mean_e, m2_e, mean_o, m2_o = (stats[j][:, :, k] for k in (1, 2, 4, 5))
                        dve.wait_ge(normed_h[j], it)
                        dve.tensor_tensor(mean[j][:], mean_e, mean_o, ALU.add)
                        dve.tensor_tensor(delta[j][:], mean_e, mean_o, ALU.subtract)
                        dve.tensor_tensor(var[j][:], m2_e, m2_o, ALU.add).then_inc(parts[j], 1)
                    for j in range(2):
                        dve.wait_ge(parts[j], it + 1)
                        dve.tensor_scalar(mean[j][:], mean[j][:], 0.5, None, ALU.mult)
                        dve.scalar_tensor_tensor(delta[j][:], delta[j][:], 0.25, delta[j][:], ALU.mult, ALU.mult)
                        dve.tensor_scalar(var[j][:], var[j][:], 1.0 / P, 1e-5, ALU.mult, ALU.add).then_inc(terms[j], 1)
                    for j in range(2):
                        dve.wait_ge(terms[j], it + 1)
                        dve.tensor_tensor(var[j][:], var[j][:], delta[j][:], ALU.add).then_inc(aggregated[j], 1)
                    for j in range(2):
                        dve.wait_ge(rooted[j], it + 1)
                        for t in range(TPC):
                            last = dve.tensor_scalar(h[j][:, t], h[j][:, t], mean[j][:, t:t + 1], rstd[j][:, t:t + 1],
                                                     ALU.subtract, ALU.mult)
                        last.then_inc(normed_h[j], 1)
                    for j in range(2):
                        for o, (_, k) in enumerate(PARTS3):
                            dve.wait_ge(gelued[j], it * F + o + 1)
                            dve.scalar_tensor_tensor(hid[j][0:k, o], up_bank(j, o)[0:k], b1[0:k, 0, o:o + 1],
                                                     gate[j][0:k, o], ALU.add, ALU.mult).then_inc(hidden[j], 1)
                    for j in range(2):
                        dve.wait_ge(down[j], it + 1)
                        ty = y[:, bass.ds(it * 8 + 4 * j, TPC), :]
                        dve.tensor_tensor(ty, ty, A1[j].rearrange("p (t w) -> p t w", t=TPC), ALU.add)\
                           .then_inc(added[j], 1)

            @block.gpsimd
            def _(pool):
                pool.memset(half_power[:], -0.5).then_inc(ready, 1)
                pool.wait_ge(ready, 1)
                with pool.Fori(0, NCH // 2) as it:
                    for j in range(2):
                        pool.wait_ge(aggregated[j], it + 1)
                        pool.wait_ge(normed_h[j], it)
                        pool.tensor_tensor(rstd[j][:], var[j][:], half_power[:], ALU.pow).then_inc(rooted[j], 1)

            @block.scalar
            def _(act):
                act.wait_ge(loaded, 16 * len(loads))
                with act.Fori(0, NCH // 2) as it:
                    for j in range(2):
                        act.wait_ge(turned[j], it + 1)
                        act.activation(hT[j][:], A1[j], ACT.Identity, scale=lg[:], bias=lb[:]).then_inc(copied[j], 1)
                    for j in range(2):
                        for o, (_, k) in enumerate(PARTS3):
                            act.wait_ge(up[j], it * F + o + 1)
                            act.activation(gate[j][0:k, o], gate_bank(j, o)[0:k], ACT.Gelu, bias=b1[0:k, 1, o:o + 1])\
                               .then_inc(gelued[j], 1)

            @block.tensor
            def _(pe):
                pe.wait_ge(loaded, 16 * len(loads))
                with pe.Fori(0, NCH // 2) as it:
                    for j in range(2):
                        pe.wait_ge(added[j], it)
                        pe.matmul(A0[j][:, 0:TPC * S], m.shift[:], y[:, bass.ds(it * 8 + 4 * j, TPC), S:P],
                                  start=True, stop=True).then_inc(moved[j], 1)
                    for j in range(2):
                        pe.wait_ge(normed_h[j], it + 1)
                        for t in range(TPC):
                            last = pe.transpose(A1[j][:, t * P:t * P + P], h[j][:, t], m.ident[:])
                        last.then_inc(turned[j], 1)
                    for j in range(2):
                        pe.wait_ge(copied[j], it + 1)
                        for o, (n, k) in enumerate(PARTS3):
                            if o >= 2:
                                pe.wait_ge(hidden[j], it * F + o - 1)
                            pe.matmul(up_bank(j, o)[0:k], w1[:, n:n + k], hT[j][:], start=True, stop=True)
                            pe.matmul(gate_bank(j, o)[0:k], w1[:, HID3 + n:HID3 + n + k], hT[j][:],
                                      start=True, stop=True).then_inc(up[j], 1)
                    for j in range(2):
                        pe.wait_ge(hidden[j], it * F + F)
                        for t in range(TPC):
                            dst = A1[j][:, t * P:t * P + P]
                            pe.matmul(dst, m.ones_row[:], b2[:], start=True, stop=False)
                            for o, (_, k) in enumerate(PARTS3):
                                last = pe.matmul(dst, hid[j][0:k, o, t * P:t * P + P], w2[0:k, o],
                                                 start=False, stop=(o == F - 1))
                        last.then_inc(down[j], 1)


def l3_ffn(nc, m, d, own):
    y = own.enter_context(nc.sbuf_tensor("l3f_y", [P, NT, P], F32))
    with Stage(nc, "l3f_in") as st:
        with nc.Block() as block:
            @block.vector
            def _(dve):
                with dve.Fori(0, PAIRS) as it:
                    for j in range(2):
                        t = it * 2 + j
                        normed(dve, m, y[:, t, :], t)
    for layer in range(2):
        local_attention(nc, m, d, y, layer)
        gated_gelu(nc, m, d, y, layer)
    with Stage(nc, "l3f_out") as st:
        with nc.Block() as block:
            @block.vector
            def _(dve):
                with dve.Fori(0, NCH) as it:
                    for xs, ys in ((m.X[:, bass.ds(it * TPC, TPC), :], y[:, bass.ds(it * TPC, TPC), :]),):
                        dve.scalar_tensor_tensor(xs, ys, m.tanh_g[:, 7:8], xs, ALU.mult, ALU.add)


class Memory:

    def __init__(self, nc, ctx):
        def sb(name, shape, dt=F32):
            return ctx.enter_context(nc.sbuf_tensor(name, list(shape), dt))

        self.X = sb("X", [P, NT, P])
        self.S6 = sb("S6", [P, NT, 6])
        self.mean, self.rstd = sb("mean", [P, NT]), sb("rstd", [P, NT])
        self.ident, self.ident_bf = sb("ident", [P, P]), sb("ident_bf", [P, P], BF16)
        self.blockones = sb("blockones", [P, P])
        self.tri = sb("tri", [P, P])
        self.shift = sb("shift", [P, P])
        self.eye64 = sb("eye64", [P, S])
        self.causal, self.causal_bf = sb("causal", [P, S]), sb("causal_bf", [P, S], BF16)
        self.half = sb("half", [P, 2])
        self.head16, self.head8 = sb("head16", [P, 16]), sb("head8", [P, 8])
        self.gates, self.tanh_g = sb("gates", [P, 8]), sb("tanh_g", [P, 8])
        self.ones_row = sb("ones_row", [1, P])
        self.A = [ctx.enter_context(nc.psum_tensor(f"A{j}", [P, 1024], F32)) for j in range(2)]
        self.B = [ctx.enter_context(nc.psum_tensor(f"B{j}", [P, 1024], F32)) for j in range(2)]


def store(nc, m, d):
    with Stage(nc, "store") as st:
        stored = st.sem("stored")
        with nc.Block() as block:
            @block.sync
            def _(sp):
                sp.dma_start(d["out"], m.X[:]).then_inc(stored, 16)
                sp.wait_ge(stored, 16)


def program(nc, d, stages=None):
    with ExitStack() as ctx:
        m = Memory(nc, ctx)
        setup(nc, m, d)
        for n, stage in enumerate(STAGES):
            if stages is None or n in stages:
                norm_header(nc, m, f"norm{n}")
                with ExitStack() as own:
                    stage(nc, m, d, own)
        store(nc, m, d)


def l0_xattn(nc, m, d, own):
    sb = lambda n, s: own.enter_context(nc.sbuf_tensor(n, s, F32))
    m.gate, m.fsum, m.a = sb("gate", [P, NT, 16]), sb("fsum", [P, NT, 8]), sb("a", [P, NT, 8])
    m.h = sb("h", [P, NT, P])
    gated_memory(nc, m, d)


STAGES = [l0_xattn, l0_ffn, l1_xattn, l1_ffn, l2_xattn, l2_ffn, l3_xattn, l3_ffn]


def shape_constants():
    i, b = np.arange(P) % S, np.arange(P) // S
    same = b[:, None] == b[None, :]
    f = lambda x: np.ascontiguousarray(x.astype(np.float32))
    return {
        "c_ident": f(np.eye(P)),
        "c_blockones": f(same),
        "c_tri": f(same & (i[:, None] <= i[None, :])),
        "c_shift": f(same & (i[:, None] + 1 == i[None, :])),
        "c_lower_e": f(np.broadcast_to(np.arange(8)[None, None, :] < np.arange(8)[None, :, None], (P, 8, 8))),
        "c_half": f(b[:, None] == np.arange(2)[None, :]),
        "c_eye64": f(i[:, None] == np.arange(S)[None, :]),
        "c_causal": f(np.where(np.arange(S)[None, :] > i[:, None], NEG, 0.0)),
        "c_head16": f(np.arange(P)[:, None] // 8 == np.arange(16)[None, :]),
        "c_head8": f(np.arange(P)[:, None] // 16 == np.arange(8)[None, :]),
    }


def rotary_tables():
    f = np.float32
    half = np.arange(0, W3, 2, dtype=f)
    freqs = np.arange(S, dtype=f)[:, None] * (f(1.0) / f(10000.0) ** (half / f(W3)))[None, :]
    freqs = np.concatenate([freqs, freqs], axis=-1)
    base = (half + f(0.4 * W3)) / f(1.4 * W3)
    power = (np.arange(S, dtype=f) - f(S // 2)) / f(S // 2)
    scale = base[None, :] ** power[:, None]
    scale = np.concatenate([scale, scale], axis=-1)
    cos, sin = np.cos(freqs), np.sin(freqs)
    sin[:, :W3 // 2] *= f(-1.0)
    both = lambda t: np.ascontiguousarray(np.tile(np.stack([t * scale, t / scale], axis=1), (2, 1, 1)).astype(f))
    return both(cos), both(sin)


def lay_out(v):
    rows = lambda a: np.ascontiguousarray(np.broadcast_to(a.reshape(1, -1), (P, a.size)))
    T = lambda a: np.ascontiguousarray(a.T)
    x, ctx = v["x"], v["ctx_1024"]
    d = dict(shape_constants())
    d["x"] = np.ascontiguousarray(x.reshape(NT, P, P).transpose(1, 0, 2))
    d["ctxT"] = np.ascontiguousarray(ctx.reshape(NT, P, P).transpose(0, 2, 1))
    d["ctx"] = np.ascontiguousarray(ctx.transpose(1, 0, 2))
    d["gates"] = rows(np.concatenate([v["g_xattn"], v["g_ffn"]]))
    wi, wf = v["L0_xattn_igate_w"], v["L0_xattn_fgate_w"]
    for n, k in enumerate("qkv"):
        d[f"l0_gate_{k}"] = T(np.concatenate([wi, wf])[:, n * P:(n + 1) * P])
    d["l0_gate_b"] = rows(np.concatenate([v["L0_xattn_igate_b"], v["L0_xattn_fgate_b"]]))
    d["l0_norm_w"] = rows(v["L0_xattn_norm_w"])
    more_layout(d, v, rows, T)
    return d


def more_layout(d, v, rows, T):
    parts = lambda a: np.ascontiguousarray(a.reshape(-1, P, a.shape[-1]).transpose(1, 0, 2))
    cols = lambda a: np.ascontiguousarray(a.reshape(-1, P).T)
    for n in ("w1", "w2"):
        d[f"l0f_{n}"] = T(v[f"L0_ffn_{n}_w"])
    for n in ("h1", "h2", "w3"):
        d[f"l0f_{n}"] = parts(v[f"L0_ffn_{n}_w"].T)
    d["l0f_s"] = np.ascontiguousarray(np.stack([cols(v[f"L0_ffn_{n}_s"]) for n in ("w1", "w2", "h1", "h2")], axis=1))
    d["l0f_s3"] = rows(v["L0_ffn_w3_s"])
    column = lambda a: np.ascontiguousarray(a.reshape(-1, 1))
    for n in "qkvo":
        d[f"l1x_w{n}"] = T(v[f"L1_xattn_w{n}"])
    d["l1x_bq"], d["l1x_bk"] = column(v["L1_xattn_bq"]), column(v["L1_xattn_bk"])
    d["l1x_bv"], d["l1x_bo"] = rows(v["L1_xattn_bv"]), v["L1_xattn_bo"].reshape(1, P)
    d["l1x_mask"] = np.ascontiguousarray(v["mask_BxS_ik0"].reshape(NT, P).T)
    d["l2x_wo"], d["l2x_bo"] = T(v["L2_xattn_W_out"]), v["L2_xattn_b_out"].reshape(1, P)
    d["l2x_mask"] = np.ascontiguousarray(v["mask_Bx1xSxS2_ik1"].reshape(NT, P, S).transpose(1, 0, 2))
    for n in "qk":
        d[f"l3x_w{n}"] = T(v[f"L3_xattn_W{n}_w"])
        d[f"l3x_b{n}"] = column(v[f"L3_xattn_W{n}_b"])
    keys = np.broadcast_to(v["mask_BxS2_ik1"].reshape(NT, 2, 1, S), (NT, 2, S, S))
    d["l3x_mask"] = np.ascontiguousarray(keys.transpose(1, 2, 0, 3)).reshape(P, NT, S)
    w = [v[f"L1_ffn_w_{n}"].reshape(3, P, P).transpose(1, 0, 2) for n in ("up", "gate")]
    d["l1f_w"] = np.ascontiguousarray(np.concatenate([*w, v["L1_ffn_w_down"].reshape(P, 3, P)], axis=1).reshape(P, 9 * P))
    d["c_cos"], d["c_sin"] = rotary_tables()
    for n, k in enumerate("qkv"):
        d[f"l3f_w{k}"] = np.ascontiguousarray(v["L3_ffn_wqkv"][:, :, n * INNER:(n + 1) * INNER])
    d["l3f_wo"] = np.ascontiguousarray(v["L3_ffn_wo"].reshape(2, -1, P, P).transpose(0, 2, 1, 3))
    scales = np.stack([v["L3_ffn_q_scale"], v["L3_ffn_k_scale"]], axis=1)
    swapped = np.concatenate([scales[:, :, W3 // 2:], scales[:, :, :W3 // 2]], axis=-1)
    for n, a in (("scale", scales), ("scale_swapped", swapped)):
        d[f"l3f_{n}"] = np.ascontiguousarray(np.broadcast_to(a[:, None], (2, P, 2, W3)))
    pad = len(PARTS3) * P - HID3
    d["l3f_w1"] = v["L3_ffn_w1"]
    d["l3f_w2"] = np.ascontiguousarray(np.pad(v["L3_ffn_w2"], ((0, 0), (0, pad), (0, 0)))
                                       .reshape(2, -1, P, P).transpose(0, 2, 1, 3))
    d["l3f_b1"] = np.ascontiguousarray(np.pad(v["L3_ffn_b1"].reshape(2, 2, HID3), ((0, 0), (0, 0), (0, pad)))
                                       .reshape(2, 2, -1, P).transpose(0, 3, 1, 2))
    d["l3f_b2"] = v["L3_ffn_b2"].reshape(2, 1, P)
    d["l3f_lg"], d["l3f_lb"] = v["L3_ffn_ln_g"].reshape(2, P, 1), v["L3_ffn_ln_b"].reshape(2, P, 1)
    d["l2f_wr"] = v["L2_ffn_Wr"]
    d["l2f_temp"] = rows(v["L2_ffn_temperature"])
    for n in ("g", "u", "d"):
        d[f"l2f_w{n}"] = np.ascontiguousarray(v[f"L2_ffn_W{n}"].transpose(1, 0, 2))


def declare(nc, arrays):
    d = {n: nc.dram_tensor(f"in_{n}", a.shape, mybir.dt.from_np(a.dtype), kind="ExternalInput").ap()
         for n, a in arrays.items()}
    d["out"] = nc.dram_tensor("out", (P, NT, P), F32, kind="ExternalOutput").ap()
    return d


def kernel(**inputs):
    import concourse.bacc as bacc
    from concourse.bass_utils import run_bass_kernel_spmd

    arrays = lay_out({n: np.asarray(a) for n, a in inputs.items()})
    nc = bacc.Bacc("TRN2", target_bir_lowering=False, num_devices=1)
    program(nc, declare(nc, arrays))
    r = run_bass_kernel_spmd(nc, [{f"in_{n}": a for n, a in arrays.items()}], core_ids=[0])
    out = r.results[0]["out"]
    return np.ascontiguousarray(out.transpose(1, 0, 2)).reshape(NB, S, P)
```

```python
from contextlib import ExitStack

import numpy as np

import concourse.bass as bass
from concourse import mybir

F32 = mybir.dt.float32
BF16 = mybir.dt.bfloat16
I32 = mybir.dt.int32
I16 = mybir.dt.int16
ALU = mybir.AluOpType
ACT = mybir.ActivationFunctionType
AX = mybir.AxisListType.X

P = 128
S = 64
NB = 128
NT = NB * S // P
PAIRS = NT // 2
CH = 512
NCH = NB * S // CH
TPC = CH // P
NEG = -1e30
ROUND = 12582912.0


def past(n):
    return n + 1


class Stage:

    def __init__(self, nc, name):
        self.nc, self.name, self.stack, self.sems = nc, name, ExitStack(), []

    def __enter__(self):
        return self

    def __exit__(self, *exc):
        if exc[0] is None:
            self.nc.clear_and_free_semaphores(self.sems)
            self.nc.all_engine_barrier()
            self.stack.close()

    def sb(self, name, shape, dt=F32):
        return self.stack.enter_context(self.nc.sbuf_tensor(f"{self.name}_{name}", list(shape), dt))

    def two(self, name, shape, dt=F32):
        return [self.sb(f"{name}{j}", shape, dt) for j in range(2)]

    def sem(self, name):
        self.sems.append(self.nc.alloc_semaphore(f"{self.name}_{name}"))
        return self.sems[-1]

    def counter(self, name):
        sem = self.sem(name)
        self.nc.sync.sem_inc(sem, 1)
        return sem

    def sem2(self, name):
        return [self.counter(f"{name}{j}") for j in range(2)]


def at(it, j, lag, work):
    pair, j = it + (j + lag) // 2, (j + lag) % 2
    if not isinstance(pair, int) or 0 <= pair < PAIRS:
        work(pair, j)


def steps(eng, step, ahead=1, behind=1):
    for it in range(-ahead, ahead):
        for j in range(2):
            step(it, j)
    with eng.Fori(ahead, PAIRS - ahead) as it:
        for j in range(2):
            step(it, j)
    for it in range(PAIRS - ahead, PAIRS + behind):
        for j in range(2):
            step(it, j)


def setup(nc, m, d):
    with Stage(nc, "setup") as st:
        loaded, filled = st.sem("loaded"), st.sem("filled")
        consts = [(m.ident, d["c_ident"]), (m.blockones, d["c_blockones"]), (m.tri, d["c_tri"]),
                  (m.shift, d["c_shift"]), (m.eye64, d["c_eye64"]), (m.causal, d["c_causal"]),
                  (m.half, d["c_half"]), (m.head_of_8, d["c_head_of_8"]), (m.head8, d["c_head8"]), (m.gates, d["gates"])]
        n_loads = 16 * (1 + len(consts))
        with nc.Block() as block:
            @block.sync
            def _(sp):
                sp.dma_start(m.X[:], d["x"]).then_inc(loaded, 16)
                for tile, src in consts:
                    sp.dma_start(tile[:], src).then_inc(loaded, 16)

            @block.scalar
            def _(act):
                act.wait_ge(loaded, n_loads)
                act.activation(m.tanh_g[:], m.gates[:], ACT.Tanh)
                act.copy(m.ident_bf[:], m.ident[:])
                act.copy(m.causal_bf[:], m.causal[:])
                act.wait_ge(filled, 1)

            @block.vector
            def _(dve):
                dve.memset(m.ones_row[:], 1.0).then_inc(filled, 1)
                dve.wait_ge(loaded, n_loads)
                with dve.Fori(0, NT) as t:
                    dve.bn_stats(m.S6[:, t, :], m.X[:, t, :])


def norm_header(nc, m, name, s6=None):
    s6 = m.S6 if s6 is None else s6
    with Stage(nc, name) as st:
        delta, spread = st.sb("delta", [P, NT]), st.sb("spread", [P, NT])
        step, rooted = st.sem("step"), st.sem("rooted")
        mean_e, m2_e, mean_o, m2_o = (s6[:, :, k] for k in (1, 2, 4, 5))
        with nc.Block() as block:
            @block.vector
            def _(dve):
                dve.tensor_tensor(m.mean[:], mean_e, mean_o, ALU.add)
                dve.tensor_tensor(delta[:], mean_e, mean_o, ALU.subtract)
                dve.tensor_tensor(spread[:], m2_e, m2_o, ALU.add).then_inc(step, 1)
                dve.wait_ge(step, 1)
                dve.tensor_scalar(m.mean[:], m.mean[:], 0.5, None, ALU.mult)
                dve.scalar_tensor_tensor(delta[:], delta[:], 0.25, delta[:], ALU.mult, ALU.mult)
                dve.tensor_scalar(spread[:], spread[:], 1.0 / P, 1e-5, ALU.mult, ALU.add).then_inc(step, 1)
                dve.wait_ge(step, 2)
                dve.tensor_tensor(spread[:], spread[:], delta[:], ALU.add).then_inc(step, 1)
                dve.wait_ge(rooted, 1)
                dve.reciprocal(m.rstd[:], delta[:])

            @block.scalar
            def _(act):
                act.wait_ge(step, 3)
                act.activation(delta[:], spread[:], ACT.Sqrt).then_inc(rooted, 1)


def normed(dve, m, dst, t, src=None):
    src = m.X if src is None else src
    return dve.tensor_scalar(dst, src[:, t, :], m.mean[:, bass.ds(t, 1)], m.rstd[:, bass.ds(t, 1)],
                             ALU.subtract, ALU.mult)


def per_head(ap, h, w):
    return ap.rearrange("p (h w) -> p h w", h=h, w=w)


def spread_heads(ap, w):
    return ap[:, :, None].broadcast_to([ap.shape[0], ap.shape[1], w])


def repeat_heads(ap, h):
    return ap[:, None, :].broadcast_to([ap.shape[0], h, ap.shape[1]])


def gated_memory(nc, m, d):
    H, W = 8, 16
    KW = H * S

    with Stage(nc, "gates") as st:
        wq, wk, wv = st.sb("wq", [P, 2 * H]), st.sb("wk", [P, 2 * H]), st.sb("wv", [P, 2 * H])
        bias, weights = st.sb("bias", [P, 2 * H]), st.sem("weights")
        xn, xnT, ctxT = st.two("xn", [P, P]), st.two("xnT", [P, P]), st.two("ctxT", [P, P])
        ctx_in, normed_x, turned, copied = (st.sem2(n) for n in ("ctx_in", "normed_x", "turned", "copied"))
        summed, biased = st.sem2("summed"), st.sem2("biased")
        with nc.Block() as block:
            @block.sync
            def _(sp):
                for tile, src in ((wq, "l0_gate_q"), (wk, "l0_gate_k"), (wv, "l0_gate_v"), (bias, "l0_gate_b")):
                    sp.dma_start(tile[:], d[src]).then_inc(weights, 16)
                with sp.Fori(0, PAIRS) as it:
                    for j in range(2):
                        sp.wait_ge(summed[j], past(it))
                        sp.dma_start(ctxT[j][:], d["ctxT"][it * 2 + j]).then_inc(ctx_in[j], 16)

            @block.vector
            def _(dve):
                dve.wait_ge(weights, 64)
                with dve.Fori(0, PAIRS) as it:
                    for j in range(2):
                        dve.wait_ge(turned[j], past(it))
                        normed(dve, m, xn[j][:], it * 2 + j).then_inc(normed_x[j], 1)
                    for j in range(2):
                        dve.wait_ge(summed[j], past(it + 1))
                        dve.tensor_tensor(m.gate[:, it * 2 + j, :], m.B[j][:, 0:2 * H], bias[:],
                                          ALU.add).then_inc(biased[j], 1)

            @block.tensor
            def _(pe):
                pe.wait_ge(weights, 64)
                with pe.Fori(0, PAIRS) as it:
                    for j in range(2):
                        pe.wait_ge(normed_x[j], past(it + 1))
                        pe.wait_ge(copied[j], past(it))
                        pe.transpose(m.A[j][:, 0:P], xn[j][:], m.ident[:]).then_inc(turned[j], 1)
                    for j in range(2):
                        pe.wait_ge(copied[j], past(it + 1))
                        pe.wait_ge(ctx_in[j], past(it * 16 + 16))
                        pe.wait_ge(biased[j], past(it))
                        g = m.B[j][:, 0:2 * H]
                        pe.matmul(g, xnT[j][:], wq[:], start=True, stop=False)
                        pe.matmul(g, ctxT[j][:], wk[:], start=False, stop=False)
                        pe.matmul(g, ctxT[j][:], wv[:], start=False, stop=True).then_inc(summed[j], 1)

            @block.scalar
            def _(act):
                with act.Fori(0, PAIRS) as it:
                    for j in range(2):
                        act.wait_ge(turned[j], past(it + 1))
                        act.wait_ge(summed[j], past(it))
                        act.copy(xnT[j][:], m.A[j][:, 0:P]).then_inc(copied[j], 1)

    with Stage(nc, "decay") as st:
        f0, l0 = st.sb("f0", [P, NT, H]), st.sb("l0", [P, NT, H])
        step, logged, cum = st.sem("step"), st.sem("logged"), st.sem("cum")
        forget = m.gate[:, :, H:2 * H]
        flat = lambda x: x[:].rearrange("p t h -> p (t h)")
        with nc.Block() as block:
            @block.vector
            def _(dve):
                dve.scalar_tensor_tensor(f0[:], forget, -1.0, forget, ALU.mult, ALU.min).then_inc(step, 1)
                dve.wait_ge(logged, 2)
                dve.scalar_tensor_tensor(f0[:], forget, 0.0, l0[:], ALU.min, ALU.subtract).then_inc(step, 1)
                dve.wait_ge(cum, 1)
                sums = m.A[0][:, 0:NT * H].rearrange("p (t h) -> p t h", t=NT)
                dve.tensor_copy(m.fsum[:], sums)
                dve.tensor_tensor(m.a[:], m.gate[:, :, 0:H], sums, ALU.subtract)

            @block.scalar
            def _(act):
                act.wait_ge(step, 1)
                act.activation(l0[:], f0[:], ACT.Exp).then_inc(logged, 1)
                act.wait_ge(logged, 1)
                act.activation(l0[:], l0[:], ACT.Ln, bias=1.0).then_inc(logged, 1)

            @block.tensor
            def _(pe):
                pe.wait_ge(step, 2)
                pe.matmul(m.A[0][:, 0:NT * H], m.tri[:], flat(f0), start=True, stop=True).then_inc(cum, 1)

    with Stage(nc, "memory") as st:
        xn, qT, ctxT = st.two("xn", [P, P]), st.two("qT", [P, P]), st.two("ctxT", [P, P])
        ctx2 = st.two("ctx2", [P, 2, P])
        kx = st.two("kx", [P, 2, H, S])
        ax = st.two("ax", [P, H, S])
        vd = st.two("vd", [P, 2, H // 2, 2, W + 1])
        dmat, cT = st.two("dmat", [P, H, S]), st.two("cT", [P, H // 2, P])
        top, low, den = st.two("top", [P, H]), st.two("low", [P, H]), st.two("den", [P, H])
        names = ("ctx_in ctx2_in normed_x turned copied keys_apart a_apart values_apart scored z_done max_done"
                 " shifted exped weighted c_turned c_copied mixed floor_in floored den_abs den_max den_eps den_inv"
                 " h_done")
        e = {n: st.sem2(n) for n in names.split()}
        ctx_in, ctx2_in, normed_x, turned, copied = (e[n] for n in ("ctx_in", "ctx2_in", "normed_x", "turned", "copied"))
        ones_set = st.sem("ones_set")
        with nc.Block() as block:
            @block.sync
            def _(sp):
                with sp.Fori(0, PAIRS) as it:
                    for j in range(2):
                        sp.wait_ge(e["keys_apart"][j], past(it))
                        sp.dma_start(ctxT[j][:], d["ctxT"][it * 2 + j]).then_inc(ctx_in[j], 16)
                        sp.wait_ge(e["values_apart"][j], past(it))
                        for half in range(2):
                            sp.dma_start(ctx2[j][half * S:half * S + S], d["ctx"][:, bass.ds(it * 4 + 2 * j, 2), :])\
                              .then_inc(ctx2_in[j], 16)

            @block.gpsimd
            def _(pool):
                for j in range(2):
                    for b in range(2):
                        pool.tensor_copy(vd[j][:, b, :, :, W], repeat_heads(m.half[:], H // 2)).then_inc(ones_set, 1)
                with pool.Fori(0, PAIRS) as it:
                    for j in range(2):
                        pool.wait_ge(ctx_in[j], past(it * 16 + 16))
                        pool.wait_ge(e["scored"][j], past(it))
                        for b in range(2):
                            last = pool.tensor_tensor(kx[j][:, b], repeat_heads(ctxT[j][:, b * S:b * S + S], H),
                                                      spread_heads(m.head8[:], S), ALU.mult)
                        last.then_inc(e["keys_apart"][j], 1)
                        pool.wait_ge(e["z_done"][j], past(it))
                        pool.tensor_tensor(ax[j][:], spread_heads(m.a[:, it * 2 + j, :], S),
                                           repeat_heads(m.eye64[:], H), ALU.mult).then_inc(e["a_apart"][j], 1)
                        pool.wait_ge(ctx2_in[j], past(it * 32 + 32))
                        pool.wait_ge(e["mixed"][j], past(it))
                        for b in range(2):
                            last = pool.tensor_tensor(
                                vd[j][:, b, :, :, 0:W], ctx2[j][:, b].rearrange("p (g u w) -> p g u w", g=H // 2, u=2),
                                m.half[:, None, :, None].broadcast_to([P, H // 2, 2, W]), ALU.mult)
                        last.then_inc(e["values_apart"][j], 1)

            @block.vector
            def _(dve):
                with dve.Fori(0, PAIRS) as it:
                    for j in range(2):
                        dve.wait_ge(turned[j], past(it))
                        normed(dve, m, xn[j][:], it * 2 + j).then_inc(normed_x[j], 1)
                    for j in range(2):
                        z = per_head(m.B[j][:, 0:KW], H, S)
                        dve.wait_ge(e["z_done"][j], past(it + 1))
                        dve.wait_ge(e["floored"][j], past(it))
                        dve.tensor_reduce(top[j][:], z, AX, ALU.max).then_inc(e["max_done"][j], 1)
                        dve.wait_ge(e["max_done"][j], past(it + 1))
                        dve.wait_ge(e["weighted"][j], past(it))
                        dve.tensor_tensor(dmat[j][:], z, spread_heads(top[j][:], S), ALU.subtract)\
                           .then_inc(e["shifted"][j], 1)
                        dve.wait_ge(e["floored"][j], past(it))
                        dve.tensor_tensor(low[j][:], top[j][:], m.fsum[:, it * 2 + j, :], ALU.add)\
                           .then_inc(e["floor_in"][j], 1)
                    for j in range(2):
                        dve.wait_ge(e["exped"][j], past(it + 1))
                        dve.wait_ge(e["scored"][j], past(it + 1))
                        dve.wait_ge(e["c_turned"][j], past(it))
                        dve.tensor_tensor(dmat[j][:], per_head(m.A[j][:, 512:512 + KW], H, S), dmat[j][:], ALU.mult)\
                           .then_inc(e["weighted"][j], 1)
                    for j in range(2):
                        out = m.A[j][:, 0:H * (W + 1)].rearrange("p (h w) -> p h w", h=H)
                        dve.wait_ge(e["mixed"][j], past(it + 1))
                        dve.tensor_reduce(den[j][:], out[:, :, W:W + 1], AX, ALU.max, apply_absolute_value=True).then_inc(e["den_abs"][j], 1)
                        dve.wait_ge(e["den_abs"][j], past(it + 1))
                        dve.wait_ge(e["floored"][j], past(it + 1))
                        dve.tensor_tensor(den[j][:], den[j][:], low[j][:], ALU.max).then_inc(e["den_max"][j], 1)
                        dve.wait_ge(e["den_max"][j], past(it + 1))
                        dve.tensor_scalar(den[j][:], den[j][:], 1e-6, None, ALU.add).then_inc(e["den_eps"][j], 1)
                        dve.wait_ge(e["den_eps"][j], past(it + 1))
                        dve.reciprocal(den[j][:], den[j][:]).then_inc(e["den_inv"][j], 1)
                        dve.wait_ge(e["den_inv"][j], past(it + 1))
                        dve.tensor_tensor(per_head(m.h[:, it * 2 + j, :], H, W), out[:, :, 0:W],
                                          spread_heads(den[j][:], W), ALU.mult).then_inc(e["h_done"][j], 1)

            @block.scalar
            def _(act):
                with act.Fori(0, PAIRS) as it:
                    for j in range(2):
                        act.wait_ge(turned[j], past(it + 1))
                        act.wait_ge(e["scored"][j], past(it))
                        act.activation(qT[j][:], m.A[j][:, 0:P], ACT.Copy, scale=float(W) ** -0.5).then_inc(copied[j], 1)
                    for j in range(2):
                        act.wait_ge(e["shifted"][j], past(it + 1))
                        act.activation(dmat[j][:], dmat[j][:], ACT.Exp).then_inc(e["exped"][j], 1)
                        act.wait_ge(e["floor_in"][j], past(it + 1))
                        act.wait_ge(e["den_max"][j], past(it))
                        act.activation(low[j][:], low[j][:], ACT.Exp, scale=-1.0).then_inc(e["floored"][j], 1)
                    for j in range(2):
                        act.wait_ge(e["c_turned"][j], past(it + 1))
                        act.wait_ge(e["mixed"][j], past(it))
                        act.copy(cT[j][:], m.B[j][:, 512:512 + KW].rearrange("p (g q) -> p g q", q=P))\
                           .then_inc(e["c_copied"][j], 1)

            @block.tensor
            def _(pe):
                pe.wait_ge(ones_set, 4)
                with pe.Fori(0, PAIRS) as it:
                    for j in range(2):
                        pe.wait_ge(normed_x[j], past(it + 1))
                        pe.wait_ge(e["h_done"][j], past(it))
                        pe.transpose(m.A[j][:, 0:P], xn[j][:], m.ident[:]).then_inc(turned[j], 1)
                    for j in range(2):
                        pe.wait_ge(e["a_apart"][j], past(it + 1))
                        pe.wait_ge(e["shifted"][j], past(it))
                        pe.matmul(m.B[j][:, 0:KW], m.blockones[:], ax[j][:], start=True, stop=False)
                        pe.matmul(m.B[j][:, 0:KW], m.ident_bf[:], repeat_heads(m.causal_bf[:], H),
                                  start=False, stop=True).then_inc(e["z_done"][j], 1)
                        pe.wait_ge(copied[j], past(it + 1))
                        pe.wait_ge(e["keys_apart"][j], past(it + 1))
                        pe.wait_ge(e["weighted"][j], past(it))
                        for b in range(2):
                            last = pe.matmul(m.A[j][b * S:b * S + S, 512:512 + KW], qT[j][:, b * S:b * S + S],
                                             kx[j][:, b], start=True, stop=True)
                        last.then_inc(e["scored"][j], 1)
                    for j in range(2):
                        pe.wait_ge(e["weighted"][j], past(it + 1))
                        pe.wait_ge(e["c_copied"][j], past(it))
                        c = dmat[j][:].rearrange("p h k -> p (h k)")
                        for g in range(H // 2):
                            last = pe.transpose(m.B[j][:, 512 + g * P:512 + g * P + P], c[:, g * P:g * P + P], m.ident[:])
                        last.then_inc(e["c_turned"][j], 1)
                    for j in range(2):
                        pe.wait_ge(e["c_copied"][j], past(it + 1))
                        pe.wait_ge(e["values_apart"][j], past(it + 1))
                        for b in range(2):
                            for g in range(H // 2):
                                n = 2 * (W + 1)
                                last = pe.matmul(m.A[j][b * S:b * S + S, g * n:g * n + n], cT[j][:, g, b * S:b * S + S],
                                                 vd[j][:, b, g], start=True, stop=True)
                        last.then_inc(e["mixed"][j], 1)

    with Stage(nc, "headnorm") as st:
        G = 8
        STEPS = NT // G
        w = st.sb("w", [P, P])
        mean, var, sq = st.sb("mean", [P, G, H]), st.sb("var", [P, G, H]), st.sb("sq", [P, G * H, W])
        loaded, scaled = st.sem("loaded"), st.sem("scaled")
        step, root, added = st.counter("step"), st.counter("root"), st.counter("added")
        with nc.Block() as block:
            @block.sync
            def _(sp):
                sp.dma_start(w[:], d["l0_norm_w"]).then_inc(loaded, 16)

            @block.vector
            def _(dve):
                dve.wait_ge(loaded, 16)
                dve.tensor_scalar(w[:], w[:], m.tanh_g[:, 0:1], None, ALU.mult).then_inc(scaled, 1)
                dve.wait_ge(scaled, 1)
                with dve.Fori(0, STEPS) as it:
                    hs = m.h[:, bass.ds(it * G, G), :]
                    heads = hs.rearrange("p t (h w) -> p (t h) w", h=H)
                    flat = lambda x: x[:].rearrange("p t h -> p (t h)")
                    base = it * 7
                    dve.tensor_reduce(flat(mean), heads, AX, ALU.add).then_inc(step, 1)
                    dve.wait_ge(step, past(base + 1))
                    dve.tensor_scalar(flat(mean), flat(mean), 1.0 / W, None, ALU.mult).then_inc(step, 1)
                    dve.wait_ge(step, past(base + 2))
                    dve.tensor_tensor(heads, heads, spread_heads(flat(mean), W), ALU.subtract).then_inc(step, 1)
                    dve.wait_ge(step, past(base + 3))
                    dve.tensor_tensor(sq[:], heads, heads, ALU.mult).then_inc(step, 1)
                    dve.wait_ge(step, past(base + 4))
                    dve.tensor_reduce(flat(var), sq[:], AX, ALU.add).then_inc(step, 1)
                    dve.wait_ge(step, past(base + 5))
                    dve.tensor_scalar(flat(var), flat(var), 1.0 / W, 1e-5, ALU.mult, ALU.add).then_inc(step, 1)
                    dve.wait_ge(root, past(it + 1))
                    dve.reciprocal(flat(mean), flat(mean)).then_inc(step, 1)
                    dve.wait_ge(step, past(base + 7))
                    dve.tensor_tensor(heads, heads, spread_heads(flat(mean), W), ALU.mult).then_inc(added, 1)
                    dve.wait_ge(added, past(it * 3 + 1))
                    dve.tensor_tensor(hs, hs, repeat_heads(w[:], G), ALU.mult).then_inc(added, 1)
                    dve.wait_ge(added, past(it * 3 + 2))
                    xs = m.X[:, bass.ds(it * G, G), :]
                    dve.tensor_tensor(xs, xs, hs, ALU.add).then_inc(added, 1)
                    dve.wait_ge(added, past(it * 3 + 3))
                    for k in range(G):
                        dve.bn_stats(m.S6[:, it * G + k, :], m.X[:, it * G + k, :])

            @block.scalar
            def _(act):
                with act.Fori(0, STEPS) as it:
                    act.wait_ge(step, past(it * 7 + 6))
                    act.activation(mean[:], var[:], ACT.Sqrt).then_inc(root, 1)


def feature_major(nc, m, name, dst, router=None):
    with Stage(nc, name) as st:
        xn, xnT = st.two("xn", [P, P]), st.two("xnT", [P, P])
        normed_x, turned, copied, placed = (st.sem2(n) for n in ("normed_x", "turned", "copied", "placed"))
        routed, kept = st.sem2("routed"), st.sem2("kept")
        with nc.Block() as block:
            @block.vector
            def _(dve):
                with dve.Fori(0, PAIRS) as it:
                    for j in range(2):
                        dve.wait_ge(turned[j], past(it))
                        normed(dve, m, xn[j][:], it * 2 + j).then_inc(normed_x[j], 1)
                    if router:
                        for j in range(2):
                            dve.wait_ge(routed[j], past(it + 1))
                            dve.tensor_copy(router[1][:, it * 2 + j, :], m.B[j][:, 0:8]).then_inc(kept[j], 1)

            @block.tensor
            def _(pe):
                with pe.Fori(0, PAIRS) as it:
                    for j in range(2):
                        pe.wait_ge(normed_x[j], past(it + 1))
                        pe.wait_ge(copied[j], past(it))
                        pe.transpose(m.A[j][:, 0:P], xn[j][:], m.ident[:]).then_inc(turned[j], 1)
                    if router:
                        for j in range(2):
                            pe.wait_ge(copied[j], past(it + 1))
                            pe.wait_ge(kept[j], past(it))
                            pe.matmul(m.B[j][:, 0:8], xnT[j][:], router[0][:], start=True, stop=True)\
                              .then_inc(routed[j], 1)

            @block.scalar
            def _(act):
                with act.Fori(0, PAIRS) as it:
                    for j in range(2):
                        act.wait_ge(turned[j], past(it + 1))
                        act.wait_ge(placed[j], past(it))
                        if router:
                            act.wait_ge(routed[j], past(it))
                        act.copy(xnT[j][:], m.A[j][:, 0:P]).then_inc(copied[j], 1)

            @block.gpsimd
            def _(pool):
                with pool.Fori(0, PAIRS) as it:
                    for j in range(2):
                        pool.wait_ge(copied[j], past(it + 1))
                        pool.tensor_copy(dst[:, it * 2 + j, :], xnT[j][:]).then_inc(placed[j], 1)


def add_tiles(dve, m, added, count, it, first, y):
    xs = m.X[:, bass.ds(first, TPC), :]
    dve.tensor_tensor(xs, xs, y, ALU.add).then_inc(added, 1)
    dve.wait_ge(added, past(count))
    for k in range(TPC):
        last = dve.bn_stats(m.S6[:, first + k, :], m.X[:, first + k, :])
    return last


def l0_ffn(nc, m, d, own):
    F = 4
    xnT = own.enter_context(nc.sbuf_tensor("l0f_xnT", [P, NT, P], F32))
    feature_major(nc, m, "l0f_turn", xnT)
    with Stage(nc, "l0f") as st:
        w1, w2 = st.sb("w1", [P, F * P]), st.sb("w2", [P, F * P])
        h1, h2, w3 = st.sb("h1", [P, F, F * P]), st.sb("h2", [P, F, F * P]), st.sb("w3", [P, F, P])
        s = st.sb("s", [P, 4, F])
        s3 = st.sb("s3", [P, P])
        gate, hid, mid, y = (st.two(n, [P, F, CH]) for n in ("gate", "hid", "mid", "y"))
        loaded, scaled = st.sem("loaded"), st.sem("scaled")
        up, silued, hidden, sum1, act1, sum2, act2 = (
            st.sem2(n) for n in ("up", "silued", "hidden", "sum1", "act1", "sum2", "act2"))
        down, scaled_y, added = st.sem2("down"), st.sem2("scaled_y"), st.sem2("added")
        banks = [m.A[0][:, 0:CH], m.A[0][:, CH:2 * CH], m.B[0][:, 0:CH], m.B[0][:, CH:2 * CH]], \
                [m.A[1][:, 0:CH], m.A[1][:, CH:2 * CH], m.B[1][:, 0:CH], m.B[1][:, CH:2 * CH]]
        srcs = [(w1, "l0f_w1"), (w2, "l0f_w2"), (h1, "l0f_h1"), (h2, "l0f_h2"), (w3, "l0f_w3"), (s, "l0f_s"),
                (s3, "l0f_s3")]
        with nc.Block() as block:
            @block.sync
            def _(sp):
                for tile, src in srcs:
                    sp.dma_start(tile[:], d[src]).then_inc(loaded, 16)

            @block.tensor
            def _(pe):
                pe.wait_ge(loaded, 16 * len(srcs))
                with pe.Fori(0, NCH // 2) as it:
                    for j in range(2):
                        x = xnT[:, bass.ds(it * 8 + 4 * j, TPC), :]
                        for o in range(F):
                            if o == 0:
                                pe.wait_ge(scaled_y[j], past(it))
                            if o >= 2:
                                pe.wait_ge(hidden[j], past(it * 4 + o - 1))
                            c = slice(o * P, o * P + P)
                            pe.matmul(banks[j][2 * (o % 2)], w1[:, c], x, start=True, stop=True)
                            pe.matmul(banks[j][2 * (o % 2) + 1], w2[:, c], x, start=True, stop=True)\
                              .then_inc(up[j], 1)
                    for weights, src, ready, done in ((h1, hid, hidden, sum1), (h2, mid, act1, sum2)):
                        for j in range(2):
                            pe.wait_ge(ready[j], past(it * 4 + 4))
                            for o in range(F):
                                for k in range(F):
                                    last = pe.matmul(banks[j][o], weights[:, k, o * P:o * P + P], src[j][:, k],
                                                     start=(k == 0), stop=(k == F - 1))
                                last.then_inc(done[j], 1)
                    for j in range(2):
                        pe.wait_ge(act2[j], past(it * 4 + 4))
                        for t in range(TPC):
                            for k in range(F):
                                last = pe.matmul(banks[j][0][:, t * P:t * P + P], hid[j][:, k, t * P:t * P + P],
                                                 w3[:, k], start=(k == 0), stop=(k == F - 1))
                        last.then_inc(down[j], 1)

            @block.scalar
            def _(act):
                act.wait_ge(loaded, 16 * len(srcs))
                with act.Fori(0, NCH // 2) as it:
                    for j in range(2):
                        for o in range(F):
                            act.wait_ge(up[j], past(it * 4 + o + 1))
                            act.activation(gate[j][:, o], banks[j][2 * (o % 2)], ACT.Silu, scale=s[:, 0, o:o + 1])\
                               .then_inc(silued[j], 1)
                    for n, ready, dst, done in ((2, sum1, mid, act1), (3, sum2, hid, act2)):
                        for j in range(2):
                            for o in range(F):
                                act.wait_ge(ready[j], past(it * 4 + o + 1))
                                act.activation(dst[j][:, o], banks[j][o], ACT.Gelu, scale=s[:, n, o:o + 1])\
                                   .then_inc(done[j], 1)

            @block.vector
            def _(dve):
                dve.wait_ge(loaded, 16 * len(srcs))
                dve.tensor_scalar(s3[:], s3[:], m.tanh_g[:, 4:5], None, ALU.mult).then_inc(scaled, 1)
                dve.wait_ge(scaled, 1)
                with dve.Fori(0, NCH // 2) as it:
                    for j in range(2):
                        for o in range(F):
                            dve.wait_ge(silued[j], past(it * 4 + o + 1))
                            dve.scalar_tensor_tensor(hid[j][:, o], banks[j][2 * (o % 2) + 1], s[:, 1, o:o + 1],
                                                     gate[j][:, o], ALU.mult, ALU.mult).then_inc(hidden[j], 1)
                    for j in range(2):
                        dve.wait_ge(down[j], past(it + 1))
                        out = banks[j][0].rearrange("p (t w) -> p t w", t=TPC)
                        z = y[j][:, 0].rearrange("p (t w) -> p t w", t=TPC)
                        dve.tensor_tensor(z, out, repeat_heads(s3[:], TPC), ALU.mult).then_inc(scaled_y[j], 1)
                        dve.wait_ge(scaled_y[j], past(it + 1))
                        add_tiles(dve, m, added[j], it + 1, it, it * 8 + 4 * j, z)


def l2_ffn(nc, m, d, own):
    E = 8
    LOWER, UPPER, CENTER = 0.5 - float(np.log(4.0 / 3.0)), 0.5, 1.0 / float(np.e)
    xnT = own.enter_context(nc.sbuf_tensor("l2f_xnT", [P, NT, P], F32))
    wr = own.enter_context(nc.sbuf_tensor("l2f_wr", [P, E], F32))
    mix = own.enter_context(nc.sbuf_tensor("l2f_mix", [P, NT, E], F32))
    temp = own.enter_context(nc.sbuf_tensor("l2f_temp", [P, 1], F32))
    lower_e = own.enter_context(nc.sbuf_tensor("l2f_lower_e", [P, E, E], F32))
    with Stage(nc, "l2f_in") as st:
        loaded = st.sem("loaded")
        with nc.Block() as block:
            @block.sync
            def _(sp):
                for tile, src in ((wr, "l2f_wr"), (temp, "l2f_temp"), (lower_e, "c_lower_e")):
                    sp.dma_start(tile[:], d[src]).then_inc(loaded, 16)
                sp.wait_ge(loaded, 48)
    feature_major(nc, m, "l2f_turn", xnT, router=(wr, mix))

    with Stage(nc, "route") as st:
        inh, w, fb, mask, dist = (st.sb(n, [P, NT, E]) for n in ("inh", "w", "fb", "mask", "dist"))
        above, equal = st.sb("above", [P, NT, E, E]), st.sb("equal", [P, NT, E, E])
        total, none, some = st.sb("total", [P, NT]), st.sb("none", [P, NT]), st.sb("some", [P, NT])
        flat = lambda x: x[:].rearrange("p t e -> p (t e)")
        step, exped = st.sem("step"), st.sem("exped")
        with nc.Block() as block:
            @block.vector
            def _(dve):
                count = [0]

                def then(ins):
                    count[0] += 1
                    ins.then_inc(step, 1)
                    dve.wait_ge(step, count[0])

                then(dve.reciprocal(temp[:], temp[:]))
                then(dve.tensor_scalar(flat(mix), flat(mix), temp[:], None, ALU.mult))
                dve.wait_ge(exped, 1)
                then(dve.tensor_scalar(flat(inh), flat(inh), 1.0, None, ALU.add))
                then(dve.reciprocal(flat(inh), flat(inh)))
                then(dve.tensor_scalar(flat(mask), flat(inh), LOWER, None, ALU.is_ge))
                then(dve.scalar_tensor_tensor(flat(mask), flat(inh), UPPER, flat(mask), ALU.is_le, ALU.mult))
                then(dve.tensor_scalar(flat(inh), flat(inh), CENTER, None, ALU.subtract))
                then(dve.scalar_tensor_tensor(flat(dist), flat(inh), -1.0, flat(inh), ALU.mult, ALU.max))
                dve.wait_ge(exped, 3)
                then(dve.tensor_tensor(flat(w), flat(w), flat(mask), ALU.mult))
                then(dve.tensor_reduce(total[:], w[:], AX, ALU.add))
                then(dve.tensor_scalar(none[:], total[:], 1e-8, None, ALU.is_lt))
                then(dve.tensor_scalar(some[:], none[:], -1.0, 1.0, ALU.mult, ALU.add))
                mine = fb[:, :, :, None].broadcast_to([P, NT, E, E])
                theirs = fb[:, :, None, :].broadcast_to([P, NT, E, E])
                then(dve.tensor_tensor(above[:], theirs, mine, ALU.is_gt))
                then(dve.tensor_tensor(equal[:], theirs, mine, ALU.is_equal))
                then(dve.tensor_tensor(equal[:], equal[:], lower_e[:, None, :, :].broadcast_to([P, NT, E, E]), ALU.mult))
                then(dve.tensor_tensor(above[:], above[:], equal[:], ALU.add))
                then(dve.tensor_reduce(mask[:], above[:], AX, ALU.add))
                then(dve.scalar_tensor_tensor(flat(fb), flat(mask), 2.0, flat(fb), ALU.is_lt, ALU.mult))
                then(dve.tensor_reduce(total[:], fb[:], AX, ALU.add))
                then(dve.tensor_scalar(total[:], total[:], 1e-8, None, ALU.max))
                then(dve.reciprocal(total[:], total[:]))
                then(dve.tensor_tensor(total[:], total[:], none[:], ALU.mult))
                then(dve.tensor_tensor(fb[:], fb[:], spread_heads(total[:], E), ALU.mult))
                then(dve.tensor_tensor(w[:], w[:], spread_heads(some[:], E), ALU.mult))
                then(dve.tensor_tensor(flat(w), flat(w), flat(fb), ALU.add))
                then(dve.tensor_reduce(total[:], w[:], AX, ALU.add))
                then(dve.tensor_scalar(total[:], total[:], 1e-8, None, ALU.max))
                then(dve.reciprocal(total[:], total[:]))
                then(dve.tensor_scalar(total[:], total[:], m.tanh_g[:, 6:7], None, ALU.mult))
                dve.tensor_tensor(mix[:], w[:], spread_heads(total[:], E), ALU.mult)

            @block.scalar
            def _(act):
                act.wait_ge(step, 2)
                act.activation(inh[:], mix[:], ACT.Exp, scale=-1.0).then_inc(exped, 1)
                act.wait_ge(step, 8)
                act.activation(w[:], dist[:], ACT.Exp, scale=-10.0).then_inc(exped, 1)
                act.activation(fb[:], dist[:], ACT.Exp, scale=-1.0 / 0.3).then_inc(exped, 1)

    with Stage(nc, "l2f") as st:
        wg, wu, wd = (st.sb(n, [P, E, P]) for n in ("wg", "wu", "wd"))
        gate, hid = st.two("gate", [P, 2, CH]), st.two("hid", [P, 2, CH])
        loaded = st.sem("loaded")
        up, silued, hidden, down, added = (st.sem2(n) for n in ("up", "silued", "hidden", "down", "added"))
        stats = st.sem("stats")
        bank = lambda j, e, n: (m.A, m.B)[e % 2][j][:, n * CH:n * CH + CH]
        with nc.Block() as block:
            @block.sync
            def _(sp):
                for tile, src in ((wg, "l2f_wg"), (wu, "l2f_wu"), (wd, "l2f_wd")):
                    sp.dma_start(tile[:], d[src]).then_inc(loaded, 16)

            @block.tensor
            def _(pe):
                pe.wait_ge(loaded, 48)
                with pe.Fori(0, NCH // 2) as it:
                    for e in range(E + 1):
                        for j in range(2):
                            if e < E:
                                x = xnT[:, bass.ds(it * 8 + 4 * j, TPC), :]
                                if e == 0:
                                    pe.wait_ge(added[j], past(it * E * TPC))
                                if e >= 2:
                                    pe.wait_ge(added[j], past(it * E * TPC + (e - 1) * TPC))
                                pe.matmul(bank(j, e, 0), wg[:, e], x, start=True, stop=True)
                                pe.matmul(bank(j, e, 1), wu[:, e], x, start=True, stop=True).then_inc(up[j], 1)
                        for j in range(2):
                            if e >= 1:
                                f = e - 1
                                pe.wait_ge(hidden[j], past(it * E + f + 1))
                                for t in range(TPC):
                                    last = pe.matmul(bank(j, f, 0)[:, t * P:t * P + P],
                                                     hid[j][:, f % 2, t * P:t * P + P], wd[:, f],
                                                     start=True, stop=True)
                                last.then_inc(down[j], 1)

            @block.scalar
            def _(act):
                with act.Fori(0, NCH // 2) as it:
                    for e in range(E):
                        for j in range(2):
                            act.wait_ge(up[j], past(it * E + e + 1))
                            act.activation(gate[j][:, e % 2], bank(j, e, 0), ACT.Silu).then_inc(silued[j], 1)

            @block.vector
            def _(dve):
                with dve.Fori(0, NCH // 2) as it:
                    for e in range(E + 1):
                        for j in range(2):
                            if e < E:
                                dve.wait_ge(silued[j], past(it * E + e + 1))
                                dve.tensor_tensor(hid[j][:, e % 2], bank(j, e, 1), gate[j][:, e % 2], ALU.mult)\
                                   .then_inc(hidden[j], 1)
                        for j in range(2):
                            if e >= 1:
                                f = e - 1
                                dve.wait_ge(down[j], past(it * E + f + 1))
                                if f:
                                    dve.wait_ge(added[j], past(it * E * TPC + f * TPC))
                                for t in range(TPC):
                                    tile = it * 8 + 4 * j + t
                                    dve.scalar_tensor_tensor(
                                        m.X[:, tile, :], bank(j, f, 0)[:, t * P:t * P + P],
                                        mix[:, tile, f:f + 1], m.X[:, tile, :],
                                        ALU.mult, ALU.add).then_inc(added[j], 1)
                    for j in range(2):
                        dve.wait_ge(added[j], past(it * E * TPC + E * TPC))
                        for t in range(TPC):
                            tile = it * 8 + 4 * j + t
                            dve.bn_stats(m.S6[:, tile, :], m.X[:, tile, :])


def attention16(nc, m, d, name, projected, gate_at):
    H, W = 16, 8
    E = H // 2
    G = E // 2
    n_pair = 2 * (W + 1)
    with Stage(nc, name) as st:
        wo, bo = st.sb("wo", [P, P]), st.sb("bo", [1, P])
        loads = [(wo[:], d[f"{name}_wo"]), (bo[:], d[f"{name}_bo"])]
        if projected:
            wq, wk, wv = st.sb("wq", [P, P]), st.sb("wk", [P, P]), st.sb("wv", [P, P])
            bq, bk, bv = st.sb("bq", [P, 1]), st.sb("bk", [P, 1]), st.sb("bv", [P, P])
            rows = st.sb("rows", [P, NB], I32)
            scale = st.sb("scale", [P, NB])
            loads += [(x[:], d[f"{name}_{n}"]) for x, n in
                      ((wq, "wq"), (wk, "wk"), (wv, "wv"), (bq, "bq"), (bk, "bk"), (bv, "bv"))]
            loads += [(rows[u * S:u * S + S], d[f"{name}_mask"]) for u in range(2)]
            xnT, kT = st.two("xnT", [P, P]), st.two("kT", [P, P])
        else:
            raw = st.sb("raw", [P, NB, S], I32)
            masks = st.sb("masks", [P, NB, S], BF16)
            loads += [(raw[u * S:u * S + S], d[f"{name}_mask"]) for u in range(2)]
            ctx2 = st.two("ctx2", [P, 2, P])
        xn, ctxT = st.two("xn", [P, P]), st.two("ctxT", [P, P])
        qx = st.two("qx", [P, 2, 2, S])
        kx = st.two("kx", [P, 2, E, S])
        vd = st.two("vd", [P, 2, E, 2, W + 1])
        prob, pT = st.two("prob", [P, H, S]), st.two("pT", [P, 2 * G, P])
        top, inv = st.two("top", [P, H]), st.two("inv", [P, H])
        o, oT = st.two("o", [P, P]), st.two("oT", [P, P])
        loaded, masked, ones_set = st.sem("loaded"), st.sem("masked"), st.sem("ones_set")
        (ctx_in, ctx2_in, normed_x, turned, copied, proj, k_set, q_set, spread, values, scored, max_done, shifted,
         exped, p_turned, p_copied, mixed, inverted, o_done, o_turned, o_copied, out_done, added) = (
            st.sem2(n) for n in ("ctx_in", "ctx2_in", "normed_x", "turned", "copied", "proj", "k_set", "q_set",
                                 "spread", "values", "scored", "max_done", "shifted", "exped", "p_turned",
                                 "p_copied", "mixed", "inverted", "o_done", "o_turned", "o_copied", "out_done",
                                 "added"))
        A, G0, F = [x[:] for x in m.A], [x[:, 0:CH] for x in m.B], [x[:, CH:2 * CH] for x in m.B]
        k_in = kT if projected else ctxT
        n_masked = 5 if projected else 3
        with nc.Block() as block:
            @block.sync
            def _(sp):
                for tile, src in loads:
                    sp.dma_start(tile, src).then_inc(loaded, 16)
                with sp.Fori(0, PAIRS) as it:
                    for j in range(2):
                        sp.wait_ge((proj if projected else spread)[j], past(it))
                        sp.dma_start(ctxT[j][:], d["ctxT"][it * 2 + j]).then_inc(ctx_in[j], 16)
                        if not projected:
                            sp.wait_ge(values[j], past(it))
                            for u in range(2):
                                sp.dma_start(ctx2[j][u * S:u * S + S], d["ctx"][:, bass.ds(it * 4 + 2 * j, 2), :])\
                                  .then_inc(ctx2_in[j], 16)

            @block.gpsimd
            def _(pool):
                for j in range(2):
                    for b in range(2):
                        pool.tensor_copy(vd[j][:, b, :, :, W], repeat_heads(m.half[:], E)).then_inc(ones_set, 1)
                with pool.Fori(0, PAIRS) as it:
                    for j in range(2):
                        if projected:
                            pool.wait_ge(k_set[j], past(it + 1))
                        else:
                            pool.wait_ge(ctx_in[j], past(it * 16 + 16))
                        pool.wait_ge(scored[j], past(it))
                        for b in range(2):
                            last = pool.tensor_tensor(kx[j][:, b], repeat_heads(k_in[j][:, b * S:b * S + S], E),
                                                      spread_heads(m.head_of_8[:], S), ALU.mult)
                        last.then_inc(spread[j], 1)
                        if not projected:
                            pool.wait_ge(ctx2_in[j], past(it * 32 + 32))
                            pool.wait_ge(mixed[j], past(it))
                            for b in range(2):
                                last = pool.tensor_tensor(
                                    vd[j][:, b, :, :, 0:W], ctx2[j][:, b].rearrange("p (g u w) -> p g u w", g=E, u=2),
                                    m.half[:, None, :, None].broadcast_to([P, E, 2, W]), ALU.mult)
                            last.then_inc(values[j], 1)

            @block.vector
            def _(dve):
                def norm_x(it, j):
                    dve.wait_ge(turned[j], past(it))
                    normed(dve, m, xn[j][:], it * 2 + j).then_inc(normed_x[j], 1)

                def keep_v(it, j):
                    dve.wait_ge(q_set[j], past(it + 1))
                    dve.wait_ge(mixed[j], past(it))
                    v = F[j][:, 2 * P:4 * P].rearrange("p (b g u w) -> p b g u w", b=2, g=E, u=2)
                    b_v = bv[:].rearrange("p (g u w) -> p g u w", g=E, u=2)
                    for u in range(2):
                        r = slice(u * S, u * S + S)
                        last = dve.tensor_tensor(vd[j][r, :, :, u, 0:W], v[r, :, :, u],
                                                 b_v[r, None, :, u].broadcast_to([S, 2, E, W]), ALU.add)
                    last.then_inc(values[j], 1)

                def shift(it, j):
                    s = per_head(A[j], H, S)
                    dve.wait_ge(scored[j], past(it + 1))
                    dve.tensor_reduce(top[j][:], s, AX, ALU.max).then_inc(max_done[j], 1)
                    dve.wait_ge(max_done[j], past(it + 1))
                    dve.wait_ge(p_turned[j], past(it))
                    dve.tensor_tensor(prob[j][:], s, spread_heads(top[j][:], S), ALU.subtract)\
                       .then_inc(shifted[j], 1)

                def outputs(it, j):
                    out = G0[j][:, 0:H * (W + 1)].rearrange("p (h w) -> p h w", h=H)
                    dve.wait_ge(mixed[j], past(it + 1))
                    dve.reciprocal(inv[j][:], out[:, :, W]).then_inc(inverted[j], 1)
                    dve.wait_ge(inverted[j], past(it + 1))
                    dve.wait_ge(o_turned[j], past(it))
                    dve.tensor_tensor(per_head(o[j][:], H, W), out[:, :, 0:W], spread_heads(inv[j][:], W),
                                      ALU.mult).then_inc(o_done[j], 1)

                def update(it, j):
                    t = it * 2 + j
                    dve.wait_ge(out_done[j], past(it + 1))
                    dve.scalar_tensor_tensor(m.X[:, t, :], G0[j][:, P:2 * P],
                                             m.tanh_g[:, gate_at:gate_at + 1], m.X[:, t, :],
                                             ALU.mult, ALU.add).then_inc(added[j], 1)
                    dve.wait_ge(added[j], past(it + 1))
                    dve.bn_stats(m.S6[:, t, :], m.X[:, t, :])

                for j in range(2):
                    if projected:
                        dve.memset(vd[j][:, :, :, :, 0:W], 0.0).then_inc(masked, 1)
                    dve.memset(qx[j][:], 0.0).then_inc(masked, 1)
                dve.wait_ge(loaded, 16 * len(loads))
                if projected:
                    dve.tensor_scalar(scale[:], rows[:], 0, float(W) ** -0.5, ALU.not_equal, ALU.mult)\
                       .then_inc(masked, 1)
                else:
                    dve.tensor_scalar(masks[:], raw[:], 0, -1e20, ALU.is_equal, ALU.mult).then_inc(masked, 1)
                dve.wait_ge(masked, n_masked)
                dve.wait_ge(ones_set, 4)

                def step(it, j):
                    at(it, j, 0, shift)
                    at(it, j, -2, update)
                    at(it, j, -1, outputs)
                    at(it, j, 2, norm_x)
                    if projected:
                        at(it, j, 1, keep_v)

                steps(dve, step)

            @block.scalar
            def _(act):
                def keep_q(j, convert):
                    for u in range(2):
                        r = slice(u * S, u * S + S)
                        last = convert(qx[j][r, :, u], F[j][r, 0:P].rearrange("p (b q) -> p b q", b=2), u)
                    return last

                def copy_x(it, j):
                    act.wait_ge(turned[j], past(it + 1))
                    if projected:
                        act.wait_ge(proj[j], past(it))
                        act.copy(xnT[j][:], F[j][:, 0:P]).then_inc(copied[j], 1)
                    else:
                        act.wait_ge(scored[j], past(it))
                        keep_q(j, lambda dst, src, u: act.copy(dst, src)).then_inc(q_set[j], 1)

                def set_k(it, j):
                    act.wait_ge(turned[j], past(it + 1))
                    act.wait_ge(spread[j], past(it))
                    act.activation(kT[j][:], F[j][:, P:2 * P], ACT.Identity, bias=bk[:]).then_inc(k_set[j], 1)

                def set_q(it, j):
                    act.wait_ge(proj[j], past(it + 1))
                    act.wait_ge(scored[j], past(it))
                    keep_q(j, lambda dst, src, u: act.activation(dst, src, ACT.Identity, bias=bq[u * S:u * S + S]))\
                        .then_inc(q_set[j], 1)

                def exps(it, j):
                    act.wait_ge(shifted[j], past(it + 1))
                    if projected:
                        for b in range(2):
                            p = prob[j][:, b * E:b * E + E]
                            last = act.activation(p, p, ACT.Exp, scale=scale[:, bass.ds(it * 4 + 2 * j + b, 1)])
                    else:
                        last = act.activation(prob[j][:], prob[j][:], ACT.Exp, scale=float(P) ** -0.5)
                    last.then_inc(exped[j], 1)

                def copy_p(it, j):
                    act.wait_ge(p_turned[j], past(it + 1))
                    act.wait_ge(mixed[j], past(it))
                    act.copy(pT[j][:], A[j].rearrange("p (g q) -> p g q", g=2 * G)).then_inc(p_copied[j], 1)

                def copy_o(it, j):
                    act.wait_ge(o_turned[j], past(it + 1))
                    act.wait_ge(out_done[j], past(it))
                    act.copy(oT[j][:], G0[j][:, 0:P]).then_inc(o_copied[j], 1)

                act.wait_ge(loaded, 16 * len(loads))
                act.wait_ge(masked, n_masked)

                def step(it, j):
                    at(it, j, -2, copy_o)
                    at(it, j, -1, copy_p)
                    at(it, j, 1, copy_x)
                    if projected:
                        at(it, j, 1, set_k)
                    at(it, j, 0, exps)
                    if projected:
                        at(it, j, 1, set_q)

                steps(act, step)

            @block.tensor
            def _(pe):
                def turn_x(it, j):
                    pe.wait_ge(normed_x[j], past(it + 1))
                    if projected:
                        pe.wait_ge(values[j], past(it))
                        pe.wait_ge(ctx_in[j], past(it * 16 + 16))
                        pe.matmul(F[j][:, P:2 * P], wk[:], ctxT[j][:], start=True, stop=True)
                        for b in range(2):
                            for u in range(2):
                                pe.matmul(F[j][u * S:u * S + S, (2 + b) * P:(3 + b) * P],
                                          ctxT[j][:, b * S:b * S + S], wv[:], start=True, stop=True)
                    else:
                        pe.wait_ge(q_set[j], past(it))
                    pe.transpose(F[j][:, 0:P], xn[j][:], m.ident[:]).then_inc(turned[j], 1)

                def project_q(it, j):
                    pe.wait_ge(copied[j], past(it + 1))
                    pe.wait_ge(k_set[j], past(it + 1))
                    pe.matmul(F[j][:, 0:P], wq[:], xnT[j][:], start=True, stop=True).then_inc(proj[j], 1)

                def scores(it, j):
                    pe.wait_ge(p_copied[j], past(it))
                    pe.wait_ge(spread[j], past(it + 1))
                    pe.wait_ge(q_set[j], past(it + 1))
                    for b in range(2):
                        s = A[j][:, b * CH:b * CH + CH]
                        if not projected:
                            pe.matmul(s, m.ident_bf[:], repeat_heads(masks[:, it * 4 + 2 * j + b, :], E),
                                      start=True, stop=False)
                        last = pe.matmul(s, qx[j][:, b].rearrange("p u q -> p (u q)"), kx[j][:, b],
                                         start=projected, stop=True)
                    last.then_inc(scored[j], 1)

                def turn_p(it, j):
                    pe.wait_ge(exped[j], past(it + 1))
                    p = prob[j][:].rearrange("p h k -> p (h k)")
                    for g in range(2 * G):
                        last = pe.transpose(A[j][:, g * P:g * P + P], p[:, g * P:g * P + P], m.ident[:])
                    last.then_inc(p_turned[j], 1)

                def mix(it, j):
                    pe.wait_ge(p_copied[j], past(it + 1))
                    pe.wait_ge(values[j], past(it + 1))
                    pe.wait_ge(added[j], past(it))
                    for b in range(2):
                        for u in range(2):
                            for g in range(G):
                                pair = u * G + g
                                last = pe.matmul(G0[j][b * S:b * S + S, pair * n_pair:(pair + 1) * n_pair],
                                                 pT[j][:, b * G + g, u * S:u * S + S],
                                                 vd[j][:, b, pair].rearrange("p u w -> p (u w)"),
                                                 start=True, stop=True)
                    last.then_inc(mixed[j], 1)

                def turn_o(it, j):
                    pe.wait_ge(o_done[j], past(it + 1))
                    pe.transpose(G0[j][:, 0:P], o[j][:], m.ident[:]).then_inc(o_turned[j], 1)

                def project_o(it, j):
                    pe.wait_ge(o_copied[j], past(it + 1))
                    y = G0[j][:, P:2 * P]
                    pe.matmul(y, m.ones_row[:], bo[:], start=True, stop=False)
                    pe.matmul(y, oT[j][:], wo[:], start=False, stop=True).then_inc(out_done[j], 1)

                pe.wait_ge(loaded, 16 * len(loads))
                pe.wait_ge(masked, n_masked)
                pe.wait_ge(ones_set, 4)

                def step(it, j):
                    at(it, j, 0, scores)
                    at(it, j, -2, turn_o)
                    at(it, j, -1, turn_p)
                    at(it, j, 1, turn_x)
                    at(it, j, -2, project_o)
                    at(it, j, -1, mix)
                    if projected:
                        at(it, j, 1, project_q)

                steps(pe, step)


def l1_xattn(nc, m, d, own):
    attention16(nc, m, d, "l1x", True, 1)


def l2_xattn(nc, m, d, own):
    attention16(nc, m, d, "l2x", False, 2)


def l3_xattn(nc, m, d, own):
    with Stage(nc, "l3x") as st:
        wq, wk, bq, bk = st.sb("wq", [P, P]), st.sb("wk", [P, P]), st.sb("bq", [P, 1]), st.sb("bk", [P, 1])
        raw = st.sb("raw", [P, NT, S], I32)
        factor, extra = st.sb("factor", [P, NT, S]), st.sb("extra", [P, NT, S])
        loads = [(wq, "l3x_wq"), (wk, "l3x_wk"), (bq, "l3x_bq"), (bk, "l3x_bk"), (raw, "l3x_mask")]
        xn, xnT, qT, kT = (st.two(n, [P, P]) for n in ("xn", "xnT", "qT", "kT"))
        ctxT = st.sb("ctxT", [P, NT, P])
        val = st.sb("val", [P, NT, P])
        score = st.two("score", [P, S])
        prob, pT = st.two("prob", [P, P]), st.two("pT", [P, P])
        top, total, inv = (st.two(n, [P, 1]) for n in ("top", "total", "inv"))
        loaded, masked, zeroed = st.sem("loaded"), st.sem("masked"), st.sem("zeroed")
        arrived = st.counter("arrived")
        (ctx_in, normed_x, turned, copied, proj, q_set, scored, times, plus, max_done, exped,
         p_turned, p_copied, mixed, inverted, gated, added) = (
            st.sem2(n) for n in ("ctx_in", "normed_x", "turned", "copied", "proj", "q_set", "scored",
                                 "times", "plus", "max_done", "exped", "p_turned", "p_copied", "mixed",
                                 "inverted", "gated", "added"))
        with nc.Block() as block:
            @block.sync
            def _(sp):
                for tile, src in loads:
                    sp.dma_start(tile[:], d[src]).then_inc(loaded, 16)
                parts = 8
                tiles = NT // parts
                with sp.Fori(0, parts) as part:
                    sp.dma_start(ctxT[:, bass.ds(part * tiles, tiles), :],
                                 d["ctxT"][bass.ds(part * tiles, tiles)].rearrange("t p k -> p t k"))\
                      .then_inc(arrived, 16)
                    sp.dma_start(val[:, bass.ds(part * tiles, tiles), :],
                                 d["ctx_rows"][:, bass.ds(part * tiles, tiles), :]).then_inc(arrived, 16)
                    sp.wait_ge(arrived, past(part * 32 + 32))
                    for j in range(2):
                        sp.sem_inc(ctx_in[j], tiles // 2)

            @block.vector
            def _(dve):
                def norm_x(it, j):
                    dve.wait_ge(turned[j], past(it))
                    normed(dve, m, xn[j][:], it * 2 + j).then_inc(normed_x[j], 1)

                def weigh(it, j):
                    t = it * 2 + j
                    dve.wait_ge(scored[j], past(it + 1))
                    dve.wait_ge(exped[j], past(it))
                    dve.tensor_tensor(score[j][:], m.B[j][:, 0:S], factor[:, t, :], ALU.mult).then_inc(times[j], 1)
                    dve.wait_ge(times[j], past(it + 1))
                    dve.tensor_tensor(score[j][:], score[j][:], extra[:, t, :], ALU.add).then_inc(plus[j], 1)
                    dve.wait_ge(plus[j], past(it + 1))
                    dve.tensor_reduce(top[j][:], score[j][:], AX, ALU.max, negate=True).then_inc(max_done[j], 1)

                def invert(it, j):
                    dve.wait_ge(exped[j], past(it + 1))
                    dve.reciprocal(inv[j][:], total[j][:]).then_inc(inverted[j], 1)
                    dve.wait_ge(inverted[j], past(it + 1))
                    dve.tensor_scalar(inv[j][:], inv[j][:], m.tanh_g[:, 3:4], None, ALU.mult).then_inc(gated[j], 1)

                def update(it, j):
                    t = it * 2 + j
                    dve.wait_ge(gated[j], past(it + 1))
                    dve.wait_ge(mixed[j], past(it + 1))
                    dve.scalar_tensor_tensor(m.X[:, t, :], m.B[j][:, 2 * P:3 * P], inv[j][:], m.X[:, t, :],
                                             ALU.mult, ALU.add).then_inc(added[j], 1)

                def measure(it, j):
                    dve.wait_ge(added[j], past(it + 1))
                    dve.bn_stats(m.S6[:, it * 2 + j, :], m.X[:, it * 2 + j, :])

                for j in range(2):
                    dve.memset(prob[j][:], 0.0).then_inc(zeroed, 1)
                dve.wait_ge(loaded, 16 * len(loads))
                dve.tensor_scalar(factor[:], raw[:], float(P) ** -0.5, None, ALU.mult)
                dve.tensor_scalar(extra[:], raw[:], 0, -1e9, ALU.is_equal, ALU.mult).then_inc(masked, 1)
                dve.wait_ge(masked, 1)

                def step(it, j):
                    at(it, j, 2, norm_x)
                    at(it, j, -2, update)
                    at(it, j, 0, weigh)
                    at(it, j, -2, measure)
                    at(it, j, -1, invert)

                steps(dve, step)

            @block.scalar
            def _(act):
                def copy_x(it, j):
                    act.wait_ge(turned[j], past(it + 1))
                    act.wait_ge(proj[j], past(it))
                    act.copy(xnT[j][:], m.A[j][:, 0:P]).then_inc(copied[j], 1)

                def set_qk(it, j):
                    act.wait_ge(proj[j], past(it + 1))
                    act.wait_ge(scored[j], past(it))
                    act.activation(kT[j][:], m.A[j][:, P:2 * P], ACT.Identity, bias=bk[:])
                    act.activation(qT[j][:], m.A[j][:, 2 * P:3 * P], ACT.Identity, bias=bq[:]).then_inc(q_set[j], 1)

                def exps(it, j):
                    act.wait_ge(max_done[j], past(it + 1))
                    act.wait_ge(inverted[j], past(it))
                    act.wait_ge(p_turned[j], past(it))
                    for b in range(2):
                        r = slice(b * S, b * S + S)
                        last = act.activation(prob[j][r, r], score[j][r], ACT.Exp, bias=top[j][r],
                                              accum_out=total[j][r])
                    last.then_inc(exped[j], 1)

                def copy_p(it, j):
                    act.wait_ge(p_turned[j], past(it + 1))
                    act.wait_ge(mixed[j], past(it))
                    act.copy(pT[j][:], m.B[j][:, CH:CH + P]).then_inc(p_copied[j], 1)

                act.wait_ge(loaded, 16 * len(loads))
                act.wait_ge(zeroed, 2)

                def step(it, j):
                    at(it, j, -1, copy_p)
                    at(it, j, 2, copy_x)
                    at(it, j, 1, set_qk)
                    at(it, j, 0, exps)

                steps(act, step)

            @block.tensor
            def _(pe):
                def turn_x(it, j):
                    pe.wait_ge(normed_x[j], past(it + 1))
                    pe.wait_ge(q_set[j], past(it))
                    pe.transpose(m.A[j][:, 0:P], xn[j][:], m.ident[:]).then_inc(turned[j], 1)

                def project(it, j):
                    pe.wait_ge(ctx_in[j], past(it + 1))
                    pe.wait_ge(copied[j], past(it + 1))
                    pe.matmul(m.A[j][:, P:2 * P], wk[:], ctxT[:, it * 2 + j, :], start=True, stop=True)
                    pe.matmul(m.A[j][:, 2 * P:3 * P], wq[:], xnT[j][:], start=True, stop=True).then_inc(proj[j], 1)

                def scores(it, j):
                    pe.wait_ge(q_set[j], past(it + 1))
                    pe.wait_ge(added[j], past(it))
                    for b in range(2):
                        last = pe.matmul(m.B[j][b * S:b * S + S, 0:S], qT[j][:, b * S:b * S + S],
                                         kT[j][:, b * S:b * S + S], start=True, stop=True)
                    last.then_inc(scored[j], 1)

                def turn_p(it, j):
                    pe.wait_ge(exped[j], past(it + 1))
                    pe.transpose(m.B[j][:, CH:CH + P], prob[j][:], m.ident[:]).then_inc(p_turned[j], 1)

                def mix(it, j):
                    pe.wait_ge(p_copied[j], past(it + 1))
                    pe.matmul(m.B[j][:, 2 * P:3 * P], pT[j][:], val[:, it * 2 + j, :], start=True, stop=True)\
                      .then_inc(mixed[j], 1)

                pe.wait_ge(loaded, 16 * len(loads))
                pe.wait_ge(zeroed, 2)

                def step(it, j):
                    at(it, j, 0, scores)
                    at(it, j, -1, turn_p)
                    at(it, j, 2, turn_x)
                    at(it, j, 1, project)
                    at(it, j, -1, mix)

                steps(pe, step)


def quantizer(nc, m, name, maxima, scale, inverse):
    with Stage(nc, name) as st:
        own, all_ = st.sb("own", [P, 1]), st.sb("all", [P, 1])
        own_max, all_max, step = st.sem("own_max"), st.sem("all_max"), st.sem("step")
        with nc.Block() as block:
            @block.vector
            def _(dve):
                dve.tensor_reduce(own[:], maxima, AX, ALU.max).then_inc(own_max, 1)
                dve.wait_ge(all_max, 1)
                dve.tensor_scalar(scale, all_[:], 1.0 / 32767.0, 1e-12, ALU.mult, ALU.max).then_inc(step, 1)
                dve.wait_ge(step, 1)
                dve.reciprocal(inverse, scale)

            @block.gpsimd
            def _(pool):
                pool.wait_ge(own_max, 1)
                pool.partition_all_reduce(all_[:], own[:], P, bass.bass_isa.ReduceOp.max).then_inc(all_max, 1)


def l1_ffn(nc, m, d, own):
    F = 3
    BLOCK = 32
    NBL = 3 * F * P // BLOCK
    sb = lambda n, s, dt=F32: own.enter_context(nc.sbuf_tensor("l1f_" + n, s, dt))
    wT = sb("wT", [P, 3 * F, P])
    xT = sb("xT", [P, NT, P])
    upq, gateq = sb("upq", [P, F, NT * P], I16), sb("gateq", [P, F, NT * P], I16)
    maxima = sb("maxima", [P, 2, NCH * F])
    sc = sb("sc", [P, 16])
    rnd = sb("rnd", [P, 1])
    col = lambda n: sc[:, n:n + 1]
    X_S, X_R, U_S, U_R, G_S, G_R, H_S, H_R, O_S, O_R, TMP, GH_R, O_F, GATE, O_U = range(15)
    banks = [[r[j][:, h * CH:h * CH + CH] for r in (m.A, m.B) for h in range(2)] for j in range(2)]

    with Stage(nc, "l1f_w") as st:
        w, q = st.sb("w", [P, 3 * F * P]), st.sb("q", [P, 3 * F * P])
        big, inv = st.sb("big", [P, NBL]), st.sb("inv", [P, NBL])
        loaded, step, turned, ready = st.sem("loaded"), st.sem("step"), st.sem("turned"), st.sem("ready")
        with nc.Block() as block:
            @block.sync
            def _(sp):
                sp.dma_start(w[:], d["l1f_w"]).then_inc(loaded, 16)

            @block.vector
            def _(dve):
                blocks = lambda x: x[:].rearrange("p (n k) -> p n k", k=BLOCK)
                count = [0]

                def then(ins):
                    count[0] += 1
                    ins.then_inc(step, 1)
                    dve.wait_ge(step, count[0])

                then(dve.memset(rnd[:], ROUND))
                dve.wait_ge(loaded, 16)
                then(dve.tensor_reduce(big[:], blocks(w), AX, ALU.max, apply_absolute_value=True))
                then(dve.tensor_scalar(big[:], big[:], 1.0 / 7.0, 1e-12, ALU.mult, ALU.max))
                then(dve.reciprocal(inv[:], big[:]))
                then(dve.tensor_tensor(blocks(q), blocks(w), spread_heads(inv[:], BLOCK), ALU.mult))
                then(dve.tensor_scalar(q[:], q[:], 7.0, -8.0, ALU.min, ALU.max))
                then(dve.tensor_scalar(q[:], q[:], ROUND, None, ALU.add))
                then(dve.tensor_scalar(q[:], q[:], -ROUND, None, ALU.add))
                dve.tensor_tensor(blocks(q), blocks(q), spread_heads(big[:], BLOCK), ALU.mult).then_inc(ready, 1)
                dve.wait_ge(turned, 1)
                for n in range(3 * F):
                    dve.tensor_copy(wT[:, n], banks[n % 2][n // 2 % 4][:, n // 8 * P:n // 8 * P + P])

            @block.tensor
            def _(pe):
                pe.wait_ge(ready, 1)
                for n in range(3 * F):
                    last = pe.transpose(banks[n % 2][n // 2 % 4][:, n // 8 * P:n // 8 * P + P],
                                        q[:, n * P:n * P + P], m.ident[:])
                last.then_inc(turned, 1)

    with Stage(nc, "l1f_xmax") as st:
        xn = st.two("xn", [P, P])
        normed_x, found = st.sem2("normed_x"), st.sem2("found")
        xmax = st.sb("xmax", [P, NT])
        with nc.Block() as block:
            @block.vector
            def _(dve):
                with dve.Fori(0, PAIRS) as it:
                    for j in range(2):
                        dve.wait_ge(found[j], past(it))
                        normed(dve, m, xn[j][:], it * 2 + j).then_inc(normed_x[j], 1)
                    for j in range(2):
                        dve.wait_ge(normed_x[j], past(it + 1))
                        dve.tensor_reduce(xmax[:, bass.ds(it * 2 + j, 1)], xn[j][:], AX, ALU.max,
                                          apply_absolute_value=True).then_inc(found[j], 1)
        quantizer(nc, m, "l1f_xs", xmax[:], col(X_S), col(X_R))

    with Stage(nc, "l1f_x") as st:
        xn, xr = st.two("xn", [P, P]), st.two("xr", [P, P])
        normed_x, rounded, quantized, turned, copied = (
            st.sem2(n) for n in ("normed_x", "rounded", "quantized", "turned", "copied"))
        with nc.Block() as block:
            @block.vector
            def _(dve):
                with dve.Fori(0, PAIRS) as it:
                    for j in range(2):
                        dve.wait_ge(rounded[j], past(it))
                        normed(dve, m, xn[j][:], it * 2 + j).then_inc(normed_x[j], 1)
                    for j in range(2):
                        dve.wait_ge(normed_x[j], past(it + 1))
                        dve.wait_ge(turned[j], past(it))
                        dve.tensor_scalar(xr[j][:], xn[j][:], col(X_R), ROUND, ALU.mult, ALU.add).then_inc(rounded[j], 1)
                    for j in range(2):
                        dve.wait_ge(rounded[j], past(it + 1))
                        dve.tensor_scalar(xr[j][:], xr[j][:], -ROUND, col(X_S), ALU.add, ALU.mult)\
                           .then_inc(quantized[j], 1)

            @block.tensor
            def _(pe):
                with pe.Fori(0, PAIRS) as it:
                    for j in range(2):
                        pe.wait_ge(quantized[j], past(it + 1))
                        pe.wait_ge(copied[j], past(it))
                        pe.transpose(m.A[j][:, 0:P], xr[j][:], m.ident[:]).then_inc(turned[j], 1)

            @block.scalar
            def _(act):
                with act.Fori(0, PAIRS) as it:
                    for j in range(2):
                        act.wait_ge(turned[j], past(it + 1))
                        act.copy(xT[:, it * 2 + j, :], m.A[j][:, 0:P]).then_inc(copied[j], 1)

    with Stage(nc, "l1f_ugmax") as st:
        made, seen = st.sem2("made"), st.sem2("seen")
        with nc.Block() as block:
            @block.tensor
            def _(pe):
                with pe.Fori(0, NCH) as it:
                    x = xT[:, bass.ds(it * TPC, TPC), :]
                    for o in range(F):
                        for n in range(2):
                            pe.wait_ge(seen[n], past(it * F))
                            pe.matmul(banks[n][o], wT[:, n * F + o], x, start=True, stop=True).then_inc(made[n], 1)

            @block.vector
            def _(dve):
                with dve.Fori(0, NCH) as it:
                    for o in range(F):
                        for n in range(2):
                            dve.wait_ge(made[n], past(it * F + o + 1))
                            dve.tensor_reduce(maxima[:, n, bass.ds(it * F + o, 1)], banks[n][o], AX, ALU.max,
                                              apply_absolute_value=True).then_inc(seen[n], 1)
    quantizer(nc, m, "l1f_us", maxima[:, 0], col(U_S), col(U_R))
    quantizer(nc, m, "l1f_gs", maxima[:, 1], col(G_S), col(G_R))

    def tokens(t, o, it):
        return t[:, o, bass.ds(it * CH, CH)]

    with Stage(nc, "l1f_ug") as st:
        ur, gr, sig, h = (st.sb(n, [P, F, CH]) for n in ("ur", "gr", "sig", "h"))
        made, up_rounded, gate_rounded, up_kept, gate_kept, siged, clipped, rounded, times, seen = (
            st.counter(n) for n in ("made", "up_rounded", "gate_rounded", "up_kept", "gate_kept", "siged", "clipped",
                                "rounded", "times", "seen"))
        with nc.Block() as block:
            @block.tensor
            def _(pe):
                with pe.Fori(0, NCH) as it:
                    x = xT[:, bass.ds(it * TPC, TPC), :]
                    for o in range(F):
                        pe.wait_ge(gate_rounded, past(it * F))
                        pe.matmul(banks[0][o], wT[:, o], x, start=True, stop=True)
                        pe.matmul(banks[1][o], wT[:, F + o], x, start=True, stop=True).then_inc(made, 1)

            @block.scalar
            def _(act):
                with act.Fori(0, NCH) as it:
                    for o in range(F):
                        n = it * F + o + 1
                        act.wait_ge(made, past(n))
                        act.wait_ge(up_kept, past(it * F))
                        act.activation(ur[:, o], banks[0][o], ACT.Identity, scale=col(U_R), bias=rnd[:])\
                           .then_inc(up_rounded, 1)
                        act.wait_ge(gate_kept, past(it * F))
                        act.activation(gr[:, o], banks[1][o], ACT.Identity, scale=col(G_R), bias=rnd[:])\
                           .then_inc(gate_rounded, 1)
                    for o in range(F):
                        act.wait_ge(gate_kept, past(it * F + o + 1))
                        act.wait_ge(times, past(it * F))
                        act.activation(sig[:, o], tokens(gateq, o, it), ACT.Sigmoid, scale=col(G_S)).then_inc(siged, 1)

            @block.vector
            def _(dve):
                with dve.Fori(0, NCH) as it:
                    for o in range(F):
                        n = it * F + o + 1
                        dve.wait_ge(gate_rounded, past(n))
                        dve.tensor_scalar(tokens(gateq, o, it), gr[:, o], -ROUND, 32767.0, ALU.add, ALU.min)\
                           .then_inc(gate_kept, 1)
                        dve.wait_ge(up_rounded, past(n))
                        dve.tensor_scalar(tokens(upq, o, it), ur[:, o], -ROUND, 32767.0, ALU.add, ALU.min)\
                           .then_inc(up_kept, 1)
                    for o in range(F):
                        dve.wait_ge(siged, past(it * F + o + 1))
                        dve.tensor_scalar(sig[:, o], sig[:, o], 65536.0, 65535.0, ALU.mult, ALU.min).then_inc(clipped, 1)
                    for o in range(F):
                        dve.wait_ge(clipped, past(it * F + o + 1))
                        dve.tensor_scalar(sig[:, o], sig[:, o], 0.0, ROUND, ALU.max, ALU.add).then_inc(rounded, 1)
                    for o in range(F):
                        n = it * F + o + 1
                        dve.wait_ge(rounded, past(n))
                        dve.scalar_tensor_tensor(h[:, o], sig[:, o], -ROUND, tokens(gateq, o, it), ALU.add, ALU.mult)\
                           .then_inc(times, 1)
                    for o in range(F):
                        dve.wait_ge(times, past(it * F + o + 1))
                        dve.tensor_reduce(maxima[:, 0, bass.ds(it * F + o, 1)], h[:, o], AX, ALU.max,
                                          apply_absolute_value=True).then_inc(seen, 1)

    def small(name, *ops):
        with Stage(nc, name) as st:
            step = st.sem("step")
            with nc.Block() as block:
                @block.vector
                def _(dve):
                    for n, op in enumerate(ops):
                        op(dve).then_inc(step, 1)
                        dve.wait_ge(step, n + 1)

    small("l1f_hunit",
          lambda dve: dve.tensor_scalar(col(TMP), col(G_S), 1.0 / 65536.0, None, ALU.mult),
          lambda dve: dve.tensor_scalar(maxima[:, 0], maxima[:, 0], col(TMP), None, ALU.mult))
    quantizer(nc, m, "l1f_hs", maxima[:, 0], col(H_S), col(H_R))
    small("l1f_hfactor",
          lambda dve: dve.tensor_scalar(col(GH_R), col(TMP), col(H_R), None, ALU.mult),
          lambda dve: dve.tensor_scalar(col(O_U), col(H_S), col(U_S), None, ALU.mult))

    with Stage(nc, "l1f_h") as st:
        sig, h, hr = (st.sb(n, [P, F, CH]) for n in ("sig", "h", "hr"))
        siged, clipped, rounded, times, h_rounded, kept, product, seen = (
            st.counter(n) for n in ("siged", "clipped", "rounded", "times", "h_rounded", "kept", "product", "seen"))
        with nc.Block() as block:
            @block.scalar
            def _(act):
                with act.Fori(0, NCH) as it:
                    for o in range(F):
                        act.wait_ge(times, past(it * F))
                        act.activation(sig[:, o], tokens(gateq, o, it), ACT.Sigmoid, scale=col(G_S)).then_inc(siged, 1)
                    for o in range(F):
                        act.wait_ge(times, past(it * F + o + 1))
                        act.wait_ge(product, past(it * F))
                        act.activation(hr[:, o], h[:, o], ACT.Identity, scale=col(GH_R), bias=rnd[:])\
                           .then_inc(h_rounded, 1)

            @block.vector
            def _(dve):
                with dve.Fori(0, NCH) as it:
                    for o in range(F):
                        dve.wait_ge(siged, past(it * F + o + 1))
                        dve.tensor_scalar(sig[:, o], sig[:, o], 65536.0, 65535.0, ALU.mult, ALU.min).then_inc(clipped, 1)
                    for o in range(F):
                        dve.wait_ge(clipped, past(it * F + o + 1))
                        dve.tensor_scalar(sig[:, o], sig[:, o], 0.0, ROUND, ALU.max, ALU.add).then_inc(rounded, 1)
                    for o in range(F):
                        dve.wait_ge(rounded, past(it * F + o + 1))
                        dve.wait_ge(seen, past(it * F))
                        dve.scalar_tensor_tensor(h[:, o], sig[:, o], -ROUND, tokens(gateq, o, it), ALU.add, ALU.mult)\
                           .then_inc(times, 1)
                    for o in range(F):
                        n = it * F + o + 1
                        dve.wait_ge(h_rounded, past(n))
                        dve.tensor_scalar(tokens(gateq, o, it), hr[:, o], -ROUND, 32767.0, ALU.add, ALU.min)\
                           .then_inc(kept, 1)
                        dve.scalar_tensor_tensor(h[:, o], hr[:, o], -ROUND, tokens(upq, o, it), ALU.add, ALU.mult)\
                           .then_inc(product, 1)
                    for o in range(F):
                        dve.wait_ge(product, past(it * F + o + 1))
                        dve.tensor_reduce(maxima[:, 0, bass.ds(it * F + o, 1)], h[:, o], AX, ALU.max,
                                          apply_absolute_value=True).then_inc(seen, 1)

    small("l1f_ounit", lambda dve: dve.tensor_scalar(maxima[:, 0], maxima[:, 0], col(O_U), None, ALU.mult))
    quantizer(nc, m, "l1f_os", maxima[:, 0], col(O_S), col(O_R))
    small("l1f_ofactor", lambda dve: dve.tensor_scalar(col(O_F), col(O_U), col(O_R), None, ALU.mult))

    with Stage(nc, "l1f_down") as st:
        prod, oq, y = st.two("prod", [P, F, CH]), st.two("oq", [P, F, CH]), st.two("y", [P, CH])
        multiplied, rounded, quantized, down, scaled, added, used = (
            st.sem2(n) for n in ("multiplied", "rounded", "quantized", "down", "scaled", "added", "used"))
        with nc.Block() as block:
            @block.vector
            def _(dve):
                with dve.Fori(0, NCH // 2) as it:
                    for j in range(2):
                        c = it * 2 + j
                        dve.wait_ge(rounded[j], past(it * F))
                        for o in range(F):
                            dve.tensor_tensor(prod[j][:, o], tokens(gateq, o, c), tokens(upq, o, c), ALU.mult)\
                               .then_inc(multiplied[j], 1)
                    for j in range(2):
                        for o in range(F):
                            dve.wait_ge(rounded[j], past(it * F + o + 1))
                            dve.tensor_scalar(oq[j][:, o], oq[j][:, o], -ROUND, col(O_S), ALU.add, ALU.mult)\
                               .then_inc(quantized[j], 1)
                    for j in range(2):
                        dve.wait_ge(down[j], past(it + 1))
                        dve.tensor_scalar(y[j][:], banks[j][0], m.tanh_g[:, 5:6], None, ALU.mult).then_inc(scaled[j], 1)
                        dve.wait_ge(scaled[j], past(it + 1))
                        add_tiles(dve, m, added[j], it + 1, it, it * 8 + 4 * j,
                                  y[j][:].rearrange("p (t w) -> p t w", t=TPC))

            @block.scalar
            def _(act):
                with act.Fori(0, NCH // 2) as it:
                    for j in range(2):
                        act.wait_ge(down[j], past(it))
                        for o in range(F):
                            act.wait_ge(multiplied[j], past(it * F + o + 1))
                            act.activation(oq[j][:, o], prod[j][:, o], ACT.Identity, scale=col(O_F), bias=rnd[:])\
                               .then_inc(rounded[j], 1)

            @block.tensor
            def _(pe):
                with pe.Fori(0, NCH // 2) as it:
                    for j in range(2):
                        pe.wait_ge(quantized[j], past(it * F + F))
                        pe.wait_ge(scaled[j], past(it))
                        for t in range(TPC):
                            for o in range(F):
                                last = pe.matmul(banks[j][0][:, t * P:t * P + P], oq[j][:, o, t * P:t * P + P],
                                                 wT[:, 2 * F + o], start=(o == 0), stop=(o == F - 1))
                        last.then_inc(down[j], 1)


HEADS3, W3 = 8, 64
INNER = HEADS3 * W3
HID3 = int(P * 4 * 2 / 3)
PARTS3 = [(n, min(P, HID3 - n)) for n in range(0, HID3, P)]


def local_attention(nc, m, d, y, layer):
    G = HEADS3 // 2
    with Stage(nc, f"la{layer}") as st:
        wq, wk, wv = (st.sb(n, [P, INNER]) for n in ("wq", "wk", "wv"))
        wo = st.sb("wo", [P, G, P])
        cos, sin = st.sb("cos", [P, 2, W3]), st.sb("sin", [P, 2, W3])
        by, by_swapped = st.sb("by", [P, 2, W3]), st.sb("by_swapped", [P, 2, W3])
        half_power = st.sb("half_power", [P, 2 * HEADS3])
        loads = [(wq, d["l3f_wq"][layer]), (wk, d["l3f_wk"][layer]), (wv, d["l3f_wv"][layer]),
                 (wo, d["l3f_wo"][layer]), (cos, d["c_cos"]), (sin, d["c_sin"]), (by, d["l3f_scale"][layer]),
                 (by_swapped, d["l3f_scale_swapped"][layer])]
        ys, hT, hT2 = st.two("ys", [P, P]), st.two("hT", [P, P]), st.two("hT2", [P, 2, 2, S])
        sq, qk, turned = (st.two(n, [P, 2, INNER]) for n in ("sq", "qk", "turned"))
        length, rlen = st.two("length", [P, 2 * HEADS3]), st.two("rlen", [P, 2 * HEADS3])
        qT = st.two("qT", [P, G, P])
        kd = st.two("kd", [P, G, 2, 2, S])
        vd = st.two("vd", [P, 2, G, 2, W3 + 1])
        prob, pT = st.two("prob", [P, HEADS3, S]), st.two("pT", [P, G, P])
        top, inv = st.two("top", [P, HEADS3]), st.two("inv", [P, HEADS3])
        o, oT = st.two("o", [P, INNER]), st.two("oT", [P, G, P])
        loaded, ready, ones_set = st.sem("loaded"), st.sem("ready"), st.sem("ones_set")
        (y_copied, y_turned, h_copied, qk_made, squared, summed, floored, rooted, scaled, v_made, v_kept_low,
         v_kept_high, cosed, sined, rotated, qk_turned, q_copied, k_kept_low, k_kept_high, scored, max_done,
         shifted, exped, p_turned, p_copied, mixed, inverted, o_done, o_turned, o_copied, out_done, added) = (
            st.sem2(n) for n in ("y_copied", "y_turned", "h_copied", "qk_made", "squared", "summed", "floored",
                                 "rooted", "scaled", "v_made", "v_kept_low", "v_kept_high", "cosed", "sined",
                                 "rotated", "qk_turned", "q_copied", "k_kept_low", "k_kept_high", "scored",
                                 "max_done", "shifted", "exped", "p_turned", "p_copied", "mixed", "inverted",
                                 "o_done", "o_turned", "o_copied", "out_done", "added"))
        F0, F1 = [x[:, 0:CH] for x in m.A], [x[:, CH:2 * CH] for x in m.A]
        G0, G1 = [x[:, 0:CH] for x in m.B], [x[:, CH:2 * CH] for x in m.B]
        blocks = lambda x: x.rearrange("p (g q) -> p g q", g=G)

        def keep_v(eng_copy, j, u):
            r = slice(u * S, u * S + S)
            for b, src in enumerate((F0[j], F1[j])):
                last = eng_copy(vd[j][r, b, :, u, 0:W3], src.rearrange("p (g u w) -> p g u w", g=G, u=2)[r, :, u])
            return last

        def keep_k(eng_copy, j, u):
            r = slice(u * S, u * S + S)
            return eng_copy(kd[j][r, :, :, u], F1[j].rearrange("p (g b k) -> p g b k", g=G, b=2)[r])

        with nc.Block() as block:
            @block.sync
            def _(sp):
                for tile, src in loads:
                    sp.dma_start(tile[:], src).then_inc(loaded, 16)

            @block.scalar
            def _(act):
                def copy_y(it, j):
                    act.wait_ge(y_turned[j], past(it))
                    act.copy(ys[j][:], y[:, it * 2 + j, :]).then_inc(y_copied[j], 1)

                def copy_h(it, j):
                    act.wait_ge(y_turned[j], past(it + 1))
                    act.wait_ge(v_made[j], past(it))
                    act.copy(hT[j][:], F0[j][:, 0:P])
                    for b in range(2):
                        last = act.copy(hT2[j][:, b], repeat_heads(F0[j][:, b * S:b * S + S], 2))
                    last.then_inc(h_copied[j], 1)

                def squares(it, j):
                    act.wait_ge(qk_made[j], past(it + 1))
                    act.wait_ge(rotated[j], past(it))
                    act.activation(sq[j][:, 0], F0[j], ACT.Square)
                    act.activation(sq[j][:, 1], F1[j], ACT.Square).then_inc(squared[j], 1)

                def values(it, j):
                    act.wait_ge(v_made[j], past(it + 1))
                    act.wait_ge(mixed[j], past(it))
                    keep_v(act.copy, j, 1).then_inc(v_kept_high[j], 1)

                def copy_qk(it, j):
                    act.wait_ge(qk_turned[j], past(it + 1))
                    act.wait_ge(scored[j], past(it))
                    act.copy(qT[j][:], blocks(F0[j])).then_inc(q_copied[j], 1)
                    keep_k(act.copy, j, 1).then_inc(k_kept_high[j], 1)

                def exps(it, j):
                    act.wait_ge(shifted[j], past(it + 1))
                    act.activation(prob[j][:], prob[j][:], ACT.Exp, scale=8.0).then_inc(exped[j], 1)

                def copy_p(it, j):
                    act.wait_ge(p_turned[j], past(it + 1))
                    act.wait_ge(mixed[j], past(it))
                    act.copy(pT[j][:], blocks(G1[j])).then_inc(p_copied[j], 1)

                def copy_o(it, j):
                    act.wait_ge(o_turned[j], past(it + 1))
                    act.wait_ge(out_done[j], past(it))
                    act.copy(oT[j][:], blocks(G0[j])).then_inc(o_copied[j], 1)

                act.wait_ge(ones_set, 8)

                def step(it, j):
                    at(it, j, 2, copy_y)
                    at(it, j, 0, copy_qk)
                    at(it, j, -1, copy_p)
                    at(it, j, 2, copy_h)
                    at(it, j, 0, exps)
                    at(it, j, 2, squares)
                    at(it, j, 1, values)
                    at(it, j, -1, copy_o)

                steps(act, step)

            @block.vector
            def _(dve):
                def lengths(it, j):
                    dve.wait_ge(squared[j], past(it + 1))
                    dve.wait_ge(rooted[j], past(it))
                    dve.tensor_reduce(length[j][:], sq[j][:].rearrange("p n (h w) -> p (n h) w", h=HEADS3), AX,
                                      ALU.add).then_inc(summed[j], 1)
                    dve.wait_ge(summed[j], past(it + 1))
                    dve.tensor_scalar(length[j][:], length[j][:], 1e-24, None, ALU.max).then_inc(floored[j], 1)

                def normalize(it, j):
                    dve.wait_ge(rooted[j], past(it + 1))
                    dve.wait_ge(qk_turned[j], past(it))
                    for n, src in enumerate((F0[j], F1[j])):
                        last = dve.tensor_tensor(per_head(qk[j][:, n], HEADS3, W3), per_head(src, HEADS3, W3),
                                                 spread_heads(rlen[j][:, n * HEADS3:(n + 1) * HEADS3], W3), ALU.mult)
                    last.then_inc(scaled[j], 1)

                def cosines(it, j):
                    dve.wait_ge(scaled[j], past(it + 1))
                    dve.wait_ge(rotated[j], past(it))
                    heads = lambda x: x.rearrange("p n (h w) -> p n h w", h=HEADS3)
                    dve.tensor_tensor(heads(turned[j][:]), heads(qk[j][:]),
                                      cos[:, :, None, :].broadcast_to([P, 2, HEADS3, W3]), ALU.mult)\
                       .then_inc(cosed[j], 1)

                def values(it, j):
                    dve.wait_ge(v_made[j], past(it + 1))
                    dve.wait_ge(mixed[j], past(it))
                    keep_v(dve.tensor_copy, j, 0).then_inc(v_kept_low[j], 1)

                def keys(it, j):
                    dve.wait_ge(qk_turned[j], past(it + 1))
                    dve.wait_ge(scored[j], past(it))
                    keep_k(dve.tensor_copy, j, 0).then_inc(k_kept_low[j], 1)

                def shift(it, j):
                    dve.wait_ge(scored[j], past(it + 1))
                    dve.tensor_reduce(top[j][:], per_head(G0[j], HEADS3, S), AX, ALU.max).then_inc(max_done[j], 1)
                    dve.wait_ge(max_done[j], past(it + 1))
                    dve.wait_ge(p_turned[j], past(it))
                    dve.tensor_tensor(prob[j][:], per_head(G0[j], HEADS3, S), spread_heads(top[j][:], S),
                                      ALU.subtract).then_inc(shifted[j], 1)

                def outputs(it, j):
                    outs = [[x[j][:, 0:4 * (W3 + 1)].rearrange("p (h w) -> p h w", h=4) for x in (G0, G1)]
                        for j in range(2)]
                    dve.wait_ge(mixed[j], past(it + 1))
                    for n in range(2):
                        last = dve.reciprocal(inv[j][:, 4 * n:4 * n + 4], outs[j][n][:, :, W3])
                    last.then_inc(inverted[j], 1)
                    dve.wait_ge(inverted[j], past(it + 1))
                    dve.wait_ge(o_turned[j], past(it))
                    for n in range(2):
                        last = dve.tensor_tensor(per_head(o[j][:], HEADS3, W3)[:, 4 * n:4 * n + 4],
                                                 outs[j][n][:, :, 0:W3],
                                                 spread_heads(inv[j][:, 4 * n:4 * n + 4], W3), ALU.mult)
                    last.then_inc(o_done[j], 1)

                def add(it, j):
                    t = it * 2 + j
                    dve.wait_ge(out_done[j], past(it + 1))
                    dve.tensor_tensor(y[:, t, :], y[:, t, :], G1[j][:, 0:P], ALU.add).then_inc(added[j], 1)

                for j in range(2):
                    dve.memset(kd[j][:], 0.0).then_inc(ones_set, 1)
                    dve.memset(vd[j][:, :, :, :, 0:W3], 0.0).then_inc(ones_set, 1)
                dve.wait_ge(loaded, 16 * len(loads))
                dve.tensor_tensor(cos[:], cos[:], by[:], ALU.mult).then_inc(ready, 1)
                dve.tensor_tensor(sin[:], sin[:], by_swapped[:], ALU.mult).then_inc(ready, 1)
                dve.wait_ge(ones_set, 8)
                dve.wait_ge(ready, 3)

                def step(it, j):
                    at(it, j, 0, keys)
                    at(it, j, 1, normalize)
                    at(it, j, 0, shift)
                    at(it, j, 1, cosines)
                    at(it, j, -1, outputs)
                    at(it, j, 2, lengths)
                    at(it, j, 1, values)
                    at(it, j, -2, add)

                steps(dve, step)

            @block.gpsimd
            def _(pool):
                for j in range(2):
                    for b in range(2):
                        pool.tensor_copy(vd[j][:, b, :, :, W3], repeat_heads(m.half[:], G)).then_inc(ones_set, 1)
                pool.memset(half_power[:], -0.5).then_inc(ready, 1)
                pool.wait_ge(ready, 3)
                with pool.Fori(0, PAIRS) as it:
                    for j in range(2):
                        pool.wait_ge(floored[j], past(it + 1))
                        pool.wait_ge(scaled[j], past(it))
                        pool.tensor_tensor(rlen[j][:], length[j][:], half_power[:], ALU.pow).then_inc(rooted[j], 1)
                        x = qk[j][:].rearrange("p n (h w) -> p n h w", h=HEADS3)
                        z = sq[j][:].rearrange("p n (h w) -> p n h w", h=HEADS3)
                        along = lambda w: sin[:, :, None, w].broadcast_to([P, 2, HEADS3, w.stop - w.start])
                        lo, hi = slice(0, W3 // 2), slice(W3 // 2, W3)
                        pool.wait_ge(scaled[j], past(it + 1))
                        pool.tensor_tensor(z[:, :, :, lo], x[:, :, :, hi], along(lo), ALU.mult)
                        pool.tensor_tensor(z[:, :, :, hi], x[:, :, :, lo], along(hi), ALU.mult).then_inc(sined[j], 1)
                        pool.wait_ge(sined[j], past(it + 1))
                        pool.wait_ge(cosed[j], past(it + 1))
                        pool.tensor_tensor(qk[j][:], turned[j][:], sq[j][:], ALU.add).then_inc(rotated[j], 1)

            @block.tensor
            def _(pe):
                def turn_y(it, j):
                    pe.wait_ge(y_copied[j], past(it + 1))
                    pe.wait_ge(q_copied[j], past(it))
                    pe.matmul(F0[j][0:S, 0:P], ys[j][:, 0:P // 2], m.ident[:], start=True, stop=True)
                    pe.matmul(F0[j][S:P, 0:P], ys[j][:, P // 2:P], m.shift[:], start=True, stop=True)\
                      .then_inc(y_turned[j], 1)

                def make_qk(it, j):
                    pe.wait_ge(h_copied[j], past(it + 1))
                    pe.wait_ge(k_kept_low[j], past(it))
                    pe.wait_ge(k_kept_high[j], past(it))
                    pe.matmul(F0[j], hT[j][:], wq[:], start=True, stop=True)
                    pe.matmul(F1[j], hT[j][:], wk[:], start=True, stop=True).then_inc(qk_made[j], 1)

                def make_v(it, j):
                    pe.wait_ge(scaled[j], past(it + 1))
                    for b, dst in enumerate((F0[j], F1[j])):
                        last = pe.matmul(dst, hT2[j][:, b].rearrange("p u k -> p (u k)"), wv[:],
                                         start=True, stop=True)
                    last.then_inc(v_made[j], 1)

                def turn_qk(it, j):
                    pe.wait_ge(rotated[j], past(it + 1))
                    pe.wait_ge(v_kept_low[j], past(it + 1))
                    pe.wait_ge(v_kept_high[j], past(it + 1))
                    for n, dst in enumerate((F0[j], F1[j])):
                        for g in range(G):
                            last = pe.transpose(dst[:, g * P:g * P + P], qk[j][:, n, g * P:g * P + P], m.ident[:])
                    last.then_inc(qk_turned[j], 1)

                def scores(it, j):
                    pe.wait_ge(o_copied[j], past(it))
                    pe.matmul(G0[j], m.ident_bf[:], repeat_heads(m.causal_bf[:], HEADS3), start=True, stop=False)
                    pe.wait_ge(q_copied[j], past(it + 1))
                    pe.wait_ge(k_kept_low[j], past(it + 1))
                    pe.wait_ge(k_kept_high[j], past(it + 1))
                    for b in range(2):
                        for g in range(G):
                            last = pe.matmul(G0[j][b * S:b * S + S, g * P:g * P + P], qT[j][:, g, b * S:b * S + S],
                                             kd[j][:, g, b].rearrange("p u k -> p (u k)"), start=False,
                                             stop=(g == G - 1))
                    last.then_inc(scored[j], 1)

                def turn_p(it, j):
                    pe.wait_ge(exped[j], past(it + 1))
                    pe.wait_ge(added[j], past(it))
                    p = prob[j][:].rearrange("p h k -> p (h k)")
                    for g in range(G):
                        last = pe.transpose(G1[j][:, g * P:g * P + P], p[:, g * P:g * P + P], m.ident[:])
                    last.then_inc(p_turned[j], 1)

                def mix(it, j):
                    pe.wait_ge(p_copied[j], past(it + 1))
                    n = 2 * (W3 + 1)
                    for b in range(2):
                        for g in range(G):
                            dst = (G0, G1)[g // 2][j]
                            last = pe.matmul(dst[b * S:b * S + S, g % 2 * n:g % 2 * n + n],
                                             pT[j][:, g, b * S:b * S + S],
                                             vd[j][:, b, g].rearrange("p u w -> p (u w)"), start=True, stop=True)
                    last.then_inc(mixed[j], 1)

                def turn_o(it, j):
                    pe.wait_ge(o_done[j], past(it + 1))
                    for g in range(G):
                        last = pe.transpose(G0[j][:, g * P:g * P + P], o[j][:, g * P:g * P + P], m.ident[:])
                    last.then_inc(o_turned[j], 1)

                def project(it, j):
                    pe.wait_ge(o_copied[j], past(it + 1))
                    for g in range(G):
                        last = pe.matmul(G1[j][:, 0:P], oT[j][:, g], wo[:, g], start=(g == 0), stop=(g == G - 1))
                    last.then_inc(out_done[j], 1)

                pe.wait_ge(loaded, 16 * len(loads))
                pe.wait_ge(ones_set, 8)

                def step(it, j):
                    at(it, j, 0, turn_qk)
                    at(it, j, -1, turn_p)
                    at(it, j, -2, project)
                    at(it, j, 2, turn_y)
                    at(it, j, 0, scores)
                    at(it, j, 2, make_qk)
                    at(it, j, -1, mix)
                    at(it, j, 1, make_v)
                    at(it, j, -1, turn_o)

                steps(pe, step)


def gated_gelu(nc, m, d, y, layer):
    with Stage(nc, f"gg{layer}") as st:
        F = len(PARTS3)
        w1, w2 = st.sb("w1", [P, 2 * HID3]), st.sb("w2", [P, F, P])
        b1, b2 = st.sb("b1", [P, 2, F]), st.sb("b2", [1, P])
        lg, lb = st.sb("lg", [P, 1]), st.sb("lb", [P, 1])
        loads = [(w1, "l3f_w1"), (w2, "l3f_w2"), (b1, "l3f_b1"), (b2, "l3f_b2"), (lg, "l3f_lg"), (lb, "l3f_lb")]
        half_power = st.sb("half_power", [P, TPC])
        h, hT = st.two("h", [P, TPC, P]), st.two("hT", [P, CH])
        stats = st.two("stats", [P, TPC, 6])
        mean, delta, var, rstd = (st.two(n, [P, TPC]) for n in ("mean", "delta", "var", "rstd"))
        gate, hid = st.two("gate", [P, F, CH]), st.two("hid", [P, F, CH])
        loaded, ready = st.sem("loaded"), st.sem("ready")
        (moved, h_set, stat, parts, terms, aggregated, rooted, normed_h, turned, copied, up, gelued, hidden, down, added) = (
            st.sem2(n) for n in ("moved", "h_set", "stat", "parts", "terms", "aggregated", "rooted", "normed_h", "turned",
                                 "copied", "up", "gelued", "hidden", "down", "added"))
        A0, A1 = [x[:, 0:CH] for x in m.A], [x[:, CH:2 * CH] for x in m.A]
        B0, B1 = [x[:, 0:CH] for x in m.B], [x[:, CH:2 * CH] for x in m.B]
        up_bank = lambda j, o: (A0, A1)[o % 2][j]
        gate_bank = lambda j, o: (B0, B1)[o % 2][j]
        with nc.Block() as block:
            @block.sync
            def _(sp):
                for tile, src in loads:
                    sp.dma_start(tile[:], d[src][layer]).then_inc(loaded, 16)

            @block.vector
            def _(dve):
                dve.wait_ge(loaded, 16 * len(loads))
                with dve.Fori(0, NCH // 2) as it:
                    for j in range(2):
                        ty = y[:, bass.ds(it * 8 + 4 * j, TPC), :]
                        dve.wait_ge(turned[j], past(it))
                        dve.tensor_copy(h[j][:, :, 0:S], ty[:, :, 0:S])
                        dve.wait_ge(moved[j], past(it + 1))
                        dve.tensor_copy(h[j][:, :, S:P], A0[j][:, 0:TPC * S].rearrange("p (t w) -> p t w", t=TPC))\
                           .then_inc(h_set[j], 1)
                    for j in range(2):
                        dve.wait_ge(h_set[j], past(it + 1))
                        for t in range(TPC):
                            last = dve.bn_stats(stats[j][:, t], h[j][:, t])
                        last.then_inc(stat[j], 1)
                    for j in range(2):
                        dve.wait_ge(stat[j], past(it + 1))
                        mean_e, m2_e, mean_o, m2_o = (stats[j][:, :, k] for k in (1, 2, 4, 5))
                        dve.wait_ge(normed_h[j], past(it))
                        dve.tensor_tensor(mean[j][:], mean_e, mean_o, ALU.add)
                        dve.tensor_tensor(delta[j][:], mean_e, mean_o, ALU.subtract)
                        dve.tensor_tensor(var[j][:], m2_e, m2_o, ALU.add).then_inc(parts[j], 1)
                    for j in range(2):
                        dve.wait_ge(parts[j], past(it + 1))
                        dve.tensor_scalar(mean[j][:], mean[j][:], 0.5, None, ALU.mult)
                        dve.scalar_tensor_tensor(delta[j][:], delta[j][:], 0.25, delta[j][:], ALU.mult, ALU.mult)
                        dve.tensor_scalar(var[j][:], var[j][:], 1.0 / P, 1e-5, ALU.mult, ALU.add).then_inc(terms[j], 1)
                    for j in range(2):
                        dve.wait_ge(terms[j], past(it + 1))
                        dve.tensor_tensor(var[j][:], var[j][:], delta[j][:], ALU.add).then_inc(aggregated[j], 1)
                    for j in range(2):
                        dve.wait_ge(rooted[j], past(it + 1))
                        for t in range(TPC):
                            last = dve.tensor_scalar(h[j][:, t], h[j][:, t], mean[j][:, t:t + 1], rstd[j][:, t:t + 1],
                                                     ALU.subtract, ALU.mult)
                        last.then_inc(normed_h[j], 1)
                    for j in range(2):
                        for o, (_, k) in enumerate(PARTS3):
                            dve.wait_ge(gelued[j], past(it * F + o + 1))
                            dve.scalar_tensor_tensor(hid[j][0:k, o], up_bank(j, o)[0:k], b1[0:k, 0, o:o + 1],
                                                     gate[j][0:k, o], ALU.add, ALU.mult).then_inc(hidden[j], 1)
                    for j in range(2):
                        dve.wait_ge(down[j], past(it + 1))
                        ty = y[:, bass.ds(it * 8 + 4 * j, TPC), :]
                        dve.tensor_tensor(ty, ty, A1[j].rearrange("p (t w) -> p t w", t=TPC), ALU.add)\
                           .then_inc(added[j], 1)

            @block.gpsimd
            def _(pool):
                pool.memset(half_power[:], -0.5).then_inc(ready, 1)
                pool.wait_ge(ready, 1)
                with pool.Fori(0, NCH // 2) as it:
                    for j in range(2):
                        pool.wait_ge(aggregated[j], past(it + 1))
                        pool.wait_ge(normed_h[j], past(it))
                        pool.tensor_tensor(rstd[j][:], var[j][:], half_power[:], ALU.pow).then_inc(rooted[j], 1)

            @block.scalar
            def _(act):
                act.wait_ge(loaded, 16 * len(loads))
                with act.Fori(0, NCH // 2) as it:
                    for j in range(2):
                        act.wait_ge(turned[j], past(it + 1))
                        act.activation(hT[j][:], A1[j], ACT.Identity, scale=lg[:], bias=lb[:]).then_inc(copied[j], 1)
                    for j in range(2):
                        for o, (_, k) in enumerate(PARTS3):
                            act.wait_ge(up[j], past(it * F + o + 1))
                            act.activation(gate[j][0:k, o], gate_bank(j, o)[0:k], ACT.Gelu, bias=b1[0:k, 1, o:o + 1])\
                               .then_inc(gelued[j], 1)

            @block.tensor
            def _(pe):
                pe.wait_ge(loaded, 16 * len(loads))
                with pe.Fori(0, NCH // 2) as it:
                    for j in range(2):
                        pe.wait_ge(added[j], past(it))
                        pe.matmul(A0[j][:, 0:TPC * S], m.shift[:], y[:, bass.ds(it * 8 + 4 * j, TPC), S:P],
                                  start=True, stop=True).then_inc(moved[j], 1)
                    for j in range(2):
                        pe.wait_ge(normed_h[j], past(it + 1))
                        for t in range(TPC):
                            last = pe.transpose(A1[j][:, t * P:t * P + P], h[j][:, t], m.ident[:])
                        last.then_inc(turned[j], 1)
                    for j in range(2):
                        pe.wait_ge(copied[j], past(it + 1))
                        for o, (n, k) in enumerate(PARTS3):
                            if o >= 2:
                                pe.wait_ge(hidden[j], past(it * F + o - 1))
                            pe.matmul(up_bank(j, o)[0:k], w1[:, n:n + k], hT[j][:], start=True, stop=True)
                            pe.matmul(gate_bank(j, o)[0:k], w1[:, HID3 + n:HID3 + n + k], hT[j][:],
                                      start=True, stop=True).then_inc(up[j], 1)
                    for j in range(2):
                        pe.wait_ge(hidden[j], past(it * F + F))
                        for t in range(TPC):
                            dst = A1[j][:, t * P:t * P + P]
                            pe.matmul(dst, m.ones_row[:], b2[:], start=True, stop=False)
                            for o, (_, k) in enumerate(PARTS3):
                                last = pe.matmul(dst, hid[j][0:k, o, t * P:t * P + P], w2[0:k, o],
                                                 start=False, stop=(o == F - 1))
                        last.then_inc(down[j], 1)


def l3_ffn(nc, m, d, own):
    y = own.enter_context(nc.sbuf_tensor("l3f_y", [P, NT, P], F32))
    with Stage(nc, "l3f_in") as st:
        with nc.Block() as block:
            @block.vector
            def _(dve):
                with dve.Fori(0, PAIRS) as it:
                    for j in range(2):
                        t = it * 2 + j
                        normed(dve, m, y[:, t, :], t)
    for layer in range(2):
        local_attention(nc, m, d, y, layer)
        gated_gelu(nc, m, d, y, layer)
    with Stage(nc, "l3f_out") as st:
        with nc.Block() as block:
            @block.vector
            def _(dve):
                with dve.Fori(0, NCH) as it:
                    for xs, ys in ((m.X[:, bass.ds(it * TPC, TPC), :], y[:, bass.ds(it * TPC, TPC), :]),):
                        dve.scalar_tensor_tensor(xs, ys, m.tanh_g[:, 7:8], xs, ALU.mult, ALU.add)


class Memory:

    def __init__(self, nc, ctx):
        def sb(name, shape, dt=F32):
            return ctx.enter_context(nc.sbuf_tensor(name, list(shape), dt))

        self.X = sb("X", [P, NT, P])
        self.S6 = sb("S6", [P, NT, 6])
        self.mean, self.rstd = sb("mean", [P, NT]), sb("rstd", [P, NT])
        self.ident, self.ident_bf = sb("ident", [P, P]), sb("ident_bf", [P, P], BF16)
        self.blockones = sb("blockones", [P, P])
        self.tri = sb("tri", [P, P])
        self.shift = sb("shift", [P, P])
        self.eye64 = sb("eye64", [P, S])
        self.causal, self.causal_bf = sb("causal", [P, S]), sb("causal_bf", [P, S], BF16)
        self.half = sb("half", [P, 2])
        self.head8 = sb("head8", [P, 8])
        self.head_of_8 = sb("head_of_8", [P, 8])
        self.gates, self.tanh_g = sb("gates", [P, 8]), sb("tanh_g", [P, 8])
        self.ones_row = sb("ones_row", [1, P])
        self.A = [ctx.enter_context(nc.psum_tensor(f"A{j}", [P, 1024], F32)) for j in range(2)]
        self.B = [ctx.enter_context(nc.psum_tensor(f"B{j}", [P, 1024], F32)) for j in range(2)]


def store(nc, m, d):
    with Stage(nc, "store") as st:
        stored = st.sem("stored")
        with nc.Block() as block:
            @block.sync
            def _(sp):
                sp.dma_start(d["out"], m.X[:]).then_inc(stored, 16)
                sp.wait_ge(stored, 16)


def program(nc, d, stages=None):
    with ExitStack() as ctx:
        m = Memory(nc, ctx)
        setup(nc, m, d)
        for n, stage in enumerate(STAGES):
            if stages is None or n in stages:
                norm_header(nc, m, f"norm{n}")
                with ExitStack() as own:
                    stage(nc, m, d, own)
        store(nc, m, d)


def l0_xattn(nc, m, d, own):
    sb = lambda n, s: own.enter_context(nc.sbuf_tensor(n, s, F32))
    m.gate, m.fsum, m.a = sb("gate", [P, NT, 16]), sb("fsum", [P, NT, 8]), sb("a", [P, NT, 8])
    m.h = sb("h", [P, NT, P])
    gated_memory(nc, m, d)


STAGES = [l0_xattn, l0_ffn, l1_xattn, l1_ffn, l2_xattn, l2_ffn, l3_xattn, l3_ffn]


def shape_constants():
    i, b = np.arange(P) % S, np.arange(P) // S
    same = b[:, None] == b[None, :]
    f = lambda x: np.ascontiguousarray(x.astype(np.float32))
    return {
        "c_ident": f(np.eye(P)),
        "c_blockones": f(same),
        "c_tri": f(same & (i[:, None] <= i[None, :])),
        "c_shift": f(same & (i[:, None] + 1 == i[None, :])),
        "c_lower_e": f(np.broadcast_to(np.arange(8)[None, None, :] < np.arange(8)[None, :, None], (P, 8, 8))),
        "c_half": f(b[:, None] == np.arange(2)[None, :]),
        "c_eye64": f(i[:, None] == np.arange(S)[None, :]),
        "c_causal": f(np.where(np.arange(S)[None, :] > i[:, None], NEG, 0.0)),
        "c_head_of_8": f(np.arange(P)[:, None] // 8 % 8 == np.arange(8)[None, :]),
        "c_head8": f(np.arange(P)[:, None] // 16 == np.arange(8)[None, :]),
    }


def rotary_tables():
    f = np.float32
    half = np.arange(0, W3, 2, dtype=f)
    freqs = np.arange(S, dtype=f)[:, None] * (f(1.0) / f(10000.0) ** (half / f(W3)))[None, :]
    freqs = np.concatenate([freqs, freqs], axis=-1)
    base = (half + f(0.4 * W3)) / f(1.4 * W3)
    power = (np.arange(S, dtype=f) - f(S // 2)) / f(S // 2)
    scale = base[None, :] ** power[:, None]
    scale = np.concatenate([scale, scale], axis=-1)
    cos, sin = np.cos(freqs), np.sin(freqs)
    sin[:, :W3 // 2] *= f(-1.0)
    both = lambda t: np.ascontiguousarray(np.tile(np.stack([t * scale, t / scale], axis=1), (2, 1, 1)).astype(f))
    return both(cos), both(sin)


def lay_out(v):
    rows = lambda a: np.ascontiguousarray(np.broadcast_to(a.reshape(1, -1), (P, a.size)))
    T = lambda a: np.ascontiguousarray(a.T)
    x, ctx = v["x"], v["ctx_1024"]
    d = dict(shape_constants())
    d["x"] = np.ascontiguousarray(x.reshape(NT, P, P).transpose(1, 0, 2))
    d["ctxT"] = np.ascontiguousarray(ctx.reshape(NT, P, P).transpose(0, 2, 1))
    d["ctx_rows"] = np.ascontiguousarray(ctx.reshape(NT, P, P).transpose(1, 0, 2))
    d["ctx"] = np.ascontiguousarray(ctx.transpose(1, 0, 2))
    d["gates"] = rows(np.concatenate([v["g_xattn"], v["g_ffn"]]))
    wi, wf = v["L0_xattn_igate_w"], v["L0_xattn_fgate_w"]
    for n, k in enumerate("qkv"):
        d[f"l0_gate_{k}"] = T(np.concatenate([wi, wf])[:, n * P:(n + 1) * P])
    d["l0_gate_b"] = rows(np.concatenate([v["L0_xattn_igate_b"], v["L0_xattn_fgate_b"]]))
    d["l0_norm_w"] = rows(v["L0_xattn_norm_w"])
    more_layout(d, v, rows, T)
    return d


def more_layout(d, v, rows, T):
    parts = lambda a: np.ascontiguousarray(a.reshape(-1, P, a.shape[-1]).transpose(1, 0, 2))
    cols = lambda a: np.ascontiguousarray(a.reshape(-1, P).T)
    for n in ("w1", "w2"):
        d[f"l0f_{n}"] = T(v[f"L0_ffn_{n}_w"])
    for n in ("h1", "h2", "w3"):
        d[f"l0f_{n}"] = parts(v[f"L0_ffn_{n}_w"].T)
    d["l0f_s"] = np.ascontiguousarray(np.stack([cols(v[f"L0_ffn_{n}_s"]) for n in ("w1", "w2", "h1", "h2")], axis=1))
    d["l0f_s3"] = rows(v["L0_ffn_w3_s"])
    column = lambda a: np.ascontiguousarray(a.reshape(-1, 1))
    for n in "qkvo":
        d[f"l1x_w{n}"] = T(v[f"L1_xattn_w{n}"])
    d["l1x_bq"], d["l1x_bk"] = column(v["L1_xattn_bq"]), column(v["L1_xattn_bk"])
    d["l1x_bv"], d["l1x_bo"] = rows(v["L1_xattn_bv"]), v["L1_xattn_bo"].reshape(1, P)
    d["l1x_mask"] = T(v["mask_BxS_ik0"])
    d["l2x_wo"], d["l2x_bo"] = T(v["L2_xattn_W_out"]), v["L2_xattn_b_out"].reshape(1, P)
    d["l2x_mask"] = np.ascontiguousarray(v["mask_Bx1xSxS2_ik1"][:, 0].transpose(1, 0, 2))
    for n in "qk":
        d[f"l3x_w{n}"] = T(v[f"L3_xattn_W{n}_w"])
        d[f"l3x_b{n}"] = column(v[f"L3_xattn_W{n}_b"])
    keys = np.broadcast_to(v["mask_BxS2_ik1"].reshape(NT, 2, 1, S), (NT, 2, S, S))
    d["l3x_mask"] = np.ascontiguousarray(keys.transpose(1, 2, 0, 3)).reshape(P, NT, S)
    w = [v[f"L1_ffn_w_{n}"].reshape(3, P, P).transpose(1, 0, 2) for n in ("up", "gate")]
    d["l1f_w"] = np.ascontiguousarray(np.concatenate([*w, v["L1_ffn_w_down"].reshape(P, 3, P)], axis=1).reshape(P, 9 * P))
    d["c_cos"], d["c_sin"] = rotary_tables()
    for n, k in enumerate("qkv"):
        d[f"l3f_w{k}"] = np.ascontiguousarray(v["L3_ffn_wqkv"][:, :, n * INNER:(n + 1) * INNER])
    d["l3f_wo"] = np.ascontiguousarray(v["L3_ffn_wo"].reshape(2, -1, P, P).transpose(0, 2, 1, 3))
    scales = np.stack([v["L3_ffn_q_scale"], v["L3_ffn_k_scale"]], axis=1)
    swapped = np.concatenate([scales[:, :, W3 // 2:], scales[:, :, :W3 // 2]], axis=-1)
    for n, a in (("scale", scales), ("scale_swapped", swapped)):
        d[f"l3f_{n}"] = np.ascontiguousarray(np.broadcast_to(a[:, None], (2, P, 2, W3)))
    pad = len(PARTS3) * P - HID3
    d["l3f_w1"] = v["L3_ffn_w1"]
    d["l3f_w2"] = np.ascontiguousarray(np.pad(v["L3_ffn_w2"], ((0, 0), (0, pad), (0, 0)))
                                       .reshape(2, -1, P, P).transpose(0, 2, 1, 3))
    d["l3f_b1"] = np.ascontiguousarray(np.pad(v["L3_ffn_b1"].reshape(2, 2, HID3), ((0, 0), (0, 0), (0, pad)))
                                       .reshape(2, 2, -1, P).transpose(0, 3, 1, 2))
    d["l3f_b2"] = v["L3_ffn_b2"].reshape(2, 1, P)
    d["l3f_lg"], d["l3f_lb"] = v["L3_ffn_ln_g"].reshape(2, P, 1), v["L3_ffn_ln_b"].reshape(2, P, 1)
    d["l2f_wr"] = v["L2_ffn_Wr"]
    d["l2f_temp"] = rows(v["L2_ffn_temperature"])
    for n in ("g", "u", "d"):
        d[f"l2f_w{n}"] = np.ascontiguousarray(v[f"L2_ffn_W{n}"].transpose(1, 0, 2))


def declare(nc, arrays):
    d = {n: nc.dram_tensor(f"in_{n}", a.shape, mybir.dt.from_np(a.dtype), kind="ExternalInput").ap()
         for n, a in arrays.items()}
    d["out"] = nc.dram_tensor("out", (P, NT, P), F32, kind="ExternalOutput").ap()
    return d


def kernel(**inputs):
    import concourse.bacc as bacc
    from concourse.bass_utils import run_bass_kernel_spmd

    arrays = lay_out({n: np.asarray(a) for n, a in inputs.items()})
    nc = bacc.Bacc("TRN2", target_bir_lowering=False, num_devices=1)
    program(nc, declare(nc, arrays))
    r = run_bass_kernel_spmd(nc, [{f"in_{n}": a for n, a in arrays.items()}], core_ids=[0])
    out = r.results[0]["out"]
    return np.ascontiguousarray(out.transpose(1, 0, 2)).reshape(NB, S, P)
```

```python
from contextlib import ExitStack

import numpy as np

import concourse.bass as bass
from concourse import mybir

F32 = mybir.dt.float32
BF16 = mybir.dt.bfloat16
I32 = mybir.dt.int32
I16 = mybir.dt.int16
ALU = mybir.AluOpType
ACT = mybir.ActivationFunctionType
AX = mybir.AxisListType.X

P = 128
S = 64
NB = 128
NT = NB * S // P
PAIRS = NT // 2
CH = 512
NCH = NB * S // CH
CHUNK_PAIRS = NCH // 2
TPC = CH // P
NEG = -1e30
ROUND = 12582912.0


def past(n):
    return n + 1


class Stage:

    def __init__(self, nc, name):
        self.nc, self.name, self.stack, self.sems = nc, name, ExitStack(), []

    def __enter__(self):
        return self

    def __exit__(self, *exc):
        if exc[0] is None:
            self.nc.clear_and_free_semaphores(self.sems)
            self.nc.all_engine_barrier()
            self.stack.close()

    def sb(self, name, shape, dt=F32):
        return self.stack.enter_context(self.nc.sbuf_tensor(f"{self.name}_{name}", list(shape), dt))

    def two(self, name, shape, dt=F32):
        return [self.sb(f"{name}{j}", shape, dt) for j in range(2)]

    def sem(self, name):
        self.sems.append(self.nc.alloc_semaphore(f"{self.name}_{name}"))
        return self.sems[-1]

    def counter(self, name, start=1):
        sem = self.sem(name)
        self.nc.sync.sem_inc(sem, start)
        return sem

    def sem2(self, name):
        return [self.counter(f"{name}{j}") for j in range(2)]


def at(it, j, lag, work, pairs=PAIRS):
    pair, j = it + (j + lag) // 2, (j + lag) % 2
    if not isinstance(pair, int) or 0 <= pair < pairs:
        work(pair, j)


def steps(eng, step, pairs=PAIRS):
    for it in (-1, 0):
        for j in range(2):
            step(it, j)
    with eng.Fori(1, pairs - 1) as it:
        for j in range(2):
            step(it, j)
    for it in (pairs - 1, pairs):
        for j in range(2):
            step(it, j)


def setup(nc, m, d):
    LOADS = 4
    part = NT // LOADS
    with Stage(nc, "setup") as st:
        loaded, filled = st.sem("loaded"), st.sem("filled")
        x_in = [st.sem(f"x_in{n}") for n in range(LOADS)]
        consts = [(m.ident, d["c_ident"]), (m.blockones, d["c_blockones"]), (m.tri, d["c_tri"]),
                  (m.shift, d["c_shift"]), (m.eye64, d["c_eye64"]), (m.causal, d["c_causal"]),
                  (m.half, d["c_half"]), (m.head_of_8, d["c_head_of_8"]), (m.head8, d["c_head8"]),
                  (m.gates, d["gates"])]
        n_loads = 16 * len(consts)
        with nc.Block() as block:
            @block.sync
            def _(sp):
                for n in range(LOADS):
                    tiles = slice(n * part, n * part + part)
                    sp.dma_start(m.X[:, tiles, :], d["x"][:, tiles, :]).then_inc(x_in[n], 16)

            @block.scalar
            def _(act):
                for tile, src in consts:
                    act.dma_start(tile[:], src).then_inc(loaded, 16)
                act.wait_ge(loaded, n_loads)
                act.activation(m.tanh_g[:], m.gates[:], ACT.Tanh)
                act.copy(m.ident_bf[:], m.ident[:])
                act.copy(m.causal_bf[:], m.causal[:])
                act.wait_ge(filled, 1)

            @block.vector
            def _(dve):
                dve.memset(m.ones_row[:], 1.0).then_inc(filled, 1)
                for n in range(LOADS):
                    dve.wait_ge(x_in[n], 16)
                    with dve.Fori(n * part // TPC, (n + 1) * part // TPC) as it:
                        for t in range(TPC):
                            dve.bn_stats(m.S6[:, it * TPC + t, :], m.X[:, it * TPC + t, :])


def norm_header(nc, m, name, s6=None):
    s6 = m.S6 if s6 is None else s6
    with Stage(nc, name) as st:
        delta, spread = st.sb("delta", [P, NT]), st.sb("spread", [P, NT])
        step, rooted = st.sem("step"), st.sem("rooted")
        mean_e, m2_e, mean_o, m2_o = (s6[:, :, k] for k in (1, 2, 4, 5))
        with nc.Block() as block:
            @block.vector
            def _(dve):
                dve.tensor_tensor(m.mean[:], mean_e, mean_o, ALU.add)
                dve.tensor_tensor(delta[:], mean_e, mean_o, ALU.subtract)
                dve.tensor_tensor(spread[:], m2_e, m2_o, ALU.add).then_inc(step, 1)
                dve.wait_ge(step, 1)
                dve.tensor_scalar(m.mean[:], m.mean[:], 0.5, None, ALU.mult)
                dve.scalar_tensor_tensor(delta[:], delta[:], 0.25, delta[:], ALU.mult, ALU.mult)
                dve.tensor_scalar(spread[:], spread[:], 1.0 / P, 1e-5, ALU.mult, ALU.add).then_inc(step, 1)
                dve.wait_ge(step, 2)
                dve.tensor_tensor(spread[:], spread[:], delta[:], ALU.add).then_inc(step, 1)
                dve.wait_ge(rooted, 1)
                dve.reciprocal(m.rstd[:], delta[:])

            @block.scalar
            def _(act):
                act.wait_ge(step, 3)
                act.activation(delta[:], spread[:], ACT.Sqrt).then_inc(rooted, 1)


def normed(dve, m, dst, t, src=None):
    src = m.X if src is None else src
    return dve.tensor_scalar(dst, src[:, t, :], m.mean[:, bass.ds(t, 1)], m.rstd[:, bass.ds(t, 1)],
                             ALU.subtract, ALU.mult)


def per_head(ap, h, w):
    return ap.rearrange("p (h w) -> p h w", h=h, w=w)


def spread_heads(ap, w):
    return ap[:, :, None].broadcast_to([ap.shape[0], ap.shape[1], w])


def repeat_heads(ap, h):
    return ap[:, None, :].broadcast_to([ap.shape[0], h, ap.shape[1]])


def gated_memory(nc, m, d):
    H, W = 8, 16
    KW = H * S

    with Stage(nc, "gates") as st:
        wq, wk, wv = st.sb("wq", [P, 2 * H]), st.sb("wk", [P, 2 * H]), st.sb("wv", [P, 2 * H])
        bias, weights = st.sb("bias", [P, 2 * H]), st.sem("weights")
        xn, xnT, ctxT = (st.two(n, [P, TPC, P]) for n in ("xn", "xnT", "ctxT"))
        ctx_in, normed_x, turned, copied = (st.sem2(n) for n in ("ctx_in", "normed_x", "turned", "copied"))
        summed, biased = st.sem2("summed"), st.sem2("biased")
        joined = st.sem("joined")
        bank = [m.A[j][:, 0:CH].rearrange("p (t k) -> p t k", t=TPC) for j in range(2)]
        sums = [m.B[j][:, 0:TPC * 2 * H].rearrange("p (t h) -> p t h", t=TPC) for j in range(2)]
        with nc.Block() as block:
            @block.sync
            def _(sp):
                for tile, src in ((wq, "l0_gate_q"), (wk, "l0_gate_k"), (wv, "l0_gate_v"), (bias, "l0_gate_b")):
                    sp.dma_start(tile[:], d[src]).then_inc(weights, 16)
                with sp.Fori(0, CHUNK_PAIRS) as it:
                    for j in range(2):
                        sp.wait_ge(summed[j], past(it))
                        sp.dma_start(ctxT[j][:], d["ctxT"][bass.ds(it * 8 + 4 * j, TPC)].rearrange("t p k -> p t k"))\
                          .then_inc(ctx_in[j], 16)

            @block.vector
            def _(dve):
                def norm_x(it, j):
                    dve.wait_ge(turned[j], past(it))
                    normed_chunk(dve, m, xn[j], it * 8 + 4 * j).then_inc(normed_x[j], 1)

                def add_bias(it, j):
                    dve.wait_ge(summed[j], past(it + 1))
                    dve.tensor_tensor(m.gate[:, bass.ds(it * 8 + 4 * j, TPC), :], sums[j], repeat_heads(bias[:], TPC),
                                      ALU.add).then_inc(biased[j], 1)

                dve.wait_ge(weights, 64)
                dve.tensor_tensor(wk[:], wk[:], wv[:], ALU.add).then_inc(joined, 1)

                def step(it, j):
                    at(it, j, 1, norm_x, CHUNK_PAIRS)
                    at(it, j, -2, add_bias, CHUNK_PAIRS)

                steps(dve, step, CHUNK_PAIRS)

            @block.tensor
            def _(pe):
                def turn_x(it, j):
                    pe.wait_ge(normed_x[j], past(it + 1))
                    pe.wait_ge(copied[j], past(it))
                    for t in range(TPC):
                        last = pe.transpose(bank[j][:, t], xn[j][:, t], m.ident[:])
                    last.then_inc(turned[j], 1)

                def gates(it, j):
                    pe.wait_ge(copied[j], past(it + 1))
                    pe.wait_ge(ctx_in[j], past(it * 16 + 16))
                    pe.wait_ge(biased[j], past(it))
                    for t in range(TPC):
                        g = sums[j][:, t]
                        pe.matmul(g, xnT[j][:, t], wq[:], start=True, stop=False)
                        last = pe.matmul(g, ctxT[j][:, t], wk[:], start=False, stop=True)
                    last.then_inc(summed[j], 1)

                pe.wait_ge(joined, 1)

                def step(it, j):
                    at(it, j, 0, turn_x, CHUNK_PAIRS)
                    at(it, j, -1, gates, CHUNK_PAIRS)

                steps(pe, step, CHUNK_PAIRS)

            @block.scalar
            def _(act):
                def copy_x(it, j):
                    act.wait_ge(turned[j], past(it + 1))
                    act.wait_ge(summed[j], past(it))
                    act.copy(xnT[j][:], bank[j]).then_inc(copied[j], 1)

                def step(it, j):
                    at(it, j, 0, copy_x, CHUNK_PAIRS)

                steps(act, step, CHUNK_PAIRS)

    with Stage(nc, "decay") as st:
        f0, l0 = st.sb("f0", [P, NT, H]), st.sb("l0", [P, NT, H])
        step, logged, cum = st.sem("step"), st.sem("logged"), st.sem("cum")
        forget = m.gate[:, :, H:2 * H]
        flat = lambda x: x[:].rearrange("p t h -> p (t h)")
        with nc.Block() as block:
            @block.vector
            def _(dve):
                dve.scalar_tensor_tensor(f0[:], forget, -1.0, forget, ALU.mult, ALU.min).then_inc(step, 1)
                dve.wait_ge(logged, 2)
                dve.scalar_tensor_tensor(f0[:], forget, 0.0, l0[:], ALU.min, ALU.subtract).then_inc(step, 1)
                dve.wait_ge(cum, 1)
                sums = m.A[0][:, 0:NT * H].rearrange("p (t h) -> p t h", t=NT)
                dve.tensor_copy(m.fsum[:], sums)
                dve.tensor_tensor(m.a[:], m.gate[:, :, 0:H], sums, ALU.subtract)

            @block.scalar
            def _(act):
                act.wait_ge(step, 1)
                act.activation(l0[:], f0[:], ACT.Exp).then_inc(logged, 1)
                act.wait_ge(logged, 1)
                act.activation(l0[:], l0[:], ACT.Ln, bias=1.0).then_inc(logged, 1)

            @block.tensor
            def _(pe):
                pe.wait_ge(step, 2)
                pe.matmul(m.A[0][:, 0:NT * H], m.tri[:], flat(f0), start=True, stop=True).then_inc(cum, 1)

    with Stage(nc, "memory") as st:
        xn, qT, ctxT = st.two("xn", [P, P]), st.two("qT", [P, P]), st.two("ctxT", [P, P])
        ctx2 = st.two("ctx2", [P, 2, P])
        kx = st.two("kx", [P, 2, H, S])
        ax = st.two("ax", [P, H, S])
        vd = st.two("vd", [P, 2, H // 2, 2, W + 1])
        dmat, cT = st.two("dmat", [P, H, S]), st.two("cT", [P, H // 2, P])
        top, low, den = st.two("top", [P, H]), st.two("low", [P, H]), st.two("den", [P, H])
        names = ("ctx_in ctx2_in normed_x turned copied keys_apart a_apart values_apart scored z_done max_done"
                 " shifted exped weighted c_turned c_copied mixed floor_in floored den_abs den_max den_eps den_inv"
                 " h_done")
        e = {n: st.sem2(n) for n in names.split()}
        ctx_in, ctx2_in, normed_x, turned, copied = (e[n] for n in ("ctx_in", "ctx2_in", "normed_x", "turned", "copied"))
        ones_set = st.sem("ones_set")
        with nc.Block() as block:
            @block.sync
            def _(sp):
                with sp.Fori(0, PAIRS) as it:
                    for j in range(2):
                        sp.wait_ge(e["keys_apart"][j], past(it))
                        sp.dma_start(ctxT[j][:], d["ctxT"][it * 2 + j]).then_inc(ctx_in[j], 16)
                        sp.wait_ge(e["values_apart"][j], past(it))
                        for half in range(2):
                            sp.dma_start(ctx2[j][half * S:half * S + S], d["ctx"][:, bass.ds(it * 4 + 2 * j, 2), :])\
                              .then_inc(ctx2_in[j], 16)

            @block.gpsimd
            def _(pool):
                for j in range(2):
                    for b in range(2):
                        pool.tensor_copy(vd[j][:, b, :, :, W], repeat_heads(m.half[:], H // 2)).then_inc(ones_set, 1)
                with pool.Fori(0, PAIRS) as it:
                    for j in range(2):
                        pool.wait_ge(ctx_in[j], past(it * 16 + 16))
                        pool.wait_ge(e["scored"][j], past(it))
                        for b in range(2):
                            last = pool.tensor_tensor(kx[j][:, b], repeat_heads(ctxT[j][:, b * S:b * S + S], H),
                                                      spread_heads(m.head8[:], S), ALU.mult)
                        last.then_inc(e["keys_apart"][j], 1)
                        pool.wait_ge(e["z_done"][j], past(it))
                        pool.tensor_tensor(ax[j][:], spread_heads(m.a[:, it * 2 + j, :], S),
                                           repeat_heads(m.eye64[:], H), ALU.mult).then_inc(e["a_apart"][j], 1)
                        pool.wait_ge(ctx2_in[j], past(it * 32 + 32))
                        pool.wait_ge(e["mixed"][j], past(it))
                        for b in range(2):
                            last = pool.tensor_tensor(
                                vd[j][:, b, :, :, 0:W], ctx2[j][:, b].rearrange("p (g u w) -> p g u w", g=H // 2, u=2),
                                m.half[:, None, :, None].broadcast_to([P, H // 2, 2, W]), ALU.mult)
                        last.then_inc(e["values_apart"][j], 1)

            @block.vector
            def _(dve):
                def norm_x(it, j):
                    dve.wait_ge(turned[j], past(it))
                    normed(dve, m, xn[j][:], it * 2 + j).then_inc(normed_x[j], 1)

                def shift(it, j):
                    z = per_head(m.B[j][:, 0:KW], H, S)
                    dve.wait_ge(e["z_done"][j], past(it + 1))
                    dve.wait_ge(e["floored"][j], past(it))
                    dve.tensor_reduce(top[j][:], z, AX, ALU.max).then_inc(e["max_done"][j], 1)
                    dve.wait_ge(e["max_done"][j], past(it + 1))
                    dve.wait_ge(e["c_turned"][j], past(it))
                    dve.tensor_tensor(dmat[j][:], z, spread_heads(top[j][:], S), ALU.subtract)\
                       .then_inc(e["shifted"][j], 1)
                    dve.tensor_tensor(low[j][:], top[j][:], m.fsum[:, it * 2 + j, :], ALU.add)\
                       .then_inc(e["floor_in"][j], 1)

                def weigh(it, j):
                    dve.wait_ge(e["exped"][j], past(it + 1))
                    dve.wait_ge(e["scored"][j], past(it + 1))
                    dve.tensor_tensor(dmat[j][:], per_head(m.A[j][:, CH:CH + KW], H, S), dmat[j][:], ALU.mult)\
                       .then_inc(e["weighted"][j], 1)

                def outputs(it, j):
                    out = m.A[j][:, 0:H * (W + 1)].rearrange("p (h w) -> p h w", h=H)
                    dve.wait_ge(e["mixed"][j], past(it + 1))
                    dve.tensor_reduce(den[j][:], out[:, :, W:W + 1], AX, ALU.max, apply_absolute_value=True)\
                       .then_inc(e["den_abs"][j], 1)
                    dve.wait_ge(e["den_abs"][j], past(it + 1))
                    dve.wait_ge(e["floored"][j], past(it + 1))
                    dve.tensor_tensor(den[j][:], den[j][:], low[j][:], ALU.max).then_inc(e["den_max"][j], 1)
                    dve.wait_ge(e["den_max"][j], past(it + 1))
                    dve.tensor_scalar(den[j][:], den[j][:], 1e-6, None, ALU.add).then_inc(e["den_eps"][j], 1)
                    dve.wait_ge(e["den_eps"][j], past(it + 1))
                    dve.reciprocal(den[j][:], den[j][:]).then_inc(e["den_inv"][j], 1)
                    dve.wait_ge(e["den_inv"][j], past(it + 1))
                    dve.tensor_tensor(per_head(m.h[:, it * 2 + j, :], H, W), out[:, :, 0:W],
                                      spread_heads(den[j][:], W), ALU.mult).then_inc(e["h_done"][j], 1)

                def step(it, j):
                    at(it, j, -1, weigh)
                    at(it, j, 2, norm_x)
                    at(it, j, -2, outputs)
                    at(it, j, 0, shift)

                steps(dve, step)

            @block.scalar
            def _(act):
                def copy_x(it, j):
                    act.wait_ge(turned[j], past(it + 1))
                    act.wait_ge(e["scored"][j], past(it))
                    act.activation(qT[j][:], m.A[j][:, CH:CH + P], ACT.Copy, scale=float(W) ** -0.5).then_inc(copied[j], 1)

                def exps(it, j):
                    act.wait_ge(e["shifted"][j], past(it + 1))
                    act.activation(dmat[j][:], dmat[j][:], ACT.Exp).then_inc(e["exped"][j], 1)
                    act.wait_ge(e["floor_in"][j], past(it + 1))
                    act.activation(low[j][:], low[j][:], ACT.Exp, scale=-1.0).then_inc(e["floored"][j], 1)

                def copy_c(it, j):
                    act.wait_ge(e["c_turned"][j], past(it + 1))
                    act.wait_ge(e["mixed"][j], past(it))
                    act.copy(cT[j][:], m.B[j][:, CH:CH + KW].rearrange("p (g q) -> p g q", q=P))\
                       .then_inc(e["c_copied"][j], 1)

                def step(it, j):
                    at(it, j, -1, copy_c)
                    at(it, j, 1, copy_x)
                    at(it, j, 0, exps)

                steps(act, step)

            @block.tensor
            def _(pe):
                def turn_x(it, j):
                    pe.wait_ge(normed_x[j], past(it + 1))
                    pe.wait_ge(e["weighted"][j], past(it))
                    pe.transpose(m.A[j][:, CH:CH + P], xn[j][:], m.ident[:]).then_inc(turned[j], 1)

                def decays(it, j):
                    pe.wait_ge(e["a_apart"][j], past(it + 1))
                    pe.wait_ge(e["shifted"][j], past(it))
                    pe.matmul(m.B[j][:, 0:KW], m.blockones[:], ax[j][:], start=True, stop=False)
                    pe.matmul(m.B[j][:, 0:KW], m.ident_bf[:], repeat_heads(m.causal_bf[:], H),
                              start=False, stop=True).then_inc(e["z_done"][j], 1)

                def scores(it, j):
                    pe.wait_ge(copied[j], past(it + 1))
                    pe.wait_ge(e["keys_apart"][j], past(it + 1))
                    for b in range(2):
                        last = pe.matmul(m.A[j][b * S:b * S + S, CH:CH + KW], qT[j][:, b * S:b * S + S],
                                         kx[j][:, b], start=True, stop=True)
                    last.then_inc(e["scored"][j], 1)

                def turn_c(it, j):
                    pe.wait_ge(e["weighted"][j], past(it + 1))
                    pe.wait_ge(e["c_copied"][j], past(it))
                    c = dmat[j][:].rearrange("p h k -> p (h k)")
                    for g in range(H // 2):
                        last = pe.transpose(m.B[j][:, CH + g * P:CH + g * P + P], c[:, g * P:g * P + P], m.ident[:])
                    last.then_inc(e["c_turned"][j], 1)

                def mix(it, j):
                    pe.wait_ge(e["c_copied"][j], past(it + 1))
                    pe.wait_ge(e["values_apart"][j], past(it + 1))
                    pe.wait_ge(e["h_done"][j], past(it))
                    for b in range(2):
                        for g in range(H // 2):
                            n = 2 * (W + 1)
                            last = pe.matmul(m.A[j][b * S:b * S + S, g * n:g * n + n], cT[j][:, g, b * S:b * S + S],
                                             vd[j][:, b, g], start=True, stop=True)
                    last.then_inc(e["mixed"][j], 1)

                pe.wait_ge(ones_set, 4)

                def step(it, j):
                    at(it, j, 0, decays)
                    at(it, j, 0, scores)
                    at(it, j, -1, turn_c)
                    at(it, j, 1, turn_x)
                    at(it, j, -1, mix)

                steps(pe, step)

    with Stage(nc, "headnorm") as st:
        w = st.sb("w", [P, P])
        mean, var = st.two("mean", [P, TPC * H]), st.two("var", [P, TPC * H])
        sq, out = st.two("sq", [P, TPC * H, W]), st.two("out", [P, TPC, P])
        loaded, scaled = st.sem("loaded"), st.sem("scaled")
        names = "sums averaged centered squared summed spread root inverted normed_h weighted added"
        n = {name: st.sem2(name) for name in names.split()}
        with nc.Block() as block:
            @block.sync
            def _(sp):
                sp.dma_start(w[:], d["l0_norm_w"]).then_inc(loaded, 16)

            def chunk(it, j):
                return m.h[:, bass.ds(it * 8 + 4 * j, TPC), :]

            def heads(x):
                return x.rearrange("p t (h w) -> p (t h) w", h=H)

            @block.vector
            def _(dve):
                def center(it, j):
                    dve.wait_ge(n["normed_h"][j], past(it))
                    dve.tensor_reduce(mean[j][:], heads(chunk(it, j)), AX, ALU.add).then_inc(n["sums"][j], 1)
                    dve.wait_ge(n["sums"][j], past(it + 1))
                    dve.tensor_scalar(mean[j][:], mean[j][:], 1.0 / W, None, ALU.mult).then_inc(n["averaged"][j], 1)
                    dve.wait_ge(n["averaged"][j], past(it + 1))
                    dve.tensor_tensor(heads(chunk(it, j)), heads(chunk(it, j)), spread_heads(mean[j][:], W),
                                      ALU.subtract).then_inc(n["centered"][j], 1)

                def variance(it, j):
                    dve.wait_ge(n["squared"][j], past(it + 1))
                    dve.wait_ge(n["root"][j], past(it))
                    dve.tensor_reduce(var[j][:], sq[j][:], AX, ALU.add).then_inc(n["summed"][j], 1)
                    dve.wait_ge(n["summed"][j], past(it + 1))
                    dve.tensor_scalar(var[j][:], var[j][:], 1.0 / W, 1e-5, ALU.mult, ALU.add).then_inc(n["spread"][j], 1)

                def invert(it, j):
                    dve.wait_ge(n["root"][j], past(it + 1))
                    dve.reciprocal(mean[j][:], mean[j][:]).then_inc(n["inverted"][j], 1)

                def update(it, j):
                    xs = m.X[:, bass.ds(it * 8 + 4 * j, TPC), :]
                    dve.wait_ge(n["weighted"][j], past(it + 1))
                    dve.tensor_tensor(xs, xs, out[j][:], ALU.add).then_inc(n["added"][j], 1)
                    dve.wait_ge(n["added"][j], past(it + 1))
                    for t in range(TPC):
                        dve.bn_stats(m.S6[:, it * 8 + 4 * j + t, :], m.X[:, it * 8 + 4 * j + t, :])

                dve.wait_ge(loaded, 16)
                dve.tensor_scalar(w[:], w[:], m.tanh_g[:, 0:1], None, ALU.mult).then_inc(scaled, 1)

                def step(it, j):
                    at(it, j, 0, variance, CHUNK_PAIRS)
                    at(it, j, 1, center, CHUNK_PAIRS)
                    at(it, j, 0, invert, CHUNK_PAIRS)
                    at(it, j, -2, update, CHUNK_PAIRS)

                steps(dve, step, CHUNK_PAIRS)

            @block.scalar
            def _(act):
                def square(it, j):
                    act.wait_ge(n["centered"][j], past(it + 1))
                    act.wait_ge(n["summed"][j], past(it))
                    act.activation(sq[j][:], heads(chunk(it, j)), ACT.Square).then_inc(n["squared"][j], 1)

                def root(it, j):
                    act.wait_ge(n["spread"][j], past(it + 1))
                    act.activation(mean[j][:], var[j][:], ACT.Sqrt).then_inc(n["root"][j], 1)

                def step(it, j):
                    at(it, j, 0, root, CHUNK_PAIRS)
                    at(it, j, 1, square, CHUNK_PAIRS)

                steps(act, step, CHUNK_PAIRS)

            @block.gpsimd
            def _(pool):
                pool.wait_ge(scaled, 1)
                with pool.Fori(0, CHUNK_PAIRS) as it:
                    for j in range(2):
                        pool.wait_ge(n["inverted"][j], past(it + 1))
                        pool.wait_ge(n["added"][j], past(it))
                        pool.tensor_tensor(heads(out[j][:]), heads(chunk(it, j)), spread_heads(mean[j][:], W),
                                           ALU.mult).then_inc(n["normed_h"][j], 1)
                        pool.wait_ge(n["normed_h"][j], past(it + 1))
                        pool.tensor_tensor(out[j][:], out[j][:], repeat_heads(w[:], TPC), ALU.mult)\
                            .then_inc(n["weighted"][j], 1)


def normed_chunk(dve, m, dst, first):
    for t in range(TPC):
        last = normed(dve, m, dst[:, t], first + t)
    return last


def feature_major(nc, m, name, dst, router=None, prefetch=()):
    with Stage(nc, name) as st:
        xn = st.two("xn", [P, TPC, P])
        xnT = st.two("xnT", [P, TPC, P]) if router else None
        normed_x, turned, copied, placed = (st.sem2(n) for n in ("normed_x", "turned", "copied", "placed"))
        routed, kept = st.sem2("routed"), st.sem2("kept")
        bank = [m.A[j][:, 0:CH].rearrange("p (t k) -> p t k", t=TPC) for j in range(2)]
        logits = [m.B[j][:, 0:TPC * 8].rearrange("p (t e) -> p t e", t=TPC) for j in range(2)]
        prefetched = st.sem("prefetched")
        with nc.Block() as block:
            @block.sync
            def _(sp):
                for tile, src in prefetch:
                    sp.dma_start(tile, src).then_inc(prefetched, 16)
                if prefetch:
                    sp.wait_ge(prefetched, 16 * len(prefetch))

            @block.vector
            def _(dve):
                def norm_x(it, j):
                    dve.wait_ge(turned[j], past(it))
                    normed_chunk(dve, m, xn[j], it * 8 + 4 * j).then_inc(normed_x[j], 1)

                def keep(it, j):
                    dve.wait_ge(routed[j], past(it + 1))
                    dve.tensor_copy(router[1][:, bass.ds(it * 8 + 4 * j, TPC), :], logits[j]).then_inc(kept[j], 1)

                def step(it, j):
                    at(it, j, 1, norm_x, CHUNK_PAIRS)
                    if router:
                        at(it, j, -2, keep, CHUNK_PAIRS)

                steps(dve, step, CHUNK_PAIRS)

            @block.tensor
            def _(pe):
                def turn(it, j):
                    pe.wait_ge(normed_x[j], past(it + 1))
                    pe.wait_ge(copied[j], past(it))
                    for t in range(TPC):
                        last = pe.transpose(bank[j][:, t], xn[j][:, t], m.ident[:])
                    last.then_inc(turned[j], 1)

                def route(it, j):
                    pe.wait_ge(copied[j], past(it + 1))
                    pe.wait_ge(kept[j], past(it))
                    for t in range(TPC):
                        last = pe.matmul(logits[j][:, t], xnT[j][:, t], router[0][:], start=True, stop=True)
                    last.then_inc(routed[j], 1)

                def step(it, j):
                    at(it, j, 0, turn, CHUNK_PAIRS)
                    if router:
                        at(it, j, -1, route, CHUNK_PAIRS)

                steps(pe, step, CHUNK_PAIRS)

            @block.scalar
            def _(act):
                def copy_x(it, j):
                    act.wait_ge(turned[j], past(it + 1))
                    if router:
                        act.wait_ge(placed[j], past(it))
                        act.wait_ge(routed[j], past(it))
                        act.copy(xnT[j][:], bank[j]).then_inc(copied[j], 1)
                    else:
                        act.copy(dst[:, bass.ds(it * 8 + 4 * j, TPC), :], bank[j]).then_inc(copied[j], 1)

                def step(it, j):
                    at(it, j, 0, copy_x, CHUNK_PAIRS)

                steps(act, step, CHUNK_PAIRS)

            @block.gpsimd
            def _(pool):
                if router:
                    with pool.Fori(0, CHUNK_PAIRS) as it:
                        for j in range(2):
                            pool.wait_ge(copied[j], past(it + 1))
                            pool.tensor_copy(dst[:, bass.ds(it * 8 + 4 * j, TPC), :], xnT[j][:]).then_inc(placed[j], 1)


def add_tiles(dve, m, added, count, it, first, y):
    xs = m.X[:, bass.ds(first, TPC), :]
    dve.tensor_tensor(xs, xs, y, ALU.add).then_inc(added, 1)
    dve.wait_ge(added, past(count))
    for k in range(TPC):
        last = dve.bn_stats(m.S6[:, first + k, :], m.X[:, first + k, :])
    return last


def l0_ffn(nc, m, d, own):
    F = 4
    xnT = own.enter_context(nc.sbuf_tensor("l0f_xnT", [P, NT, P], F32))
    sb = lambda n, shape: own.enter_context(nc.sbuf_tensor(f"l0f_{n}", shape, F32))
    w1, w2 = sb("w1", [P, F * P]), sb("w2", [P, F * P])
    h1, h2, w3 = sb("h1", [P, F, F * P]), sb("h2", [P, F, F * P]), sb("w3", [P, F, P])
    s = sb("s", [P, 4, F])
    s3 = sb("s3", [P, P])
    srcs = [(w1, "l0f_w1"), (w2, "l0f_w2"), (h1, "l0f_h1"), (h2, "l0f_h2"), (w3, "l0f_w3"), (s, "l0f_s"),
            (s3, "l0f_s3")]
    feature_major(nc, m, "l0f_turn", xnT, prefetch=[(tile[:], d[src]) for tile, src in srcs])
    with Stage(nc, "l0f") as st:
        gate, hid, mid, y = (st.two(n, [P, F, CH]) for n in ("gate", "hid", "mid", "y"))
        scaled = st.sem("scaled")
        up, silued, hidden, sum1, act1, sum2, act2 = (
            st.sem2(n) for n in ("up", "silued", "hidden", "sum1", "act1", "sum2", "act2"))
        down, scaled_y, added = st.sem2("down"), st.sem2("scaled_y"), st.sem2("added")
        banks = [m.A[0][:, 0:CH], m.A[0][:, CH:2 * CH], m.B[0][:, 0:CH], m.B[0][:, CH:2 * CH]], \
                [m.A[1][:, 0:CH], m.A[1][:, CH:2 * CH], m.B[1][:, 0:CH], m.B[1][:, CH:2 * CH]]
        with nc.Block() as block:
            @block.tensor
            def _(pe):
                with pe.Fori(0, NCH // 2) as it:
                    for j in range(2):
                        x = xnT[:, bass.ds(it * 8 + 4 * j, TPC), :]
                        for o in range(F):
                            if o == 0:
                                pe.wait_ge(scaled_y[j], past(it))
                            if o >= 2:
                                pe.wait_ge(hidden[j], past(it * 4 + o - 1))
                            c = slice(o * P, o * P + P)
                            pe.matmul(banks[j][2 * (o % 2)], w1[:, c], x, start=True, stop=True)
                            pe.matmul(banks[j][2 * (o % 2) + 1], w2[:, c], x, start=True, stop=True)\
                              .then_inc(up[j], 1)
                    for weights, src, ready, done in ((h1, hid, hidden, sum1), (h2, mid, act1, sum2)):
                        for j in range(2):
                            pe.wait_ge(ready[j], past(it * 4 + 4))
                            for o in range(F):
                                for k in range(F):
                                    last = pe.matmul(banks[j][o], weights[:, k, o * P:o * P + P], src[j][:, k],
                                                     start=(k == 0), stop=(k == F - 1))
                                last.then_inc(done[j], 1)
                    for j in range(2):
                        pe.wait_ge(act2[j], past(it * 4 + 4))
                        for t in range(TPC):
                            for k in range(F):
                                last = pe.matmul(banks[j][0][:, t * P:t * P + P], hid[j][:, k, t * P:t * P + P],
                                                 w3[:, k], start=(k == 0), stop=(k == F - 1))
                        last.then_inc(down[j], 1)

            @block.scalar
            def _(act):
                with act.Fori(0, NCH // 2) as it:
                    for j in range(2):
                        for o in range(F):
                            act.wait_ge(up[j], past(it * 4 + o + 1))
                            act.activation(gate[j][:, o], banks[j][2 * (o % 2)], ACT.Silu, scale=s[:, 0, o:o + 1])\
                               .then_inc(silued[j], 1)
                    for n, ready, dst, done in ((2, sum1, mid, act1), (3, sum2, hid, act2)):
                        for j in range(2):
                            for o in range(F):
                                act.wait_ge(ready[j], past(it * 4 + o + 1))
                                act.activation(dst[j][:, o], banks[j][o], ACT.Gelu, scale=s[:, n, o:o + 1])\
                                   .then_inc(done[j], 1)

            @block.vector
            def _(dve):
                dve.tensor_scalar(s3[:], s3[:], m.tanh_g[:, 4:5], None, ALU.mult).then_inc(scaled, 1)
                dve.wait_ge(scaled, 1)
                with dve.Fori(0, NCH // 2) as it:
                    for j in range(2):
                        for o in range(F):
                            dve.wait_ge(silued[j], past(it * 4 + o + 1))
                            dve.scalar_tensor_tensor(hid[j][:, o], banks[j][2 * (o % 2) + 1], s[:, 1, o:o + 1],
                                                     gate[j][:, o], ALU.mult, ALU.mult).then_inc(hidden[j], 1)
                    for j in range(2):
                        dve.wait_ge(down[j], past(it + 1))
                        out = banks[j][0].rearrange("p (t w) -> p t w", t=TPC)
                        z = y[j][:, 0].rearrange("p (t w) -> p t w", t=TPC)
                        dve.tensor_tensor(z, out, repeat_heads(s3[:], TPC), ALU.mult).then_inc(scaled_y[j], 1)
                        dve.wait_ge(scaled_y[j], past(it + 1))
                        add_tiles(dve, m, added[j], it + 1, it, it * 8 + 4 * j, z)


def l2_ffn(nc, m, d, own):
    E = 8
    LOWER, UPPER, CENTER = 0.5 - float(np.log(4.0 / 3.0)), 0.5, 1.0 / float(np.e)
    xnT = own.enter_context(nc.sbuf_tensor("l2f_xnT", [P, NT, P], F32))
    wr = own.enter_context(nc.sbuf_tensor("l2f_wr", [P, E], F32))
    mix = own.enter_context(nc.sbuf_tensor("l2f_mix", [P, NT, E], F32))
    temp = own.enter_context(nc.sbuf_tensor("l2f_temp", [P, 1], F32))
    lower_e = own.enter_context(nc.sbuf_tensor("l2f_lower_e", [P, E, E], F32))
    with Stage(nc, "l2f_in") as st:
        loaded = st.sem("loaded")
        with nc.Block() as block:
            @block.sync
            def _(sp):
                for tile, src in ((wr, "l2f_wr"), (temp, "l2f_temp"), (lower_e, "c_lower_e")):
                    sp.dma_start(tile[:], d[src]).then_inc(loaded, 16)
                sp.wait_ge(loaded, 48)
    wg, wu, wd = (own.enter_context(nc.sbuf_tensor(f"l2f_{n}", [P, E, P], F32)) for n in ("wg", "wu", "wd"))
    feature_major(nc, m, "l2f_turn", xnT, router=(wr, mix),
                  prefetch=[(wg[:], d["l2f_wg"]), (wu[:], d["l2f_wu"]), (wd[:], d["l2f_wd"])])

    with Stage(nc, "route") as st:
        inh, w, fb, mask, dist = (st.sb(n, [P, NT, E]) for n in ("inh", "w", "fb", "mask", "dist"))
        above, equal = st.sb("above", [P, NT, E, E]), st.sb("equal", [P, NT, E, E])
        total, none, some = st.sb("total", [P, NT]), st.sb("none", [P, NT]), st.sb("some", [P, NT])
        flat = lambda x: x[:].rearrange("p t e -> p (t e)")
        step, exped = st.sem("step"), st.sem("exped")
        with nc.Block() as block:
            @block.vector
            def _(dve):
                count = [0]

                def then(ins):
                    count[0] += 1
                    ins.then_inc(step, 1)
                    dve.wait_ge(step, count[0])

                then(dve.reciprocal(temp[:], temp[:]))
                then(dve.tensor_scalar(flat(mix), flat(mix), temp[:], None, ALU.mult))
                dve.wait_ge(exped, 1)
                then(dve.tensor_scalar(flat(inh), flat(inh), 1.0, None, ALU.add))
                then(dve.reciprocal(flat(inh), flat(inh)))
                then(dve.tensor_scalar(flat(mask), flat(inh), LOWER, None, ALU.is_ge))
                then(dve.scalar_tensor_tensor(flat(mask), flat(inh), UPPER, flat(mask), ALU.is_le, ALU.mult))
                then(dve.tensor_scalar(flat(inh), flat(inh), CENTER, None, ALU.subtract))
                then(dve.scalar_tensor_tensor(flat(dist), flat(inh), -1.0, flat(inh), ALU.mult, ALU.max))
                dve.wait_ge(exped, 3)
                then(dve.tensor_tensor(flat(w), flat(w), flat(mask), ALU.mult))
                then(dve.tensor_reduce(total[:], w[:], AX, ALU.add))
                then(dve.tensor_scalar(none[:], total[:], 1e-8, None, ALU.is_lt))
                then(dve.tensor_scalar(some[:], none[:], -1.0, 1.0, ALU.mult, ALU.add))
                mine = fb[:, :, :, None].broadcast_to([P, NT, E, E])
                theirs = fb[:, :, None, :].broadcast_to([P, NT, E, E])
                then(dve.tensor_tensor(above[:], theirs, mine, ALU.is_gt))
                then(dve.tensor_tensor(equal[:], theirs, mine, ALU.is_equal))
                then(dve.tensor_tensor(equal[:], equal[:], lower_e[:, None, :, :].broadcast_to([P, NT, E, E]), ALU.mult))
                then(dve.tensor_tensor(above[:], above[:], equal[:], ALU.add))
                then(dve.tensor_reduce(mask[:], above[:], AX, ALU.add))
                then(dve.scalar_tensor_tensor(flat(fb), flat(mask), 2.0, flat(fb), ALU.is_lt, ALU.mult))
                then(dve.tensor_reduce(total[:], fb[:], AX, ALU.add))
                then(dve.tensor_scalar(total[:], total[:], 1e-8, None, ALU.max))
                then(dve.reciprocal(total[:], total[:]))
                then(dve.tensor_tensor(total[:], total[:], none[:], ALU.mult))
                then(dve.tensor_tensor(fb[:], fb[:], spread_heads(total[:], E), ALU.mult))
                then(dve.tensor_tensor(w[:], w[:], spread_heads(some[:], E), ALU.mult))
                then(dve.tensor_tensor(flat(w), flat(w), flat(fb), ALU.add))
                then(dve.tensor_reduce(total[:], w[:], AX, ALU.add))
                then(dve.tensor_scalar(total[:], total[:], 1e-8, None, ALU.max))
                then(dve.reciprocal(total[:], total[:]))
                then(dve.tensor_scalar(total[:], total[:], m.tanh_g[:, 6:7], None, ALU.mult))
                dve.tensor_tensor(mix[:], w[:], spread_heads(total[:], E), ALU.mult)

            @block.scalar
            def _(act):
                act.wait_ge(step, 2)
                act.activation(inh[:], mix[:], ACT.Exp, scale=-1.0).then_inc(exped, 1)
                act.wait_ge(step, 8)
                act.activation(w[:], dist[:], ACT.Exp, scale=-10.0).then_inc(exped, 1)
                act.activation(fb[:], dist[:], ACT.Exp, scale=-1.0 / 0.3).then_inc(exped, 1)

    with Stage(nc, "l2f") as st:
        gate, hid = st.two("gate", [P, 2, CH]), st.two("hid", [P, 2, CH])
        up, silued, hidden, down = (st.sem2(n) for n in ("up", "silued", "hidden", "down"))
        added = [st.counter(f"added{j}", TPC + 1) for j in range(2)]

        def used(experts):
            return (experts + 1) * TPC + 1

        bank = lambda j, e, n: (m.A, m.B)[e % 2][j][:, n * CH:n * CH + CH]
        with nc.Block() as block:
            def before(it, e):
                return (it, e - 1) if e else (it - 1, E - 1)

            def each_expert(eng, step):
                for e in range(E):
                    step(0, e)
                with eng.Fori(1, CHUNK_PAIRS) as it:
                    for e in range(E):
                        step(it, e)
                step(CHUNK_PAIRS, 0)

            def exists(it):
                return not isinstance(it, int) or 0 <= it < CHUNK_PAIRS

            @block.tensor
            def _(pe):
                def expand(it, e, j):
                    x = xnT[:, bass.ds(it * 8 + 4 * j, TPC), :]
                    pe.wait_ge(added[j], used(it * E + e - 1))
                    pe.matmul(bank(j, e, 0), wg[:, e], x, start=True, stop=True)
                    pe.matmul(bank(j, e, 1), wu[:, e], x, start=True, stop=True).then_inc(up[j], 1)

                def contract(it, e, j):
                    pe.wait_ge(hidden[j], past(it * E + e + 1))
                    for t in range(TPC):
                        last = pe.matmul(bank(j, e, 0)[:, t * P:t * P + P],
                                         hid[j][:, e % 2, t * P:t * P + P], wd[:, e],
                                         start=True, stop=True)
                    last.then_inc(down[j], 1)

                def step(it, e):
                    if exists(it):
                        expand(it, e, 0)
                    if exists(before(it, e)[0]):
                        contract(*before(it, e), 1)
                    if exists(it):
                        expand(it, e, 1)
                        contract(it, e, 0)

                each_expert(pe, step)

            @block.scalar
            def _(act):
                with act.Fori(0, CHUNK_PAIRS) as it:
                    for e in range(E):
                        for j in range(2):
                            act.wait_ge(up[j], past(it * E + e + 1))
                            act.activation(gate[j][:, e % 2], bank(j, e, 0), ACT.Silu).then_inc(silued[j], 1)

            @block.vector
            def _(dve):
                def multiply(it, e, j):
                    dve.wait_ge(silued[j], past(it * E + e + 1))
                    dve.tensor_tensor(hid[j][:, e % 2], bank(j, e, 1), gate[j][:, e % 2], ALU.mult)\
                       .then_inc(hidden[j], 1)

                def add(it, e, j):
                    dve.wait_ge(down[j], past(it * E + e + 1))
                    dve.wait_ge(added[j], used(it * E + e))
                    for t in range(TPC):
                        tile = it * 8 + 4 * j + t
                        dve.scalar_tensor_tensor(m.X[:, tile, :], bank(j, e, 0)[:, t * P:t * P + P],
                                                 mix[:, tile, e:e + 1], m.X[:, tile, :],
                                                 ALU.mult, ALU.add).then_inc(added[j], 1)

                def measure(it, j):
                    dve.wait_ge(added[j], used(it * E + E))
                    for t in range(TPC):
                        tile = it * 8 + 4 * j + t
                        dve.bn_stats(m.S6[:, tile, :], m.X[:, tile, :])

                def step(it, e):
                    if exists(it):
                        multiply(it, e, 0)
                    if exists(before(it, e)[0]):
                        add(*before(it, e), 1)
                        if e == 0:
                            measure(it - 1, 1)
                    if exists(it):
                        multiply(it, e, 1)
                        add(it, e, 0)
                        if e == E - 1:
                            measure(it, 0)

                each_expert(dve, step)


def attention16(nc, m, d, name, projected, gate_at):
    H, W = 16, 8
    E = H // 2
    G = E // 2
    n_pair = 2 * (W + 1)
    with Stage(nc, name) as st:
        wo, bo = st.sb("wo", [P, P]), st.sb("bo", [1, P])
        loads = [(wo[:], d[f"{name}_wo"]), (bo[:], d[f"{name}_bo"])]
        if projected:
            wq, wk, wv = st.sb("wq", [P, P]), st.sb("wk", [P, P]), st.sb("wv", [P, P])
            bq, bk, bv = st.sb("bq", [P, 1]), st.sb("bk", [P, 1]), st.sb("bv", [P, P])
            rows = st.sb("rows", [P, NB], I32)
            scale = st.sb("scale", [P, NB])
            loads += [(x[:], d[f"{name}_{n}"]) for x, n in
                      ((wq, "wq"), (wk, "wk"), (wv, "wv"), (bq, "bq"), (bk, "bk"), (bv, "bv"))]
            loads += [(rows[u * S:u * S + S], d[f"{name}_mask"]) for u in range(2)]
            xnT, kT = st.two("xnT", [P, P]), st.two("kT", [P, P])
        else:
            raw = st.sb("raw", [P, NB, S], I32)
            masks = st.sb("masks", [P, NB, S], BF16)
            loads += [(raw[u * S:u * S + S], d[f"{name}_mask"]) for u in range(2)]
            ctx2 = st.two("ctx2", [P, 2, P])
        xn, ctxT = st.two("xn", [P, P]), st.two("ctxT", [P, P])
        qx = st.two("qx", [P, 2, 2, S])
        kx = st.two("kx", [P, 2, E, S])
        vd = st.two("vd", [P, 2, E, 2, W + 1])
        prob, pT = st.two("prob", [P, H, S]), st.two("pT", [P, 2 * G, P])
        top, inv = st.two("top", [P, H]), st.two("inv", [P, H])
        o, oT = st.two("o", [P, P]), st.two("oT", [P, P])
        loaded, masked, ones_set = st.sem("loaded"), st.sem("masked"), st.sem("ones_set")
        (ctx_in, ctx2_in, normed_x, turned, copied, proj, k_set, q_set, spread, values, scored, max_done, shifted,
         exped, p_turned, p_copied, mixed, inverted, o_done, o_turned, o_copied, out_done, added) = (
            st.sem2(n) for n in ("ctx_in", "ctx2_in", "normed_x", "turned", "copied", "proj", "k_set", "q_set",
                                 "spread", "values", "scored", "max_done", "shifted", "exped", "p_turned",
                                 "p_copied", "mixed", "inverted", "o_done", "o_turned", "o_copied", "out_done",
                                 "added"))
        A, G0, F = [x[:] for x in m.A], [x[:, 0:CH] for x in m.B], [x[:, CH:2 * CH] for x in m.B]
        k_in = kT if projected else ctxT
        n_masked = 5 if projected else 3
        with nc.Block() as block:
            @block.sync
            def _(sp):
                for tile, src in loads:
                    sp.dma_start(tile, src).then_inc(loaded, 16)
                with sp.Fori(0, PAIRS) as it:
                    for j in range(2):
                        sp.wait_ge((proj if projected else spread)[j], past(it))
                        sp.dma_start(ctxT[j][:], d["ctxT"][it * 2 + j]).then_inc(ctx_in[j], 16)
                        if not projected:
                            sp.wait_ge(values[j], past(it))
                            for u in range(2):
                                sp.dma_start(ctx2[j][u * S:u * S + S], d["ctx"][:, bass.ds(it * 4 + 2 * j, 2), :])\
                                  .then_inc(ctx2_in[j], 16)

            @block.gpsimd
            def _(pool):
                for j in range(2):
                    for b in range(2):
                        pool.tensor_copy(vd[j][:, b, :, :, W], repeat_heads(m.half[:], E)).then_inc(ones_set, 1)
                with pool.Fori(0, PAIRS) as it:
                    for j in range(2):
                        if projected:
                            pool.wait_ge(k_set[j], past(it + 1))
                        else:
                            pool.wait_ge(ctx_in[j], past(it * 16 + 16))
                        pool.wait_ge(scored[j], past(it))
                        for b in range(2):
                            last = pool.tensor_tensor(kx[j][:, b], repeat_heads(k_in[j][:, b * S:b * S + S], E),
                                                      spread_heads(m.head_of_8[:], S), ALU.mult)
                        last.then_inc(spread[j], 1)
                        if not projected:
                            pool.wait_ge(ctx2_in[j], past(it * 32 + 32))
                            pool.wait_ge(mixed[j], past(it))
                            for b in range(2):
                                last = pool.tensor_tensor(
                                    vd[j][:, b, :, :, 0:W], ctx2[j][:, b].rearrange("p (g u w) -> p g u w", g=E, u=2),
                                    m.half[:, None, :, None].broadcast_to([P, E, 2, W]), ALU.mult)
                            last.then_inc(values[j], 1)

            @block.vector
            def _(dve):
                def norm_x(it, j):
                    dve.wait_ge(turned[j], past(it))
                    normed(dve, m, xn[j][:], it * 2 + j).then_inc(normed_x[j], 1)

                def keep_v(it, j):
                    dve.wait_ge(q_set[j], past(it + 1))
                    dve.wait_ge(mixed[j], past(it))
                    v = F[j][:, 2 * P:4 * P].rearrange("p (b g u w) -> p b g u w", b=2, g=E, u=2)
                    b_v = bv[:].rearrange("p (g u w) -> p g u w", g=E, u=2)
                    for u in range(2):
                        r = slice(u * S, u * S + S)
                        last = dve.tensor_tensor(vd[j][r, :, :, u, 0:W], v[r, :, :, u],
                                                 b_v[r, None, :, u].broadcast_to([S, 2, E, W]), ALU.add)
                    last.then_inc(values[j], 1)

                def shift(it, j):
                    s = per_head(A[j], H, S)
                    dve.wait_ge(scored[j], past(it + 1))
                    dve.tensor_reduce(top[j][:], s, AX, ALU.max).then_inc(max_done[j], 1)
                    dve.wait_ge(max_done[j], past(it + 1))
                    dve.wait_ge(p_turned[j], past(it))
                    dve.tensor_tensor(prob[j][:], s, spread_heads(top[j][:], S), ALU.subtract)\
                       .then_inc(shifted[j], 1)

                def outputs(it, j):
                    out = G0[j][:, 0:H * (W + 1)].rearrange("p (h w) -> p h w", h=H)
                    dve.wait_ge(mixed[j], past(it + 1))
                    dve.reciprocal(inv[j][:], out[:, :, W]).then_inc(inverted[j], 1)
                    dve.wait_ge(inverted[j], past(it + 1))
                    dve.wait_ge(o_turned[j], past(it))
                    dve.tensor_tensor(per_head(o[j][:], H, W), out[:, :, 0:W], spread_heads(inv[j][:], W),
                                      ALU.mult).then_inc(o_done[j], 1)

                def update(it, j):
                    t = it * 2 + j
                    dve.wait_ge(out_done[j], past(it + 1))
                    dve.scalar_tensor_tensor(m.X[:, t, :], G0[j][:, P:2 * P],
                                             m.tanh_g[:, gate_at:gate_at + 1], m.X[:, t, :],
                                             ALU.mult, ALU.add).then_inc(added[j], 1)
                    dve.wait_ge(added[j], past(it + 1))
                    dve.bn_stats(m.S6[:, t, :], m.X[:, t, :])

                for j in range(2):
                    if projected:
                        dve.memset(vd[j][:, :, :, :, 0:W], 0.0).then_inc(masked, 1)
                    dve.memset(qx[j][:], 0.0).then_inc(masked, 1)
                dve.wait_ge(loaded, 16 * len(loads))
                if projected:
                    dve.tensor_scalar(scale[:], rows[:], 0, float(W) ** -0.5, ALU.not_equal, ALU.mult)\
                       .then_inc(masked, 1)
                else:
                    dve.tensor_scalar(masks[:], raw[:], 0, -1e20, ALU.is_equal, ALU.mult).then_inc(masked, 1)
                dve.wait_ge(masked, n_masked)
                dve.wait_ge(ones_set, 4)

                def step(it, j):
                    at(it, j, 2, norm_x)
                    at(it, j, 0, shift)
                    at(it, j, -2, update)
                    at(it, j, -1, outputs)
                    if projected:
                        at(it, j, 1, keep_v)

                steps(dve, step)

            @block.scalar
            def _(act):
                def keep_q(j, convert):
                    for u in range(2):
                        r = slice(u * S, u * S + S)
                        last = convert(qx[j][r, :, u], F[j][r, 0:P].rearrange("p (b q) -> p b q", b=2), u)
                    return last

                def copy_x(it, j):
                    act.wait_ge(turned[j], past(it + 1))
                    if projected:
                        act.wait_ge(proj[j], past(it))
                        act.copy(xnT[j][:], F[j][:, 0:P]).then_inc(copied[j], 1)
                    else:
                        act.wait_ge(scored[j], past(it))
                        keep_q(j, lambda dst, src, u: act.copy(dst, src)).then_inc(q_set[j], 1)

                def set_k(it, j):
                    act.wait_ge(turned[j], past(it + 1))
                    act.wait_ge(spread[j], past(it))
                    act.activation(kT[j][:], F[j][:, P:2 * P], ACT.Identity, bias=bk[:]).then_inc(k_set[j], 1)

                def set_q(it, j):
                    act.wait_ge(proj[j], past(it + 1))
                    act.wait_ge(scored[j], past(it))
                    keep_q(j, lambda dst, src, u: act.activation(dst, src, ACT.Identity, bias=bq[u * S:u * S + S]))\
                        .then_inc(q_set[j], 1)

                def exps(it, j):
                    act.wait_ge(shifted[j], past(it + 1))
                    if projected:
                        for b in range(2):
                            p = prob[j][:, b * E:b * E + E]
                            last = act.activation(p, p, ACT.Exp, scale=scale[:, bass.ds(it * 4 + 2 * j + b, 1)])
                    else:
                        last = act.activation(prob[j][:], prob[j][:], ACT.Exp, scale=float(P) ** -0.5)
                    last.then_inc(exped[j], 1)

                def copy_p(it, j):
                    act.wait_ge(p_turned[j], past(it + 1))
                    act.wait_ge(mixed[j], past(it))
                    act.copy(pT[j][:], A[j].rearrange("p (g q) -> p g q", g=2 * G)).then_inc(p_copied[j], 1)

                def copy_o(it, j):
                    act.wait_ge(o_turned[j], past(it + 1))
                    act.wait_ge(out_done[j], past(it))
                    act.copy(oT[j][:], G0[j][:, 0:P]).then_inc(o_copied[j], 1)

                act.wait_ge(loaded, 16 * len(loads))
                act.wait_ge(masked, n_masked)

                def step(it, j):
                    at(it, j, -2, copy_o)
                    at(it, j, -1, copy_p)
                    if projected:
                        at(it, j, 1, set_q)
                    at(it, j, 2, copy_x)
                    if projected:
                        at(it, j, 2, set_k)
                    at(it, j, 0, exps)

                steps(act, step)

            @block.tensor
            def _(pe):
                def turn_x(it, j):
                    pe.wait_ge(normed_x[j], past(it + 1))
                    if projected:
                        pe.wait_ge(values[j], past(it))
                        pe.wait_ge(ctx_in[j], past(it * 16 + 16))
                        pe.matmul(F[j][:, P:2 * P], wk[:], ctxT[j][:], start=True, stop=True)
                        for b in range(2):
                            for u in range(2):
                                pe.matmul(F[j][u * S:u * S + S, (2 + b) * P:(3 + b) * P],
                                          ctxT[j][:, b * S:b * S + S], wv[:], start=True, stop=True)
                    else:
                        pe.wait_ge(q_set[j], past(it))
                    pe.transpose(F[j][:, 0:P], xn[j][:], m.ident[:]).then_inc(turned[j], 1)

                def project_q(it, j):
                    pe.wait_ge(copied[j], past(it + 1))
                    pe.wait_ge(k_set[j], past(it + 1))
                    pe.matmul(F[j][:, 0:P], wq[:], xnT[j][:], start=True, stop=True).then_inc(proj[j], 1)

                def scores(it, j):
                    pe.wait_ge(p_copied[j], past(it))
                    pe.wait_ge(spread[j], past(it + 1))
                    pe.wait_ge(q_set[j], past(it + 1))
                    for b in range(2):
                        s = A[j][:, b * CH:b * CH + CH]
                        if not projected:
                            pe.matmul(s, m.ident_bf[:], repeat_heads(masks[:, it * 4 + 2 * j + b, :], E),
                                      start=True, stop=False)
                        last = pe.matmul(s, qx[j][:, b].rearrange("p u q -> p (u q)"), kx[j][:, b],
                                         start=projected, stop=True)
                    last.then_inc(scored[j], 1)

                def turn_p(it, j):
                    pe.wait_ge(exped[j], past(it + 1))
                    p = prob[j][:].rearrange("p h k -> p (h k)")
                    for g in range(2 * G):
                        last = pe.transpose(A[j][:, g * P:g * P + P], p[:, g * P:g * P + P], m.ident[:])
                    last.then_inc(p_turned[j], 1)

                def mix(it, j):
                    pe.wait_ge(p_copied[j], past(it + 1))
                    pe.wait_ge(values[j], past(it + 1))
                    pe.wait_ge(added[j], past(it))
                    for b in range(2):
                        for u in range(2):
                            for g in range(G):
                                pair = u * G + g
                                last = pe.matmul(G0[j][b * S:b * S + S, pair * n_pair:(pair + 1) * n_pair],
                                                 pT[j][:, b * G + g, u * S:u * S + S],
                                                 vd[j][:, b, pair].rearrange("p u w -> p (u w)"),
                                                 start=True, stop=True)
                    last.then_inc(mixed[j], 1)

                def turn_o(it, j):
                    pe.wait_ge(o_done[j], past(it + 1))
                    pe.transpose(G0[j][:, 0:P], o[j][:], m.ident[:]).then_inc(o_turned[j], 1)

                def project_o(it, j):
                    pe.wait_ge(o_copied[j], past(it + 1))
                    y = G0[j][:, P:2 * P]
                    pe.matmul(y, m.ones_row[:], bo[:], start=True, stop=False)
                    pe.matmul(y, oT[j][:], wo[:], start=False, stop=True).then_inc(out_done[j], 1)

                pe.wait_ge(loaded, 16 * len(loads))
                pe.wait_ge(masked, n_masked)
                pe.wait_ge(ones_set, 4)

                def step(it, j):
                    if projected:
                        at(it, j, 1, project_q)
                    at(it, j, 0, scores)
                    at(it, j, -2, turn_o)
                    at(it, j, -1, turn_p)
                    at(it, j, 2, turn_x)
                    at(it, j, -2, project_o)
                    at(it, j, -1, mix)

                steps(pe, step)


def l1_xattn(nc, m, d, own):
    attention16(nc, m, d, "l1x", True, 1)


def l2_xattn(nc, m, d, own):
    attention16(nc, m, d, "l2x", False, 2)


def l3_xattn(nc, m, d, own):
    with Stage(nc, "l3x") as st:
        wq, wk, bq, bk = st.sb("wq", [P, P]), st.sb("wk", [P, P]), st.sb("bq", [P, 1]), st.sb("bk", [P, 1])
        raw = st.sb("raw", [P, NT, S], I32)
        factor, extra = st.sb("factor", [P, NT, S]), st.sb("extra", [P, NT, S])
        loads = [(wq, "l3x_wq"), (wk, "l3x_wk"), (bq, "l3x_bq"), (bk, "l3x_bk"), (raw, "l3x_mask")]
        xn, xnT, qT, kT = (st.two(n, [P, P]) for n in ("xn", "xnT", "qT", "kT"))
        ctxT = st.sb("ctxT", [P, NT, P])
        val = st.sb("val", [P, NT, P])
        score = st.two("score", [P, S])
        prob, pT = st.two("prob", [P, P]), st.two("pT", [P, P])
        top, total, inv = (st.two(n, [P, 1]) for n in ("top", "total", "inv"))
        loaded, masked, zeroed = st.sem("loaded"), st.sem("masked"), st.sem("zeroed")
        arrived = st.counter("arrived")
        (ctx_in, normed_x, turned, copied, proj, q_set, scored, times, plus, max_done, exped,
         p_turned, p_copied, mixed, inverted, gated, added) = (
            st.sem2(n) for n in ("ctx_in", "normed_x", "turned", "copied", "proj", "q_set", "scored",
                                 "times", "plus", "max_done", "exped", "p_turned", "p_copied", "mixed",
                                 "inverted", "gated", "added"))
        with nc.Block() as block:
            @block.sync
            def _(sp):
                for tile, src in loads:
                    sp.dma_start(tile[:], d[src]).then_inc(loaded, 16)
                parts = 8
                tiles = NT // parts
                with sp.Fori(0, parts) as part:
                    sp.dma_start(ctxT[:, bass.ds(part * tiles, tiles), :],
                                 d["ctxT"][bass.ds(part * tiles, tiles)].rearrange("t p k -> p t k"))\
                      .then_inc(arrived, 16)
                    sp.dma_start(val[:, bass.ds(part * tiles, tiles), :],
                                 d["ctx_rows"][:, bass.ds(part * tiles, tiles), :]).then_inc(arrived, 16)
                    sp.wait_ge(arrived, past(part * 32 + 32))
                    for j in range(2):
                        sp.sem_inc(ctx_in[j], tiles // 2)

            @block.vector
            def _(dve):
                def norm_x(it, j):
                    dve.wait_ge(turned[j], past(it))
                    normed(dve, m, xn[j][:], it * 2 + j).then_inc(normed_x[j], 1)

                def weigh(it, j):
                    t = it * 2 + j
                    dve.wait_ge(scored[j], past(it + 1))
                    dve.wait_ge(exped[j], past(it))
                    dve.tensor_tensor(score[j][:], m.B[j][:, 0:S], factor[:, t, :], ALU.mult).then_inc(times[j], 1)
                    dve.wait_ge(times[j], past(it + 1))
                    dve.tensor_tensor(score[j][:], score[j][:], extra[:, t, :], ALU.add).then_inc(plus[j], 1)
                    dve.wait_ge(plus[j], past(it + 1))
                    dve.tensor_reduce(top[j][:], score[j][:], AX, ALU.max, negate=True).then_inc(max_done[j], 1)

                def invert(it, j):
                    dve.wait_ge(exped[j], past(it + 1))
                    dve.reciprocal(inv[j][:], total[j][:]).then_inc(inverted[j], 1)
                    dve.wait_ge(inverted[j], past(it + 1))
                    dve.tensor_scalar(inv[j][:], inv[j][:], m.tanh_g[:, 3:4], None, ALU.mult).then_inc(gated[j], 1)

                def update(it, j):
                    t = it * 2 + j
                    dve.wait_ge(gated[j], past(it + 1))
                    dve.wait_ge(mixed[j], past(it + 1))
                    dve.scalar_tensor_tensor(m.X[:, t, :], m.B[j][:, 2 * P:3 * P], inv[j][:], m.X[:, t, :],
                                             ALU.mult, ALU.add).then_inc(added[j], 1)

                def measure(it, j):
                    dve.wait_ge(added[j], past(it + 1))
                    dve.bn_stats(m.S6[:, it * 2 + j, :], m.X[:, it * 2 + j, :])

                for j in range(2):
                    dve.memset(prob[j][:], 0.0).then_inc(zeroed, 1)
                dve.wait_ge(loaded, 16 * len(loads))
                dve.tensor_scalar(factor[:], raw[:], float(P) ** -0.5, None, ALU.mult)
                dve.tensor_scalar(extra[:], raw[:], 0, -1e9, ALU.is_equal, ALU.mult).then_inc(masked, 1)
                dve.wait_ge(masked, 1)

                def step(it, j):
                    at(it, j, 2, norm_x)
                    at(it, j, -2, update)
                    at(it, j, -1, invert)
                    at(it, j, 0, weigh)
                    at(it, j, -2, measure)

                steps(dve, step)

            @block.scalar
            def _(act):
                def copy_x(it, j):
                    act.wait_ge(turned[j], past(it + 1))
                    act.wait_ge(proj[j], past(it))
                    act.copy(xnT[j][:], m.A[j][:, 0:P]).then_inc(copied[j], 1)

                def set_qk(it, j):
                    act.wait_ge(proj[j], past(it + 1))
                    act.wait_ge(scored[j], past(it))
                    act.activation(kT[j][:], m.A[j][:, P:2 * P], ACT.Identity, bias=bk[:])
                    act.activation(qT[j][:], m.A[j][:, 2 * P:3 * P], ACT.Identity, bias=bq[:]).then_inc(q_set[j], 1)

                def exps(it, j):
                    act.wait_ge(max_done[j], past(it + 1))
                    act.wait_ge(inverted[j], past(it))
                    act.wait_ge(p_turned[j], past(it))
                    for b in range(2):
                        r = slice(b * S, b * S + S)
                        last = act.activation(prob[j][r, r], score[j][r], ACT.Exp, bias=top[j][r],
                                              accum_out=total[j][r])
                    last.then_inc(exped[j], 1)

                def copy_p(it, j):
                    act.wait_ge(p_turned[j], past(it + 1))
                    act.wait_ge(mixed[j], past(it))
                    act.copy(pT[j][:], m.B[j][:, CH:CH + P]).then_inc(p_copied[j], 1)

                act.wait_ge(loaded, 16 * len(loads))
                act.wait_ge(zeroed, 2)

                def step(it, j):
                    at(it, j, 1, set_qk)
                    at(it, j, -1, copy_p)
                    at(it, j, 2, copy_x)
                    at(it, j, 0, exps)

                steps(act, step)

            @block.tensor
            def _(pe):
                def turn_x(it, j):
                    pe.wait_ge(normed_x[j], past(it + 1))
                    pe.wait_ge(q_set[j], past(it))
                    pe.transpose(m.A[j][:, 0:P], xn[j][:], m.ident[:]).then_inc(turned[j], 1)

                def project(it, j):
                    pe.wait_ge(ctx_in[j], past(it + 1))
                    pe.wait_ge(copied[j], past(it + 1))
                    pe.matmul(m.A[j][:, P:2 * P], wk[:], ctxT[:, it * 2 + j, :], start=True, stop=True)
                    pe.matmul(m.A[j][:, 2 * P:3 * P], wq[:], xnT[j][:], start=True, stop=True).then_inc(proj[j], 1)

                def scores(it, j):
                    pe.wait_ge(q_set[j], past(it + 1))
                    pe.wait_ge(added[j], past(it))
                    for b in range(2):
                        last = pe.matmul(m.B[j][b * S:b * S + S, 0:S], qT[j][:, b * S:b * S + S],
                                         kT[j][:, b * S:b * S + S], start=True, stop=True)
                    last.then_inc(scored[j], 1)

                def turn_p(it, j):
                    pe.wait_ge(exped[j], past(it + 1))
                    pe.transpose(m.B[j][:, CH:CH + P], prob[j][:], m.ident[:]).then_inc(p_turned[j], 1)

                def mix(it, j):
                    pe.wait_ge(p_copied[j], past(it + 1))
                    pe.matmul(m.B[j][:, 2 * P:3 * P], pT[j][:], val[:, it * 2 + j, :], start=True, stop=True)\
                      .then_inc(mixed[j], 1)

                pe.wait_ge(loaded, 16 * len(loads))
                pe.wait_ge(zeroed, 2)

                def step(it, j):
                    at(it, j, 1, project)
                    at(it, j, 0, scores)
                    at(it, j, -1, turn_p)
                    at(it, j, 2, turn_x)
                    at(it, j, -1, mix)

                steps(pe, step)


def quantizer(nc, m, name, maxima, scale, inverse):
    with Stage(nc, name) as st:
        own, all_ = st.sb("own", [P, 1]), st.sb("all", [P, 1])
        own_max, all_max, step = st.sem("own_max"), st.sem("all_max"), st.sem("step")
        with nc.Block() as block:
            @block.vector
            def _(dve):
                dve.tensor_reduce(own[:], maxima, AX, ALU.max).then_inc(own_max, 1)
                dve.wait_ge(all_max, 1)
                dve.tensor_scalar(scale, all_[:], 1.0 / 32767.0, 1e-12, ALU.mult, ALU.max).then_inc(step, 1)
                dve.wait_ge(step, 1)
                dve.reciprocal(inverse, scale)

            @block.gpsimd
            def _(pool):
                pool.wait_ge(own_max, 1)
                pool.partition_all_reduce(all_[:], own[:], P, bass.bass_isa.ReduceOp.max).then_inc(all_max, 1)


def l1_ffn(nc, m, d, own):
    F = 3
    BLOCK = 32
    NBL = 3 * F * P // BLOCK
    sb = lambda n, s, dt=F32: own.enter_context(nc.sbuf_tensor("l1f_" + n, s, dt))
    wT = sb("wT", [P, 3 * F, P])
    xT = sb("xT", [P, NT, P])
    upq, gateq = sb("upq", [P, F, NT * P], I16), sb("gateq", [P, F, NT * P], I16)
    maxima = sb("maxima", [P, 2, NCH * F])
    sc = sb("sc", [P, 16])
    rnd = sb("rnd", [P, 1])
    col = lambda n: sc[:, n:n + 1]
    X_S, X_R, U_S, U_R, G_S, G_R, H_S, H_R, O_S, O_R, TMP, GH_R, O_F, GATE, O_U = range(15)
    banks = [[r[j][:, h * CH:h * CH + CH] for r in (m.A, m.B) for h in range(2)] for j in range(2)]

    with Stage(nc, "l1f_w") as st:
        w, q = st.sb("w", [P, 3 * F * P]), st.sb("q", [P, 3 * F * P])
        big, inv = st.sb("big", [P, NBL]), st.sb("inv", [P, NBL])
        loaded, step, turned, ready = st.sem("loaded"), st.sem("step"), st.sem("turned"), st.sem("ready")
        with nc.Block() as block:
            @block.sync
            def _(sp):
                sp.dma_start(w[:], d["l1f_w"]).then_inc(loaded, 16)

            @block.vector
            def _(dve):
                blocks = lambda x: x[:].rearrange("p (n k) -> p n k", k=BLOCK)
                count = [0]

                def then(ins):
                    count[0] += 1
                    ins.then_inc(step, 1)
                    dve.wait_ge(step, count[0])

                then(dve.memset(rnd[:], ROUND))
                dve.wait_ge(loaded, 16)
                then(dve.tensor_reduce(big[:], blocks(w), AX, ALU.max, apply_absolute_value=True))
                then(dve.tensor_scalar(big[:], big[:], 1.0 / 7.0, 1e-12, ALU.mult, ALU.max))
                then(dve.reciprocal(inv[:], big[:]))
                then(dve.tensor_tensor(blocks(q), blocks(w), spread_heads(inv[:], BLOCK), ALU.mult))
                then(dve.tensor_scalar(q[:], q[:], 7.0, -8.0, ALU.min, ALU.max))
                then(dve.tensor_scalar(q[:], q[:], ROUND, None, ALU.add))
                then(dve.tensor_scalar(q[:], q[:], -ROUND, None, ALU.add))
                dve.tensor_tensor(blocks(q), blocks(q), spread_heads(big[:], BLOCK), ALU.mult).then_inc(ready, 1)
                dve.wait_ge(turned, 1)
                for n in range(3 * F):
                    dve.tensor_copy(wT[:, n], banks[n % 2][n // 2 % 4][:, n // 8 * P:n // 8 * P + P])

            @block.tensor
            def _(pe):
                pe.wait_ge(ready, 1)
                for n in range(3 * F):
                    last = pe.transpose(banks[n % 2][n // 2 % 4][:, n // 8 * P:n // 8 * P + P],
                                        q[:, n * P:n * P + P], m.ident[:])
                last.then_inc(turned, 1)

    with Stage(nc, "l1f_xmax") as st:
        ends = st.sb("ends", [P, 2, NT])
        found = st.sem("found")
        spread_mean = m.mean[:, None, :].broadcast_to([P, 2, NT])
        spread_rstd = m.rstd[:, None, :].broadcast_to([P, 2, NT])
        with nc.Block() as block:
            @block.vector
            def _(dve):
                dve.tensor_reduce(ends[:, 0], m.X[:], AX, ALU.max)
                dve.tensor_reduce(ends[:, 1], m.X[:], AX, ALU.min).then_inc(found, 1)
                dve.wait_ge(found, 1)
                dve.tensor_tensor(ends[:], ends[:], spread_mean, ALU.subtract).then_inc(found, 1)
                dve.wait_ge(found, 2)
                dve.tensor_tensor(ends[:], ends[:], spread_rstd, ALU.mult).then_inc(found, 1)
                dve.wait_ge(found, 3)
        quantizer(nc, m, "l1f_xs", ends[:].rearrange("p n t -> p (n t)"), col(X_S), col(X_R))

    with Stage(nc, "l1f_x") as st:
        xn, xr = st.two("xn", [P, TPC, P]), st.two("xr", [P, TPC, P])
        normed_x, rounded, quantized, turned, copied = (
            st.sem2(n) for n in ("normed_x", "rounded", "quantized", "turned", "copied"))
        bank = [m.A[j][:, 0:CH].rearrange("p (t k) -> p t k", t=TPC) for j in range(2)]
        with nc.Block() as block:
            @block.vector
            def _(dve):
                def norm_x(it, j):
                    dve.wait_ge(rounded[j], past(it))
                    normed_chunk(dve, m, xn[j], it * 8 + 4 * j).then_inc(normed_x[j], 1)

                def quantize(it, j):
                    dve.wait_ge(rounded[j], past(it + 1))
                    dve.tensor_scalar(xr[j][:], xr[j][:], -ROUND, col(X_S), ALU.add, ALU.mult).then_inc(quantized[j], 1)

                def step(it, j):
                    at(it, j, 1, norm_x, CHUNK_PAIRS)
                    at(it, j, 0, quantize, CHUNK_PAIRS)

                steps(dve, step, CHUNK_PAIRS)

            @block.tensor
            def _(pe):
                def turn(it, j):
                    pe.wait_ge(quantized[j], past(it + 1))
                    pe.wait_ge(copied[j], past(it))
                    for t in range(TPC):
                        last = pe.transpose(bank[j][:, t], xr[j][:, t], m.ident[:])
                    last.then_inc(turned[j], 1)

                def step(it, j):
                    at(it, j, 0, turn, CHUNK_PAIRS)

                steps(pe, step, CHUNK_PAIRS)

            @block.scalar
            def _(act):
                def scale_and_round(it, j):
                    act.wait_ge(normed_x[j], past(it + 1))
                    act.wait_ge(turned[j], past(it))
                    act.activation(xr[j][:], xn[j][:], ACT.Identity, scale=col(X_R), bias=rnd[:]).then_inc(rounded[j], 1)

                def copy_x(it, j):
                    act.wait_ge(turned[j], past(it + 1))
                    act.copy(xT[:, bass.ds(it * 8 + 4 * j, TPC), :], bank[j]).then_inc(copied[j], 1)

                def step(it, j):
                    at(it, j, 1, scale_and_round, CHUNK_PAIRS)
                    at(it, j, 0, copy_x, CHUNK_PAIRS)

                steps(act, step, CHUNK_PAIRS)

    with Stage(nc, "l1f_ugmax") as st:
        made, seen = st.sem2("made"), st.sem2("seen")
        with nc.Block() as block:
            @block.tensor
            def _(pe):
                with pe.Fori(0, NCH) as it:
                    x = xT[:, bass.ds(it * TPC, TPC), :]
                    for o in range(F):
                        for n in range(2):
                            pe.wait_ge(seen[n], past(it * F))
                            pe.matmul(banks[n][o], wT[:, n * F + o], x, start=True, stop=True).then_inc(made[n], 1)

            @block.vector
            def _(dve):
                with dve.Fori(0, NCH) as it:
                    for o in range(F):
                        for n in range(2):
                            dve.wait_ge(made[n], past(it * F + o + 1))
                            dve.tensor_reduce(maxima[:, n, bass.ds(it * F + o, 1)], banks[n][o], AX, ALU.max,
                                              apply_absolute_value=True).then_inc(seen[n], 1)
    quantizer(nc, m, "l1f_us", maxima[:, 0], col(U_S), col(U_R))
    quantizer(nc, m, "l1f_gs", maxima[:, 1], col(G_S), col(G_R))

    def tokens(t, o, it):
        return t[:, o, bass.ds(it * CH, CH)]

    def done(c, o):
        return c * F + o + 1 + F

    def freed(c, o):
        return c * F + o + 1

    def lagging(c, lag, work, *args):
        if not isinstance(c, int) or 0 <= c + lag < NCH:
            work(c + lag, *args)

    def each_chunk(eng, step):
        for c in range(2):
            for o in range(F):
                step(c, o)
        with eng.Fori(2, NCH) as c:
            for o in range(F):
                step(c, o)
        for c in range(NCH, NCH + 2):
            for o in range(F):
                step(c, o)

    POOL_PARTS = (1, 2)

    with Stage(nc, "l1f_ug") as st:
        ur, gr, sig, h = (st.sb(n, [P, F, CH]) for n in ("ur", "gr", "sig", "h"))
        made, up_rounded, gate_rounded, up_kept, gate_kept, siged, rounded, clipped, seen = (
            st.counter(n, F) for n in ("made", "up_rounded", "gate_rounded", "up_kept", "gate_kept", "siged", "rounded",
                                    "clipped", "seen"))
        times, spread = [st.counter(f"times{o}") for o in range(F)], st.counter("spread")
        with nc.Block() as block:
            @block.tensor
            def _(pe):
                with pe.Fori(0, NCH) as it:
                    x = xT[:, bass.ds(it * TPC, TPC), :]
                    for o in range(F):
                        pe.wait_ge(gate_rounded, freed(it, o))
                        pe.matmul(banks[0][o], wT[:, o], x, start=True, stop=True)
                        pe.matmul(banks[1][o], wT[:, F + o], x, start=True, stop=True).then_inc(made, 1)

            @block.scalar
            def _(act):
                def round_both(c, o):
                    act.wait_ge(made, done(c, o))
                    act.wait_ge(up_kept, freed(c, o))
                    act.activation(ur[:, o], banks[0][o], ACT.Identity, scale=col(U_R), bias=rnd[:])\
                       .then_inc(up_rounded, 1)
                    act.wait_ge(gate_kept, freed(c, o))
                    act.activation(gr[:, o], banks[1][o], ACT.Identity, scale=col(G_R), bias=rnd[:])\
                       .then_inc(gate_rounded, 1)

                def sigmoid(c, o):
                    act.wait_ge(gate_kept, done(c, o))
                    act.wait_ge(times[o], past(c))
                    act.activation(sig[:, o], tokens(gateq, o, c), ACT.Sigmoid, scale=col(G_S)).then_inc(siged, 1)

                def step(c, o):
                    lagging(c, 0, round_both, o)
                    lagging(c, -1, sigmoid, o)

                each_chunk(act, step)

            @block.vector
            def _(dve):
                def keep(c, o, rounded_in, src, dst, kept):
                    dve.wait_ge(rounded_in, done(c, o))
                    dve.tensor_scalar(tokens(dst, o, c), src[:, o], -ROUND, 32767.0, ALU.add, ALU.min).then_inc(kept, 1)

                def round_sigmoid(c, o):
                    dve.wait_ge(siged, done(c, o))
                    dve.tensor_scalar(sig[:, o], sig[:, o], 65536.0, ROUND, ALU.mult, ALU.add).then_inc(rounded, 1)

                def clip_sigmoid(c, o):
                    dve.wait_ge(rounded, done(c, o))
                    dve.tensor_scalar(sig[:, o], sig[:, o], ROUND + 65535.0, -ROUND, ALU.min, ALU.add)\
                       .then_inc(clipped, 1)

                def multiply_sigmoid(c, o):
                    if o not in POOL_PARTS:
                        dve.wait_ge(clipped, done(c, o))
                        dve.wait_ge(seen, freed(c, o))
                        dve.tensor_tensor(h[:, o], sig[:, o], tokens(gateq, o, c), ALU.mult).then_inc(times[o], 1)

                def find(c, o):
                    dve.wait_ge(times[o], past(c + 1))
                    dve.tensor_reduce(maxima[:, 0, bass.ds(c * F + o, 1)], h[:, o], AX, ALU.max,
                                      apply_absolute_value=True).then_inc(seen, 1)

                def step(c, o):
                    lagging(c, 0, keep, o, gate_rounded, gr, gateq, gate_kept)
                    lagging(c, -1, round_sigmoid, o)
                    lagging(c, 0, keep, o, up_rounded, ur, upq, up_kept)
                    lagging(c, -1, clip_sigmoid, o)
                    lagging(c, -2, find, o)
                    lagging(c, -1, multiply_sigmoid, o)

                each_chunk(dve, step)

            @block.gpsimd
            def _(pool):
                with pool.Fori(0, NCH) as it:
                    for o in POOL_PARTS:
                        pool.wait_ge(gate_kept, done(it, o))
                        pool.wait_ge(seen, freed(it, o))
                        pool.tensor_copy(h[:, o], tokens(gateq, o, it)).then_inc(spread, 1)
                        pool.wait_ge(clipped, done(it, o))
                        pool.wait_ge(spread, past(it * len(POOL_PARTS) + o))
                        pool.tensor_tensor(h[:, o], sig[:, o], h[:, o], ALU.mult).then_inc(times[o], 1)

    def small(name, *ops):
        with Stage(nc, name) as st:
            step = st.sem("step")
            with nc.Block() as block:
                @block.vector
                def _(dve):
                    for n, op in enumerate(ops):
                        op(dve).then_inc(step, 1)
                        dve.wait_ge(step, n + 1)

    small("l1f_hunit",
          lambda dve: dve.tensor_scalar(col(TMP), col(G_S), 1.0 / 65536.0, None, ALU.mult),
          lambda dve: dve.tensor_scalar(maxima[:, 0], maxima[:, 0], col(TMP), None, ALU.mult))
    quantizer(nc, m, "l1f_hs", maxima[:, 0], col(H_S), col(H_R))
    small("l1f_hfactor",
          lambda dve: dve.tensor_scalar(col(GH_R), col(TMP), col(H_R), None, ALU.mult),
          lambda dve: dve.tensor_scalar(col(O_U), col(H_S), col(U_S), None, ALU.mult))

    with Stage(nc, "l1f_h") as st:
        sig, h, hr, prod = (st.sb(n, [P, F, CH]) for n in ("sig", "h", "hr", "prod"))
        siged, rounded, clipped, h_rounded, kept, product, seen = (
            st.counter(n, F) for n in ("siged", "rounded", "clipped", "h_rounded", "kept", "product", "seen"))
        times, spread = [st.counter(f"times{o}") for o in range(F)], st.counter("spread")
        with nc.Block() as block:
            @block.scalar
            def _(act):
                def sigmoid(c, o):
                    act.wait_ge(times[o], past(c))
                    act.activation(sig[:, o], tokens(gateq, o, c), ACT.Sigmoid, scale=col(G_S)).then_inc(siged, 1)

                def round_h(c, o):
                    act.wait_ge(times[o], past(c + 1))
                    act.wait_ge(product, freed(c, o))
                    act.wait_ge(kept, freed(c, o))
                    act.activation(hr[:, o], h[:, o], ACT.Identity, scale=col(GH_R), bias=rnd[:])\
                       .then_inc(h_rounded, 1)

                def step(c, o):
                    lagging(c, 0, sigmoid, o)
                    lagging(c, -1, round_h, o)

                each_chunk(act, step)

            @block.vector
            def _(dve):
                def round_sigmoid(c, o):
                    dve.wait_ge(siged, done(c, o))
                    dve.tensor_scalar(sig[:, o], sig[:, o], 65536.0, ROUND, ALU.mult, ALU.add).then_inc(rounded, 1)

                def clip_sigmoid(c, o):
                    dve.wait_ge(rounded, done(c, o))
                    dve.tensor_scalar(sig[:, o], sig[:, o], ROUND + 65535.0, -ROUND, ALU.min, ALU.add)\
                       .then_inc(clipped, 1)

                def multiply(c, o):
                    dve.wait_ge(h_rounded, done(c, o))
                    dve.wait_ge(seen, freed(c, o))
                    dve.scalar_tensor_tensor(prod[:, o], hr[:, o], -ROUND, tokens(upq, o, c), ALU.add, ALU.mult)\
                       .then_inc(product, 1)
                    dve.tensor_scalar(tokens(gateq, o, c), hr[:, o], -ROUND, 32767.0, ALU.add, ALU.min)\
                       .then_inc(kept, 1)

                def multiply_sigmoid(c, o):
                    if o not in POOL_PARTS:
                        dve.wait_ge(clipped, done(c, o))
                        dve.wait_ge(h_rounded, freed(c, o))
                        dve.tensor_tensor(h[:, o], sig[:, o], tokens(gateq, o, c), ALU.mult).then_inc(times[o], 1)

                def find(c, o):
                    dve.wait_ge(product, done(c, o))
                    dve.tensor_reduce(maxima[:, 0, bass.ds(c * F + o, 1)], prod[:, o], AX, ALU.max,
                                      apply_absolute_value=True).then_inc(seen, 1)

                def step(c, o):
                    lagging(c, 0, round_sigmoid, o)
                    lagging(c, -2, find, o)
                    lagging(c, 0, clip_sigmoid, o)
                    lagging(c, -1, multiply, o)
                    lagging(c, 0, multiply_sigmoid, o)

                each_chunk(dve, step)

            @block.gpsimd
            def _(pool):
                with pool.Fori(0, NCH) as it:
                    for o in POOL_PARTS:
                        pool.wait_ge(h_rounded, freed(it, o))
                        pool.tensor_copy(h[:, o], tokens(gateq, o, it)).then_inc(spread, 1)
                        pool.wait_ge(clipped, done(it, o))
                        pool.wait_ge(spread, past(it * len(POOL_PARTS) + o))
                        pool.tensor_tensor(h[:, o], sig[:, o], h[:, o], ALU.mult).then_inc(times[o], 1)

    small("l1f_ounit", lambda dve: dve.tensor_scalar(maxima[:, 0], maxima[:, 0], col(O_U), None, ALU.mult))
    quantizer(nc, m, "l1f_os", maxima[:, 0], col(O_S), col(O_R))
    small("l1f_ofactor", lambda dve: dve.tensor_scalar(col(O_F), col(O_U), col(O_R), None, ALU.mult))

    with Stage(nc, "l1f_down") as st:
        prod, oq = st.two("prod", [P, F, CH]), st.two("oq", [P, F, CH])
        multiplied, rounded, quantized, down, added = (
            st.sem2(n) for n in ("multiplied", "rounded", "quantized", "down", "added"))
        with nc.Block() as block:
            @block.vector
            def _(dve):
                def multiply(it, j):
                    c = it * 2 + j
                    dve.wait_ge(rounded[j], past(it * F))
                    for o in range(F):
                        dve.tensor_tensor(prod[j][:, o], tokens(gateq, o, c), tokens(upq, o, c), ALU.mult)\
                           .then_inc(multiplied[j], 1)

                def quantize(it, j):
                    dve.wait_ge(rounded[j], past(it * F + F))
                    dve.tensor_scalar(oq[j][:], oq[j][:], -ROUND, col(O_S), ALU.add, ALU.mult).then_inc(quantized[j], 1)

                def update(it, j):
                    xs = m.X[:, bass.ds(it * 8 + 4 * j, TPC), :]
                    dve.wait_ge(down[j], past(it + 1))
                    dve.scalar_tensor_tensor(xs, banks[j][0].rearrange("p (t w) -> p t w", t=TPC), m.tanh_g[:, 5:6], xs,
                                             ALU.mult, ALU.add).then_inc(added[j], 1)
                    dve.wait_ge(added[j], past(it + 1))
                    for t in range(TPC):
                        dve.bn_stats(m.S6[:, it * 8 + 4 * j + t, :], m.X[:, it * 8 + 4 * j + t, :])

                def step(it, j):
                    at(it, j, 1, multiply, CHUNK_PAIRS)
                    at(it, j, 0, quantize, CHUNK_PAIRS)
                    at(it, j, -1, update, CHUNK_PAIRS)

                steps(dve, step, CHUNK_PAIRS)

            @block.scalar
            def _(act):
                def scale_and_round(it, j):
                    act.wait_ge(down[j], past(it))
                    for o in range(F):
                        act.wait_ge(multiplied[j], past(it * F + o + 1))
                        act.activation(oq[j][:, o], prod[j][:, o], ACT.Identity, scale=col(O_F), bias=rnd[:])\
                           .then_inc(rounded[j], 1)

                def step(it, j):
                    at(it, j, 1, scale_and_round, CHUNK_PAIRS)

                steps(act, step, CHUNK_PAIRS)

            @block.tensor
            def _(pe):
                def contract(it, j):
                    pe.wait_ge(quantized[j], past(it + 1))
                    pe.wait_ge(added[j], past(it))
                    for t in range(TPC):
                        for o in range(F):
                            last = pe.matmul(banks[j][0][:, t * P:t * P + P], oq[j][:, o, t * P:t * P + P],
                                             wT[:, 2 * F + o], start=(o == 0), stop=(o == F - 1))
                    last.then_inc(down[j], 1)

                def step(it, j):
                    at(it, j, 0, contract, CHUNK_PAIRS)

                steps(pe, step, CHUNK_PAIRS)


HEADS3, W3 = 8, 64
INNER = HEADS3 * W3
HID3 = int(P * 4 * 2 / 3)
PARTS3 = [(n, min(P, HID3 - n)) for n in range(0, HID3, P)]


def local_attention(nc, m, d, y, layer):
    G = HEADS3 // 2
    with Stage(nc, f"la{layer}") as st:
        wq, wk, wv = (st.sb(n, [P, INNER]) for n in ("wq", "wk", "wv"))
        wo = st.sb("wo", [P, G, P])
        cos, sin = st.sb("cos", [P, 2, W3]), st.sb("sin", [P, 2, W3])
        by, by_swapped = st.sb("by", [P, 2, W3]), st.sb("by_swapped", [P, 2, W3])
        half_power = st.sb("half_power", [P, 2 * HEADS3])
        loads = [(wq, d["l3f_wq"][layer]), (wk, d["l3f_wk"][layer]), (wv, d["l3f_wv"][layer]),
                 (wo, d["l3f_wo"][layer]), (cos, d["c_cos"]), (sin, d["c_sin"]), (by, d["l3f_scale"][layer]),
                 (by_swapped, d["l3f_scale_swapped"][layer])]
        ys, hT, hT2 = st.two("ys", [P, P]), st.two("hT", [P, P]), st.two("hT2", [P, 2, 2, S])
        sq, qk, turned = (st.two(n, [P, 2, INNER]) for n in ("sq", "qk", "turned"))
        length, rlen = st.two("length", [P, 2 * HEADS3]), st.two("rlen", [P, 2 * HEADS3])
        qT = st.two("qT", [P, G, P])
        kd = st.two("kd", [P, G, 2, 2, S])
        vd = st.two("vd", [P, 2, G, 2, W3 + 1])
        prob, pT = st.two("prob", [P, HEADS3, S]), st.two("pT", [P, G, P])
        top, inv = st.two("top", [P, HEADS3]), st.two("inv", [P, HEADS3])
        o, oT = st.two("o", [P, INNER]), st.two("oT", [P, G, P])
        loaded, ready, ones_set = st.sem("loaded"), st.sem("ready"), st.sem("ones_set")
        (y_copied, y_turned, h_copied, qk_made, squared, summed, floored, rooted, scaled, v_made, v_kept,
         cosed, sined, rotated, qk_turned, q_copied, k_kept_low, k_kept_high, scored, max_done,
         shifted, exped, p_turned, p_copied, mixed, inverted, o_done, o_turned, o_copied, out_done, added) = (
            st.sem2(n) for n in ("y_copied", "y_turned", "h_copied", "qk_made", "squared", "summed", "floored",
                                 "rooted", "scaled", "v_made", "v_kept", "cosed", "sined",
                                 "rotated", "qk_turned", "q_copied", "k_kept_low", "k_kept_high", "scored",
                                 "max_done", "shifted", "exped", "p_turned", "p_copied", "mixed", "inverted",
                                 "o_done", "o_turned", "o_copied", "out_done", "added"))
        F0, F1 = [x[:, 0:CH] for x in m.A], [x[:, CH:2 * CH] for x in m.A]
        G0, G1 = [x[:, 0:CH] for x in m.B], [x[:, CH:2 * CH] for x in m.B]
        blocks = lambda x: x.rearrange("p (g q) -> p g q", g=G)

        def keep_v(eng_copy, j, u):
            r = slice(u * S, u * S + S)
            for b, src in enumerate((F0[j], F1[j])):
                last = eng_copy(vd[j][r, b, :, u, 0:W3], src.rearrange("p (g u w) -> p g u w", g=G, u=2)[r, :, u])
            return last

        def keep_k(eng_copy, j, u):
            r = slice(u * S, u * S + S)
            return eng_copy(kd[j][r, :, :, u], F1[j].rearrange("p (g b k) -> p g b k", g=G, b=2)[r])

        with nc.Block() as block:
            @block.sync
            def _(sp):
                for tile, src in loads:
                    sp.dma_start(tile[:], src).then_inc(loaded, 16)

            @block.scalar
            def _(act):
                def copy_y(it, j):
                    act.wait_ge(y_turned[j], past(it))
                    act.copy(ys[j][:], y[:, it * 2 + j, :]).then_inc(y_copied[j], 1)

                def copy_h(it, j):
                    act.wait_ge(y_turned[j], past(it + 1))
                    act.wait_ge(v_made[j], past(it))
                    act.copy(hT[j][:], F0[j][:, 0:P])
                    for b in range(2):
                        last = act.copy(hT2[j][:, b], repeat_heads(F0[j][:, b * S:b * S + S], 2))
                    last.then_inc(h_copied[j], 1)

                def squares(it, j):
                    act.wait_ge(qk_made[j], past(it + 1))
                    act.wait_ge(rotated[j], past(it))
                    act.activation(sq[j][:, 0], F0[j], ACT.Square)
                    act.activation(sq[j][:, 1], F1[j], ACT.Square).then_inc(squared[j], 1)

                def values(it, j):
                    act.wait_ge(v_made[j], past(it + 1))
                    act.wait_ge(mixed[j], past(it))
                    keep_v(act.copy, j, 0)
                    keep_v(act.copy, j, 1).then_inc(v_kept[j], 1)

                def copy_qk(it, j):
                    act.wait_ge(qk_turned[j], past(it + 1))
                    act.wait_ge(scored[j], past(it))
                    act.copy(qT[j][:], blocks(F0[j])).then_inc(q_copied[j], 1)
                    keep_k(act.copy, j, 1).then_inc(k_kept_high[j], 1)

                def exps(it, j):
                    act.wait_ge(shifted[j], past(it + 1))
                    act.activation(prob[j][:], prob[j][:], ACT.Exp, scale=8.0).then_inc(exped[j], 1)

                def copy_p(it, j):
                    act.wait_ge(p_turned[j], past(it + 1))
                    act.wait_ge(mixed[j], past(it))
                    act.copy(pT[j][:], blocks(G1[j])).then_inc(p_copied[j], 1)

                def copy_o(it, j):
                    act.wait_ge(o_turned[j], past(it + 1))
                    act.wait_ge(out_done[j], past(it))
                    act.copy(oT[j][:], blocks(G0[j])).then_inc(o_copied[j], 1)

                act.wait_ge(ones_set, 8)

                def step(it, j):
                    at(it, j, 2, copy_y)
                    at(it, j, 0, copy_qk)
                    at(it, j, -1, copy_p)
                    at(it, j, 2, copy_h)
                    at(it, j, 0, exps)
                    at(it, j, 2, squares)
                    at(it, j, 1, values)
                    at(it, j, -1, copy_o)

                steps(act, step)

            @block.vector
            def _(dve):
                def lengths(it, j):
                    dve.wait_ge(squared[j], past(it + 1))
                    dve.wait_ge(rooted[j], past(it))
                    dve.tensor_reduce(length[j][:], sq[j][:].rearrange("p n (h w) -> p (n h) w", h=HEADS3), AX,
                                      ALU.add).then_inc(summed[j], 1)
                    dve.wait_ge(summed[j], past(it + 1))
                    dve.tensor_scalar(length[j][:], length[j][:], 1e-24, None, ALU.max).then_inc(floored[j], 1)

                def normalize(it, j):
                    dve.wait_ge(rooted[j], past(it + 1))
                    dve.wait_ge(qk_turned[j], past(it))
                    for n, src in enumerate((F0[j], F1[j])):
                        last = dve.tensor_tensor(per_head(qk[j][:, n], HEADS3, W3), per_head(src, HEADS3, W3),
                                                 spread_heads(rlen[j][:, n * HEADS3:(n + 1) * HEADS3], W3), ALU.mult)
                    last.then_inc(scaled[j], 1)

                def cosines(it, j):
                    dve.wait_ge(scaled[j], past(it + 1))
                    dve.wait_ge(rotated[j], past(it))
                    heads = lambda x: x.rearrange("p n (h w) -> p n h w", h=HEADS3)
                    dve.tensor_tensor(heads(turned[j][:]), heads(qk[j][:]),
                                      cos[:, :, None, :].broadcast_to([P, 2, HEADS3, W3]), ALU.mult)\
                       .then_inc(cosed[j], 1)

                def keys(it, j):
                    dve.wait_ge(qk_turned[j], past(it + 1))
                    dve.wait_ge(scored[j], past(it))
                    keep_k(dve.tensor_copy, j, 0).then_inc(k_kept_low[j], 1)

                def shift(it, j):
                    dve.wait_ge(scored[j], past(it + 1))
                    dve.tensor_reduce(top[j][:], per_head(G0[j], HEADS3, S), AX, ALU.max).then_inc(max_done[j], 1)
                    dve.wait_ge(max_done[j], past(it + 1))
                    dve.wait_ge(p_turned[j], past(it))
                    dve.tensor_tensor(prob[j][:], per_head(G0[j], HEADS3, S), spread_heads(top[j][:], S),
                                      ALU.subtract).then_inc(shifted[j], 1)

                def outputs(it, j):
                    outs = [[x[j][:, 0:4 * (W3 + 1)].rearrange("p (h w) -> p h w", h=4) for x in (G0, G1)]
                        for j in range(2)]
                    dve.wait_ge(mixed[j], past(it + 1))
                    for n in range(2):
                        last = dve.reciprocal(inv[j][:, 4 * n:4 * n + 4], outs[j][n][:, :, W3])
                    last.then_inc(inverted[j], 1)
                    dve.wait_ge(inverted[j], past(it + 1))
                    dve.wait_ge(o_turned[j], past(it))
                    for n in range(2):
                        last = dve.tensor_tensor(per_head(o[j][:], HEADS3, W3)[:, 4 * n:4 * n + 4],
                                                 outs[j][n][:, :, 0:W3],
                                                 spread_heads(inv[j][:, 4 * n:4 * n + 4], W3), ALU.mult)
                    last.then_inc(o_done[j], 1)

                def add(it, j):
                    t = it * 2 + j
                    dve.wait_ge(out_done[j], past(it + 1))
                    dve.tensor_tensor(y[:, t, :], y[:, t, :], G1[j][:, 0:P], ALU.add).then_inc(added[j], 1)

                for j in range(2):
                    dve.memset(kd[j][:], 0.0).then_inc(ones_set, 1)
                    dve.memset(vd[j][:, :, :, :, 0:W3], 0.0).then_inc(ones_set, 1)
                dve.wait_ge(loaded, 16 * len(loads))
                dve.tensor_tensor(cos[:], cos[:], by[:], ALU.mult).then_inc(ready, 1)
                dve.tensor_tensor(sin[:], sin[:], by_swapped[:], ALU.mult).then_inc(ready, 1)
                dve.wait_ge(ones_set, 8)
                dve.wait_ge(ready, 3)

                def step(it, j):
                    at(it, j, 0, keys)
                    at(it, j, 1, normalize)
                    at(it, j, 0, shift)
                    at(it, j, 1, cosines)
                    at(it, j, -1, outputs)
                    at(it, j, 2, lengths)
                    at(it, j, -2, add)

                steps(dve, step)

            @block.gpsimd
            def _(pool):
                for j in range(2):
                    for b in range(2):
                        pool.tensor_copy(vd[j][:, b, :, :, W3], repeat_heads(m.half[:], G)).then_inc(ones_set, 1)
                pool.memset(half_power[:], -0.5).then_inc(ready, 1)
                pool.wait_ge(ready, 3)
                with pool.Fori(0, PAIRS) as it:
                    for j in range(2):
                        pool.wait_ge(floored[j], past(it + 1))
                        pool.wait_ge(scaled[j], past(it))
                        pool.tensor_tensor(rlen[j][:], length[j][:], half_power[:], ALU.pow).then_inc(rooted[j], 1)
                        x = qk[j][:].rearrange("p n (h w) -> p n h w", h=HEADS3)
                        z = sq[j][:].rearrange("p n (h w) -> p n h w", h=HEADS3)
                        along = lambda w: sin[:, :, None, w].broadcast_to([P, 2, HEADS3, w.stop - w.start])
                        lo, hi = slice(0, W3 // 2), slice(W3 // 2, W3)
                        pool.wait_ge(scaled[j], past(it + 1))
                        pool.tensor_tensor(z[:, :, :, lo], x[:, :, :, hi], along(lo), ALU.mult)
                        pool.tensor_tensor(z[:, :, :, hi], x[:, :, :, lo], along(hi), ALU.mult).then_inc(sined[j], 1)
                        pool.wait_ge(sined[j], past(it + 1))
                        pool.wait_ge(cosed[j], past(it + 1))
                        pool.tensor_tensor(qk[j][:], turned[j][:], sq[j][:], ALU.add).then_inc(rotated[j], 1)

            @block.tensor
            def _(pe):
                def turn_y(it, j):
                    pe.wait_ge(y_copied[j], past(it + 1))
                    pe.wait_ge(q_copied[j], past(it))
                    pe.matmul(F0[j][0:S, 0:P], ys[j][:, 0:P // 2], m.ident[:], start=True, stop=True)
                    pe.matmul(F0[j][S:P, 0:P], ys[j][:, P // 2:P], m.shift[:], start=True, stop=True)\
                      .then_inc(y_turned[j], 1)

                def make_qk(it, j):
                    pe.wait_ge(h_copied[j], past(it + 1))
                    pe.wait_ge(k_kept_low[j], past(it))
                    pe.wait_ge(k_kept_high[j], past(it))
                    pe.matmul(F0[j], hT[j][:], wq[:], start=True, stop=True)
                    pe.matmul(F1[j], hT[j][:], wk[:], start=True, stop=True).then_inc(qk_made[j], 1)

                def make_v(it, j):
                    pe.wait_ge(scaled[j], past(it + 1))
                    for b, dst in enumerate((F0[j], F1[j])):
                        last = pe.matmul(dst, hT2[j][:, b].rearrange("p u k -> p (u k)"), wv[:],
                                         start=True, stop=True)
                    last.then_inc(v_made[j], 1)

                def turn_qk(it, j):
                    pe.wait_ge(rotated[j], past(it + 1))
                    pe.wait_ge(v_kept[j], past(it + 1))
                    for n, dst in enumerate((F0[j], F1[j])):
                        for g in range(G):
                            last = pe.transpose(dst[:, g * P:g * P + P], qk[j][:, n, g * P:g * P + P], m.ident[:])
                    last.then_inc(qk_turned[j], 1)

                def scores(it, j):
                    pe.wait_ge(o_copied[j], past(it))
                    pe.matmul(G0[j], m.ident_bf[:], repeat_heads(m.causal_bf[:], HEADS3), start=True, stop=False)
                    pe.wait_ge(q_copied[j], past(it + 1))
                    pe.wait_ge(k_kept_low[j], past(it + 1))
                    pe.wait_ge(k_kept_high[j], past(it + 1))
                    for b in range(2):
                        for g in range(G):
                            last = pe.matmul(G0[j][b * S:b * S + S, g * P:g * P + P], qT[j][:, g, b * S:b * S + S],
                                             kd[j][:, g, b].rearrange("p u k -> p (u k)"), start=False,
                                             stop=(g == G - 1))
                    last.then_inc(scored[j], 1)

                def turn_p(it, j):
                    pe.wait_ge(exped[j], past(it + 1))
                    pe.wait_ge(added[j], past(it))
                    p = prob[j][:].rearrange("p h k -> p (h k)")
                    for g in range(G):
                        last = pe.transpose(G1[j][:, g * P:g * P + P], p[:, g * P:g * P + P], m.ident[:])
                    last.then_inc(p_turned[j], 1)

                def mix(it, j):
                    pe.wait_ge(p_copied[j], past(it + 1))
                    n = 2 * (W3 + 1)
                    for b in range(2):
                        for g in range(G):
                            dst = (G0, G1)[g // 2][j]
                            last = pe.matmul(dst[b * S:b * S + S, g % 2 * n:g % 2 * n + n],
                                             pT[j][:, g, b * S:b * S + S],
                                             vd[j][:, b, g].rearrange("p u w -> p (u w)"), start=True, stop=True)
                    last.then_inc(mixed[j], 1)

                def turn_o(it, j):
                    pe.wait_ge(o_done[j], past(it + 1))
                    for g in range(G):
                        last = pe.transpose(G0[j][:, g * P:g * P + P], o[j][:, g * P:g * P + P], m.ident[:])
                    last.then_inc(o_turned[j], 1)

                def project(it, j):
                    pe.wait_ge(o_copied[j], past(it + 1))
                    for g in range(G):
                        last = pe.matmul(G1[j][:, 0:P], oT[j][:, g], wo[:, g], start=(g == 0), stop=(g == G - 1))
                    last.then_inc(out_done[j], 1)

                pe.wait_ge(loaded, 16 * len(loads))
                pe.wait_ge(ones_set, 8)

                def step(it, j):
                    at(it, j, 0, turn_qk)
                    at(it, j, -1, turn_p)
                    at(it, j, -2, project)
                    at(it, j, 2, turn_y)
                    at(it, j, 0, scores)
                    at(it, j, 2, make_qk)
                    at(it, j, -1, mix)
                    at(it, j, 1, make_v)
                    at(it, j, -1, turn_o)

                steps(pe, step)


def gated_gelu(nc, m, d, y, layer):
    with Stage(nc, f"gg{layer}") as st:
        F = len(PARTS3)
        w1, w2 = st.sb("w1", [P, 2 * HID3]), st.sb("w2", [P, F, P])
        b1, b2 = st.sb("b1", [P, 2, F]), st.sb("b2", [1, P])
        lg, lb = st.sb("lg", [P, 1]), st.sb("lb", [P, 1])
        loads = [(w1, "l3f_w1"), (w2, "l3f_w2"), (b1, "l3f_b1"), (b2, "l3f_b2"), (lg, "l3f_lg"), (lb, "l3f_lb")]
        half_power = st.sb("half_power", [P, TPC])
        h, hT = st.two("h", [P, TPC, P]), st.two("hT", [P, CH])
        stats = st.two("stats", [P, TPC, 6])
        mean, delta, var, rstd = (st.two(n, [P, TPC]) for n in ("mean", "delta", "var", "rstd"))
        gate, hid = st.two("gate", [P, F, CH]), st.two("hid", [P, F, CH])
        loaded, ready = st.sem("loaded"), st.sem("ready")
        (moved, h_set, stat, parts, terms, aggregated, rooted, normed_h, turned, copied, up, gelued, hidden, down, added) = (
            st.sem2(n) for n in ("moved", "h_set", "stat", "parts", "terms", "aggregated", "rooted", "normed_h", "turned",
                                 "copied", "up", "gelued", "hidden", "down", "added"))
        A0, A1 = [x[:, 0:CH] for x in m.A], [x[:, CH:2 * CH] for x in m.A]
        B0, B1 = [x[:, 0:CH] for x in m.B], [x[:, CH:2 * CH] for x in m.B]
        up_bank = lambda j, o: (A0, A1)[o % 2][j]
        gate_bank = lambda j, o: (B0, B1)[o % 2][j]
        with nc.Block() as block:
            @block.sync
            def _(sp):
                for tile, src in loads:
                    sp.dma_start(tile[:], d[src][layer]).then_inc(loaded, 16)

            @block.vector
            def _(dve):
                def shift_in(it, j):
                    ty = y[:, bass.ds(it * 8 + 4 * j, TPC), :]
                    dve.wait_ge(turned[j], past(it))
                    dve.tensor_copy(h[j][:, :, 0:S], ty[:, :, 0:S])
                    dve.wait_ge(moved[j], past(it + 1))
                    dve.tensor_copy(h[j][:, :, S:P], A0[j][:, 0:TPC * S].rearrange("p (t w) -> p t w", t=TPC))\
                       .then_inc(h_set[j], 1)

                def moments(it, j):
                    dve.wait_ge(h_set[j], past(it + 1))
                    for t in range(TPC):
                        last = dve.bn_stats(stats[j][:, t], h[j][:, t])
                    last.then_inc(stat[j], 1)
                    dve.wait_ge(stat[j], past(it + 1))
                    mean_e, m2_e, mean_o, m2_o = (stats[j][:, :, k] for k in (1, 2, 4, 5))
                    dve.wait_ge(normed_h[j], past(it))
                    dve.tensor_tensor(mean[j][:], mean_e, mean_o, ALU.add)
                    dve.tensor_tensor(delta[j][:], mean_e, mean_o, ALU.subtract)
                    dve.tensor_tensor(var[j][:], m2_e, m2_o, ALU.add).then_inc(parts[j], 1)
                    dve.wait_ge(parts[j], past(it + 1))
                    dve.tensor_scalar(mean[j][:], mean[j][:], 0.5, None, ALU.mult)
                    dve.scalar_tensor_tensor(delta[j][:], delta[j][:], 0.25, delta[j][:], ALU.mult, ALU.mult)
                    dve.tensor_scalar(var[j][:], var[j][:], 1.0 / P, 1e-5, ALU.mult, ALU.add).then_inc(terms[j], 1)
                    dve.wait_ge(terms[j], past(it + 1))
                    dve.tensor_tensor(var[j][:], var[j][:], delta[j][:], ALU.add).then_inc(aggregated[j], 1)

                def normalize(it, j):
                    dve.wait_ge(rooted[j], past(it + 1))
                    for t in range(TPC):
                        last = dve.tensor_scalar(h[j][:, t], h[j][:, t], mean[j][:, t:t + 1], rstd[j][:, t:t + 1],
                                                 ALU.subtract, ALU.mult)
                    last.then_inc(normed_h[j], 1)

                def products(it, j, some):
                    dve.wait_ge(down[j], past(it))
                    for o in some:
                        k = PARTS3[o][1]
                        dve.wait_ge(gelued[j], past(it * F + o + 1))
                        dve.scalar_tensor_tensor(hid[j][0:k, o], up_bank(j, o)[0:k], b1[0:k, 0, o:o + 1],
                                                 gate[j][0:k, o], ALU.add, ALU.mult).then_inc(hidden[j], 1)

                def add(it, j):
                    dve.wait_ge(down[j], past(it + 1))
                    ty = y[:, bass.ds(it * 8 + 4 * j, TPC), :]
                    dve.tensor_tensor(ty, ty, A1[j].rearrange("p (t w) -> p t w", t=TPC), ALU.add)\
                       .then_inc(added[j], 1)

                dve.wait_ge(loaded, 16 * len(loads))

                def step(it, j):
                    at(it, j, -2, add, CHUNK_PAIRS)
                    at(it, j, 1, shift_in, CHUNK_PAIRS)
                    at(it, j, 1, moments, CHUNK_PAIRS)
                    at(it, j, 0, lambda it, j: products(it, j, (0,)), CHUNK_PAIRS)
                    at(it, j, 1, normalize, CHUNK_PAIRS)
                    at(it, j, 0, lambda it, j: products(it, j, range(1, F)), CHUNK_PAIRS)

                steps(dve, step, CHUNK_PAIRS)

            @block.gpsimd
            def _(pool):
                pool.memset(half_power[:], -0.5).then_inc(ready, 1)
                pool.wait_ge(ready, 1)
                with pool.Fori(0, CHUNK_PAIRS) as it:
                    for j in range(2):
                        pool.wait_ge(aggregated[j], past(it + 1))
                        pool.wait_ge(normed_h[j], past(it))
                        pool.tensor_tensor(rstd[j][:], var[j][:], half_power[:], ALU.pow).then_inc(rooted[j], 1)

            @block.scalar
            def _(act):
                def copy_h(it, j):
                    act.wait_ge(turned[j], past(it + 1))
                    act.wait_ge(hidden[j], past(it * F))
                    act.activation(hT[j][:], B0[j], ACT.Identity, scale=lg[:], bias=lb[:]).then_inc(copied[j], 1)

                def gelus(it, j):
                    for o, (_, k) in enumerate(PARTS3):
                        act.wait_ge(up[j], past(it * F + o + 1))
                        act.activation(gate[j][0:k, o], gate_bank(j, o)[0:k], ACT.Gelu, bias=b1[0:k, 1, o:o + 1])\
                           .then_inc(gelued[j], 1)

                act.wait_ge(loaded, 16 * len(loads))

                def step(it, j):
                    at(it, j, 0, gelus, CHUNK_PAIRS)
                    at(it, j, 1, copy_h, CHUNK_PAIRS)

                steps(act, step, CHUNK_PAIRS)

            @block.tensor
            def _(pe):
                def move(it, j):
                    pe.wait_ge(hidden[j], past(it * F))
                    pe.matmul(A0[j][:, 0:TPC * S], m.shift[:], y[:, bass.ds(it * 8 + 4 * j, TPC), S:P],
                              start=True, stop=True).then_inc(moved[j], 1)

                def turn(it, j):
                    pe.wait_ge(normed_h[j], past(it + 1))
                    for t in range(TPC):
                        last = pe.transpose(B0[j][:, t * P:t * P + P], h[j][:, t], m.ident[:])
                    last.then_inc(turned[j], 1)

                def expand(it, j):
                    pe.wait_ge(copied[j], past(it + 1))
                    pe.wait_ge(added[j], past(it))
                    for o, (n, k) in enumerate(PARTS3):
                        if o >= 2:
                            pe.wait_ge(hidden[j], past(it * F + o - 1))
                        pe.matmul(up_bank(j, o)[0:k], w1[:, n:n + k], hT[j][:], start=True, stop=True)
                        pe.matmul(gate_bank(j, o)[0:k], w1[:, HID3 + n:HID3 + n + k], hT[j][:],
                                  start=True, stop=True).then_inc(up[j], 1)

                def contract(it, j):
                    pe.wait_ge(hidden[j], past(it * F + F))
                    for t in range(TPC):
                        dst = A1[j][:, t * P:t * P + P]
                        pe.matmul(dst, m.ones_row[:], b2[:], start=True, stop=False)
                        for o, (_, k) in enumerate(PARTS3):
                            last = pe.matmul(dst, hid[j][0:k, o, t * P:t * P + P], w2[0:k, o],
                                             start=False, stop=(o == F - 1))
                    last.then_inc(down[j], 1)

                pe.wait_ge(loaded, 16 * len(loads))

                def step(it, j):
                    at(it, j, 1, move, CHUNK_PAIRS)
                    at(it, j, 0, expand, CHUNK_PAIRS)
                    at(it, j, 1, turn, CHUNK_PAIRS)
                    at(it, j, -1, contract, CHUNK_PAIRS)

                steps(pe, step, CHUNK_PAIRS)


def l3_ffn(nc, m, d, own):
    y = own.enter_context(nc.sbuf_tensor("l3f_y", [P, NT, P], F32))
    with Stage(nc, "l3f_in") as st:
        with nc.Block() as block:
            @block.vector
            def _(dve):
                with dve.Fori(0, NCH // 2) as it:
                    for t in range(2 * TPC):
                        normed(dve, m, y[:, it * 2 * TPC + t, :], it * 2 * TPC + t)
    for layer in range(2):
        local_attention(nc, m, d, y, layer)
        gated_gelu(nc, m, d, y, layer)
    with Stage(nc, "l3f_out") as st:
        with nc.Block() as block:
            @block.vector
            def _(dve):
                with dve.Fori(0, NCH) as it:
                    for xs, ys in ((m.X[:, bass.ds(it * TPC, TPC), :], y[:, bass.ds(it * TPC, TPC), :]),):
                        dve.scalar_tensor_tensor(xs, ys, m.tanh_g[:, 7:8], xs, ALU.mult, ALU.add)


class Memory:

    def __init__(self, nc, ctx):
        def sb(name, shape, dt=F32):
            return ctx.enter_context(nc.sbuf_tensor(name, list(shape), dt))

        self.X = sb("X", [P, NT, P])
        self.S6 = sb("S6", [P, NT, 6])
        self.mean, self.rstd = sb("mean", [P, NT]), sb("rstd", [P, NT])
        self.ident, self.ident_bf = sb("ident", [P, P]), sb("ident_bf", [P, P], BF16)
        self.blockones = sb("blockones", [P, P])
        self.tri = sb("tri", [P, P])
        self.shift = sb("shift", [P, P])
        self.eye64 = sb("eye64", [P, S])
        self.causal, self.causal_bf = sb("causal", [P, S]), sb("causal_bf", [P, S], BF16)
        self.half = sb("half", [P, 2])
        self.head8 = sb("head8", [P, 8])
        self.head_of_8 = sb("head_of_8", [P, 8])
        self.gates, self.tanh_g = sb("gates", [P, 8]), sb("tanh_g", [P, 8])
        self.ones_row = sb("ones_row", [1, P])
        self.A = [ctx.enter_context(nc.psum_tensor(f"A{j}", [P, 1024], F32)) for j in range(2)]
        self.B = [ctx.enter_context(nc.psum_tensor(f"B{j}", [P, 1024], F32)) for j in range(2)]


def store(nc, m, d):
    with Stage(nc, "store") as st:
        stored = st.sem("stored")
        with nc.Block() as block:
            @block.sync
            def _(sp):
                sp.dma_start(d["out"], m.X[:]).then_inc(stored, 16)
                sp.wait_ge(stored, 16)


def program(nc, d, stages=None):
    with ExitStack() as ctx:
        m = Memory(nc, ctx)
        setup(nc, m, d)
        for n, stage in enumerate(STAGES):
            if stages is None or n in stages:
                norm_header(nc, m, f"norm{n}")
                with ExitStack() as own:
                    stage(nc, m, d, own)
        store(nc, m, d)


def l0_xattn(nc, m, d, own):
    sb = lambda n, s: own.enter_context(nc.sbuf_tensor(n, s, F32))
    m.gate, m.fsum, m.a = sb("gate", [P, NT, 16]), sb("fsum", [P, NT, 8]), sb("a", [P, NT, 8])
    m.h = sb("h", [P, NT, P])
    gated_memory(nc, m, d)


STAGES = [l0_xattn, l0_ffn, l1_xattn, l1_ffn, l2_xattn, l2_ffn, l3_xattn, l3_ffn]


def shape_constants():
    i, b = np.arange(P) % S, np.arange(P) // S
    same = b[:, None] == b[None, :]
    f = lambda x: np.ascontiguousarray(x.astype(np.float32))
    return {
        "c_ident": f(np.eye(P)),
        "c_blockones": f(same),
        "c_tri": f(same & (i[:, None] <= i[None, :])),
        "c_shift": f(same & (i[:, None] + 1 == i[None, :])),
        "c_lower_e": f(np.broadcast_to(np.arange(8)[None, None, :] < np.arange(8)[None, :, None], (P, 8, 8))),
        "c_half": f(b[:, None] == np.arange(2)[None, :]),
        "c_eye64": f(i[:, None] == np.arange(S)[None, :]),
        "c_causal": f(np.where(np.arange(S)[None, :] > i[:, None], NEG, 0.0)),
        "c_head_of_8": f(np.arange(P)[:, None] // 8 % 8 == np.arange(8)[None, :]),
        "c_head8": f(np.arange(P)[:, None] // 16 == np.arange(8)[None, :]),
    }


def rotary_tables():
    f = np.float32
    half = np.arange(0, W3, 2, dtype=f)
    freqs = np.arange(S, dtype=f)[:, None] * (f(1.0) / f(10000.0) ** (half / f(W3)))[None, :]
    freqs = np.concatenate([freqs, freqs], axis=-1)
    base = (half + f(0.4 * W3)) / f(1.4 * W3)
    power = (np.arange(S, dtype=f) - f(S // 2)) / f(S // 2)
    scale = base[None, :] ** power[:, None]
    scale = np.concatenate([scale, scale], axis=-1)
    cos, sin = np.cos(freqs), np.sin(freqs)
    sin[:, :W3 // 2] *= f(-1.0)
    both = lambda t: np.ascontiguousarray(np.tile(np.stack([t * scale, t / scale], axis=1), (2, 1, 1)).astype(f))
    return both(cos), both(sin)


def lay_out(v):
    rows = lambda a: np.ascontiguousarray(np.broadcast_to(a.reshape(1, -1), (P, a.size)))
    T = lambda a: np.ascontiguousarray(a.T)
    x, ctx = v["x"], v["ctx_1024"]
    d = dict(shape_constants())
    d["x"] = np.ascontiguousarray(x.reshape(NT, P, P).transpose(1, 0, 2))
    d["ctxT"] = np.ascontiguousarray(ctx.reshape(NT, P, P).transpose(0, 2, 1))
    d["ctx_rows"] = np.ascontiguousarray(ctx.reshape(NT, P, P).transpose(1, 0, 2))
    d["ctx"] = np.ascontiguousarray(ctx.transpose(1, 0, 2))
    d["gates"] = rows(np.concatenate([v["g_xattn"], v["g_ffn"]]))
    wi, wf = v["L0_xattn_igate_w"], v["L0_xattn_fgate_w"]
    for n, k in enumerate("qkv"):
        d[f"l0_gate_{k}"] = T(np.concatenate([wi, wf])[:, n * P:(n + 1) * P])
    d["l0_gate_b"] = rows(np.concatenate([v["L0_xattn_igate_b"], v["L0_xattn_fgate_b"]]))
    d["l0_norm_w"] = rows(v["L0_xattn_norm_w"])
    more_layout(d, v, rows, T)
    return d


def more_layout(d, v, rows, T):
    parts = lambda a: np.ascontiguousarray(a.reshape(-1, P, a.shape[-1]).transpose(1, 0, 2))
    cols = lambda a: np.ascontiguousarray(a.reshape(-1, P).T)
    for n in ("w1", "w2"):
        d[f"l0f_{n}"] = T(v[f"L0_ffn_{n}_w"])
    for n in ("h1", "h2", "w3"):
        d[f"l0f_{n}"] = parts(v[f"L0_ffn_{n}_w"].T)
    d["l0f_s"] = np.ascontiguousarray(np.stack([cols(v[f"L0_ffn_{n}_s"]) for n in ("w1", "w2", "h1", "h2")], axis=1))
    d["l0f_s3"] = rows(v["L0_ffn_w3_s"])
    column = lambda a: np.ascontiguousarray(a.reshape(-1, 1))
    for n in "qkvo":
        d[f"l1x_w{n}"] = T(v[f"L1_xattn_w{n}"])
    d["l1x_bq"], d["l1x_bk"] = column(v["L1_xattn_bq"]), column(v["L1_xattn_bk"])
    d["l1x_bv"], d["l1x_bo"] = rows(v["L1_xattn_bv"]), v["L1_xattn_bo"].reshape(1, P)
    d["l1x_mask"] = T(v["mask_BxS_ik0"])
    d["l2x_wo"], d["l2x_bo"] = T(v["L2_xattn_W_out"]), v["L2_xattn_b_out"].reshape(1, P)
    d["l2x_mask"] = np.ascontiguousarray(v["mask_Bx1xSxS2_ik1"][:, 0].transpose(1, 0, 2))
    for n in "qk":
        d[f"l3x_w{n}"] = T(v[f"L3_xattn_W{n}_w"])
        d[f"l3x_b{n}"] = column(v[f"L3_xattn_W{n}_b"])
    keys = np.broadcast_to(v["mask_BxS2_ik1"].reshape(NT, 2, 1, S), (NT, 2, S, S))
    d["l3x_mask"] = np.ascontiguousarray(keys.transpose(1, 2, 0, 3)).reshape(P, NT, S)
    w = [v[f"L1_ffn_w_{n}"].reshape(3, P, P).transpose(1, 0, 2) for n in ("up", "gate")]
    d["l1f_w"] = np.ascontiguousarray(np.concatenate([*w, v["L1_ffn_w_down"].reshape(P, 3, P)], axis=1).reshape(P, 9 * P))
    d["c_cos"], d["c_sin"] = rotary_tables()
    for n, k in enumerate("qkv"):
        d[f"l3f_w{k}"] = np.ascontiguousarray(v["L3_ffn_wqkv"][:, :, n * INNER:(n + 1) * INNER])
    d["l3f_wo"] = np.ascontiguousarray(v["L3_ffn_wo"].reshape(2, -1, P, P).transpose(0, 2, 1, 3))
    scales = np.stack([v["L3_ffn_q_scale"], v["L3_ffn_k_scale"]], axis=1)
    swapped = np.concatenate([scales[:, :, W3 // 2:], scales[:, :, :W3 // 2]], axis=-1)
    for n, a in (("scale", scales), ("scale_swapped", swapped)):
        d[f"l3f_{n}"] = np.ascontiguousarray(np.broadcast_to(a[:, None], (2, P, 2, W3)))
    pad = len(PARTS3) * P - HID3
    d["l3f_w1"] = v["L3_ffn_w1"]
    d["l3f_w2"] = np.ascontiguousarray(np.pad(v["L3_ffn_w2"], ((0, 0), (0, pad), (0, 0)))
                                       .reshape(2, -1, P, P).transpose(0, 2, 1, 3))
    d["l3f_b1"] = np.ascontiguousarray(np.pad(v["L3_ffn_b1"].reshape(2, 2, HID3), ((0, 0), (0, 0), (0, pad)))
                                       .reshape(2, 2, -1, P).transpose(0, 3, 1, 2))
    d["l3f_b2"] = v["L3_ffn_b2"].reshape(2, 1, P)
    d["l3f_lg"], d["l3f_lb"] = v["L3_ffn_ln_g"].reshape(2, P, 1), v["L3_ffn_ln_b"].reshape(2, P, 1)
    d["l2f_wr"] = v["L2_ffn_Wr"]
    d["l2f_temp"] = rows(v["L2_ffn_temperature"])
    for n in ("g", "u", "d"):
        d[f"l2f_w{n}"] = np.ascontiguousarray(v[f"L2_ffn_W{n}"].transpose(1, 0, 2))


def declare(nc, arrays):
    d = {n: nc.dram_tensor(f"in_{n}", a.shape, mybir.dt.from_np(a.dtype), kind="ExternalInput").ap()
         for n, a in arrays.items()}
    d["out"] = nc.dram_tensor("out", (P, NT, P), F32, kind="ExternalOutput").ap()
    return d


def kernel(**inputs):
    import concourse.bacc as bacc
    from concourse.bass_utils import run_bass_kernel_spmd

    arrays = lay_out({n: np.asarray(a) for n, a in inputs.items()})
    nc = bacc.Bacc("TRN2", target_bir_lowering=False, num_devices=1)
    program(nc, declare(nc, arrays))
    r = run_bass_kernel_spmd(nc, [{f"in_{n}": a for n, a in arrays.items()}], core_ids=[0])
    out = r.results[0]["out"]
    return np.ascontiguousarray(out.transpose(1, 0, 2)).reshape(NB, S, P)
```
